# Optimizing a Trainium2 kernel written in Bass

```python
import numpy as np
import jax
import jax.numpy as jnp

def _softmax(x, axis=-1):
    return jax.nn.softmax(x, axis=axis)

def _gelu(x):
    return jax.nn.gelu(x, approximate=True)

def _silu(x):
    return jax.nn.silu(x)

def _sigmoid(x):
    return jax.nn.sigmoid(x)

def _layernorm(x, axis=-1, eps=1e-05):
    m = jnp.mean(x, axis=axis, keepdims=True)
    v = jnp.var(x, axis=axis, keepdims=True)
    return (x - m) / jnp.sqrt(v + eps)

def _scatter_add(tgt, idx, src, axis=0):
    return tgt.at[idx].add(src)

def _segment_sum(src, seg, n):
    return jax.ops.segment_sum(src, seg, n)
kernel_name = 'mk_early_fusion_d1_tok_img256_r4_aef951'

def setup_inputs(seed: int=0):
    np.random.seed(seed)
    _w = jnp.asarray

    def _rec_inputs():
        import jax
        import jax.numpy as jnp
        _rk = jax.random.key(seed)
        x = -0.000202321 + 1.00025 * jax.random.normal(jax.random.fold_in(_rk, 1), (4, 64, 56, 56), jnp.float32)
        txt = 0.00140203 + 0.288157 * jax.random.normal(jax.random.fold_in(_rk, 2), (4, 77, 64), jnp.float32)
        return (x, txt)
    x, txt = _rec_inputs()

    def _L0_tok_setup():
        import jax, jax.numpy as jnp
        import numpy as np
        B, C, H, W = (8, 64, 56, 56)
        K = 3

        def _unfold3x3(x):
            b, c, h, w = x.shape
            xp = jnp.pad(x, ((0, 0), (0, 0), (1, 1), (1, 1)))
            patches = jnp.stack([xp[:, :, i:i + h, j:j + w] for i in range(K) for j in range(K)], axis=2)
            return patches.reshape(b, c * K * K, h * w).transpose(0, 2, 1)
        key = jax.random.key(seed)
        ks = jax.random.split(key, 8)
        d = C * K * K
        s1 = 1.0 / np.sqrt(d)
        s2 = 1.0 / np.sqrt(C)
        return {'x': jax.random.normal(ks[0], (B, C, H, W), jnp.float32), 'W1': jax.random.uniform(ks[1], (d, C), jnp.float32, -s1, s1), 'b1': jax.random.uniform(ks[2], (C,), jnp.float32, -s1, s1), 'W2': jax.random.uniform(ks[3], (C, d), jnp.float32, -s2, s2), 'b2': jax.random.uniform(ks[4], (d,), jnp.float32, -s2, s2), 'W3': jax.random.uniform(ks[5], (d, C), jnp.float32, -s1, s1), 'b3': jax.random.uniform(ks[6], (C,), jnp.float32, -s1, s1)}
    _L0_tok_all = _L0_tok_setup()
    _L0_tok_in = {k: v for k, v in _L0_tok_all.items() if k in ('W1', 'b1', 'W2', 'b2', 'W3', 'b3')}
    del _L0_tok_all

    def _L0_attn_setup():
        import math
        import jax, jax.numpy as jnp
        import numpy as np
        B, T, C = (4, 512, 64)
        LEVELS = 3
        NEAR_WINDOW = 16
        THETA = 10000.0
        EPS_L2 = 1e-08
        EPS_VAR = 1e-06

        def haar_basis(T, levels):
            cols = []
            for j in range(levels):
                bc = 2 ** j
                bs = T // bc
                half = bs // 2
                for k in range(bc):
                    v = np.zeros(T, np.float32)
                    s = k * bs
                    v[s:s + half] = 1.0 / math.sqrt(half)
                    v[s + half:s + bs] = -1.0 / math.sqrt(half)
                    cols.append(v)
            return jnp.asarray(np.stack(cols, axis=1))

        def rope_tables(T, dim):
            half = dim // 2
            inv_freq = 1.0 / THETA ** (np.arange(half, dtype=np.float32) / half)
            ang = np.arange(T, dtype=np.float32)[:, None] * inv_freq[None, :]
            return (jnp.asarray(np.cos(ang)), jnp.asarray(np.sin(ang)))

        def apply_rope(x, cos, sin):
            half = x.shape[-1] // 2
            x1, x2 = (x[..., :half], x[..., half:])
            return jnp.concatenate([x1 * cos - x2 * sin, x1 * sin + x2 * cos], axis=-1)

        def l2_normalize(x, eps=EPS_L2):
            return x / (jnp.linalg.norm(x, axis=-1, keepdims=True) + eps)

        def variance_scaled_softmax(scores, eps=EPS_VAR):
            finite = jnp.isfinite(scores)
            m = finite.astype(scores.dtype)
            n = jnp.clip(jnp.sum(m, axis=-1, keepdims=True), 1.0, None)
            safe = jnp.where(finite, scores, 0.0)
            mean = jnp.sum(safe * m, axis=-1, keepdims=True) / n
            var = jnp.sum((safe - mean) ** 2 * m, axis=-1, keepdims=True) / n
            std = jnp.sqrt(jnp.clip(var, eps, None))
            scaled = jnp.where(finite, (safe - mean) / std, -jnp.inf)
            out = jax.nn.softmax(scaled, axis=-1)
            return jnp.where(n == 0, jnp.zeros_like(out), out)
        key = jax.random.key(seed)
        kx, kq, kv, ko = jax.random.split(key, 4)
        lim = math.sqrt(6.0 / (C + C))
        return {'x': jax.random.normal(kx, (B, T, C), dtype=jnp.float32), 'W_Q': jax.random.uniform(kq, (C, C), jnp.float32, -lim, lim), 'W_V': jax.random.normal(kv, (C, C), jnp.float32) * 0.02, 'W_O': jax.random.normal(ko, (C, C), jnp.float32) * 0.02}
    _L0_attn_all = _L0_attn_setup()
    _L0_attn_in = {k: v for k, v in _L0_attn_all.items() if k in ('W_Q', 'W_V', 'W_O')}
    del _L0_attn_all

    def _L0_ffn_setup():
        import jax, jax.numpy as jnp
        import numpy as np
        B, T, D, H, E = (16, 1024, 64, 128, 8)
        key = jax.random.key(seed)
        ks = jax.random.split(key, 5)
        x = jax.random.normal(ks[0], (B, T, D), dtype=jnp.float32)
        gate_w = jax.random.normal(ks[1], (D, E), dtype=jnp.float32) * 0.02
        gate_b = jnp.zeros((E,), dtype=jnp.float32)
        W1 = jax.random.normal(ks[2], (E, D, H), dtype=jnp.float32) * 0.02
        b1 = jnp.zeros((E, H), dtype=jnp.float32)
        W2 = jax.random.normal(ks[3], (E, H, D), dtype=jnp.float32) * 0.02
        b2 = jnp.zeros((E, D), dtype=jnp.float32)
        return {'x': x, 'gate_w': gate_w, 'gate_b': gate_b, 'W1': W1, 'b1': b1, 'W2': W2, 'b2': b2}
    _L0_ffn_all = _L0_ffn_setup()
    _L0_ffn_in = {k: v for k, v in _L0_ffn_all.items() if k in ('gate_w', 'gate_b', 'W1', 'b1', 'W2', 'b2')}
    del _L0_ffn_all
    return {'x': x, 'txt': txt, 'L0_tok_W1': _L0_tok_in['W1'], 'L0_tok_b1': _L0_tok_in['b1'], 'L0_tok_W2': _L0_tok_in['W2'], 'L0_tok_b2': _L0_tok_in['b2'], 'L0_tok_W3': _L0_tok_in['W3'], 'L0_tok_b3': _L0_tok_in['b3'], 'L0_attn_W_Q': _L0_attn_in['W_Q'], 'L0_attn_W_V': _L0_attn_in['W_V'], 'L0_attn_W_O': _L0_attn_in['W_O'], 'L0_ffn_gate_w': _L0_ffn_in['gate_w'], 'L0_ffn_gate_b': _L0_ffn_in['gate_b'], 'L0_ffn_W1': _L0_ffn_in['W1'], 'L0_ffn_b1': _L0_ffn_in['b1'], 'L0_ffn_W2': _L0_ffn_in['W2'], 'L0_ffn_b2': _L0_ffn_in['b2']}

def reference(x, txt, L0_tok_W1, L0_tok_b1, L0_tok_W2, L0_tok_b2, L0_tok_W3, L0_tok_b3, L0_attn_W_Q, L0_attn_W_V, L0_attn_W_O, L0_ffn_gate_w, L0_ffn_gate_b, L0_ffn_W1, L0_ffn_b1, L0_ffn_W2, L0_ffn_b2):
    import jax
    import jax.numpy as jnp

    def _L0_tok_ref(x, W1, b1, W2, b2, W3, b3):
        import jax, jax.numpy as jnp
        import numpy as np
        B, C, H, W = (8, 64, 56, 56)
        K = 3

        def _unfold3x3(x):
            b, c, h, w = x.shape
            xp = jnp.pad(x, ((0, 0), (0, 0), (1, 1), (1, 1)))
            patches = jnp.stack([xp[:, :, i:i + h, j:j + w] for i in range(K) for j in range(K)], axis=2)
            return patches.reshape(b, c * K * K, h * w).transpose(0, 2, 1)
        t = _unfold3x3(x)
        h1 = jax.nn.relu(jnp.einsum('bld,dc->blc', t, W1) + b1)
        s = jax.nn.sigmoid(jnp.einsum('blc,cd->bld', h1, W2) + b2)
        out = jnp.einsum('bld,dc->blc', t * s, W3) + b3
        return out

    def _L0_attn_ref(x, W_Q, W_V, W_O):
        import math
        import jax, jax.numpy as jnp
        import numpy as np
        B, T, C = (4, 512, 64)
        LEVELS = 3
        NEAR_WINDOW = 16
        THETA = 10000.0
        EPS_L2 = 1e-08
        EPS_VAR = 1e-06

        def haar_basis(T, levels):
            cols = []
            for j in range(levels):
                bc = 2 ** j
                bs = T // bc
                half = bs // 2
                for k in range(bc):
                    v = np.zeros(T, np.float32)
                    s = k * bs
                    v[s:s + half] = 1.0 / math.sqrt(half)
                    v[s + half:s + bs] = -1.0 / math.sqrt(half)
                    cols.append(v)
            return jnp.asarray(np.stack(cols, axis=1))

        def rope_tables(T, dim):
            half = dim // 2
            inv_freq = 1.0 / THETA ** (np.arange(half, dtype=np.float32) / half)
            ang = np.arange(T, dtype=np.float32)[:, None] * inv_freq[None, :]
            return (jnp.asarray(np.cos(ang)), jnp.asarray(np.sin(ang)))

        def apply_rope(x, cos, sin):
            half = x.shape[-1] // 2
            x1, x2 = (x[..., :half], x[..., half:])
            return jnp.concatenate([x1 * cos - x2 * sin, x1 * sin + x2 * cos], axis=-1)

        def l2_normalize(x, eps=EPS_L2):
            return x / (jnp.linalg.norm(x, axis=-1, keepdims=True) + eps)

        def variance_scaled_softmax(scores, eps=EPS_VAR):
            finite = jnp.isfinite(scores)
            m = finite.astype(scores.dtype)
            n = jnp.clip(jnp.sum(m, axis=-1, keepdims=True), 1.0, None)
            safe = jnp.where(finite, scores, 0.0)
            mean = jnp.sum(safe * m, axis=-1, keepdims=True) / n
            var = jnp.sum((safe - mean) ** 2 * m, axis=-1, keepdims=True) / n
            std = jnp.sqrt(jnp.clip(var, eps, None))
            scaled = jnp.where(finite, (safe - mean) / std, -jnp.inf)
            out = jax.nn.softmax(scaled, axis=-1)
            return jnp.where(n == 0, jnp.zeros_like(out), out)
        Bx, Tx, Cx = x.shape
        cos, sin = rope_tables(Tx, Cx)
        W_h = haar_basis(Tx, LEVELS)
        WK = jnp.linalg.pinv(W_Q)
        q = x @ W_Q
        k = x @ WK.T
        v = x @ W_V.T
        q = l2_normalize(apply_rope(q, cos, sin))
        k = l2_normalize(apply_rope(k, cos, sin))
        pos = jnp.arange(Tx)
        dist = pos[None, :] - pos[:, None]
        near_mask = (dist >= 0) & (dist <= NEAR_WINDOW)
        causal = dist <= 0
        scale = 1.0 / math.sqrt(Cx)
        attn_scores = jnp.einsum('btc,bsc->bts', q, k) * scale
        attn_near = jnp.where(near_mask, attn_scores, -jnp.inf)
        q_coef = jnp.einsum('tw,btc->bwc', W_h, q)
        k_coef = jnp.einsum('tw,btc->bwc', W_h, k)
        attn_coef = jnp.einsum('bwc,bvc->bwv', q_coef, k_coef) * scale
        attn_far = jnp.einsum('tw,bwv,sv->bts', W_h, attn_coef, W_h)
        attn = jnp.where(near_mask, attn_near, attn_far)
        attn = jnp.where(causal, attn, -jnp.inf)
        n_visible = jnp.clip(jnp.sum(jnp.isfinite(attn), axis=-1, keepdims=True).astype(attn.dtype), 1.0, None)
        attn = attn / jnp.sqrt(n_visible)
        attn = variance_scaled_softmax(attn)
        y = jnp.einsum('bts,bsc->btc', attn, v)
        return y @ W_O.T

    def _L0_ffn_ref(x, gate_w, gate_b, W1, b1, W2, b2):
        import jax, jax.numpy as jnp
        import numpy as np
        B, T, D, H, E = (16, 1024, 64, 128, 8)
        Bb, Tt, Dd = x.shape
        Ee = gate_w.shape[1]
        xf = x.reshape(-1, Dd)
        N = xf.shape[0]
        logits = xf @ gate_w + gate_b
        probs = jax.nn.softmax(logits, axis=-1)
        top2_vals, top2_idx = jax.lax.top_k(probs, 2)
        cw = jnp.zeros((N, Ee), dtype=xf.dtype).at[jnp.arange(N)[:, None], top2_idx].add(top2_vals)

        def step(acc, params):
            w1, bb1, w2, bb2, we = params
            h = jax.nn.gelu(xf @ w1 + bb1, approximate=False)
            y = h @ w2 + bb2
            return (acc + we[:, None] * y, None)
        out, _ = jax.lax.scan(step, jnp.zeros_like(xf), (W1, b1, W2, b2, cw.T))
        return out.reshape(Bb, Tt, Dd)
    h = _L0_tok_ref(x, L0_tok_W1, L0_tok_b1, L0_tok_W2, L0_tok_b2, L0_tok_W3, L0_tok_b3)
    h = jnp.concatenate([h, txt], axis=1)
    h = h + _L0_attn_ref(_layernorm(h, axis=-1), L0_attn_W_Q, L0_attn_W_V, L0_attn_W_O)
    h = h + _L0_ffn_ref(_layernorm(h, axis=-1), L0_ffn_gate_w, L0_ffn_gate_b, L0_ffn_W1, L0_ffn_b1, L0_ffn_W2, L0_ffn_b2)
    return h

_drawn_inputs = setup_inputs


def setup_inputs(seed=0):
    import zlib

    import numpy as np

    out = dict(_drawn_inputs(seed))
    spreads = {'L0_ffn_gate_b': (0.0, 0.1), 'L0_ffn_b1': (0.0, 0.8), 'L0_ffn_b2': (0.0, 0.1)}
    factors = {'L0_tok_b1': 8.0,
     'L0_attn_W_Q': 8.0,
     'L0_attn_W_V': 5.561,
     'L0_attn_W_O': 5.433,
     'L0_ffn_W1': 4.007,
     'L0_ffn_W2': 3.436}
    for name, (base, spread) in spreads.items():
        noise = np.random.default_rng([zlib.crc32(name.encode()), seed]).standard_normal(out[name].shape)
        drawn = base * np.exp(spread * noise) if base else spread * noise
        out[name] = jnp.asarray(drawn.astype(out[name].dtype))
    for name, factor in factors.items():
        out[name] = (out[name] * factor).astype(out[name].dtype)
    return out
```

```python
from contextlib import ExitStack

import numpy as np

import concourse.bass as bass
from concourse import mybir

ALU = mybir.AluOpType
ACT = mybir.ActivationFunctionType
AX = mybir.AxisListType
F32 = mybir.dt.float32
F32R = mybir.dt.float32r

B, C, HW, TXT = 4, 64, 56, 77
PW = HW + 2
SEQ = HW * HW + TXT
TP = 2 * HW
UR = 8
UN = UR * HW
UT = UN // TP
UPI = HW // UR
UNITS = B * UPI
TI = UPI * UT
TT = TI + 1
NT = B * TT
NU = NT // UT
XA_IMG = 3424
XH_IMG = 3368
STEP = UR * PW
CHUNKS = 5
E, HID = 8, 128
LEVELS = 3
EPS_LN, EPS_L2, EPS_VAR = 1e-5, 1e-8, 1e-6
SCALE = 1.0 / 8.0
PSTEPS = UNITS


def haar_rows():
    cols = []
    for j in range(LEVELS):
        bc = 2 ** j
        bs = SEQ // bc
        half = bs // 2
        for k in range(bc):
            v = np.zeros(SEQ)
            v[k * bs:k * bs + half] = 1 / np.sqrt(half)
            v[k * bs + half:(k + 1) * bs] = -1 / np.sqrt(half)
            cols.append(v)
    w = np.stack(cols, 1)
    starts = [0] + [t for t in range(1, SEQ) if (w[t] != w[t - 1]).any()]
    return starts, w[starts]


STARTS, HAAR = haar_rows()
NSEG = len(STARTS)
NF = NSEG - 1
NV = NF + 1
NSUM = TT + NF


def rho_schedule():
    low, out = 1e-9, []
    while low < 1 - 1e-7:
        r = 2 / (1 + low)
        out.append(r)
        low = 1 - (1 - r * low) ** 2
    return out + [1.0] * (PSTEPS - len(out))


SMALL = {}
TABLE = {}
_at = 0
for _n, _w in (("ident", 128), ("two_i", C), ("dup_i", 128), ("rho", PSTEPS), ("basis", NSEG), ("ones", C),
               ("half_pow", 2 * UT), ("neg_half_pow", NT), ("rank", E)):
    SMALL[_n] = (_at, _at + _w)
    _at += _w
NSMALL = _at
_at = 0
for _n, _w in (("cos", TT * 32), ("sin", TT * 32), ("sums", TT * NSUM), ("seg", TT * NSEG), ("count", TT * NV),
               ("absent", TT * NV), ("before", TT * NF), ("own", TT * NF), ("inv_n", TT), ("root_n", TT),
               ("prefix", TP)):
    TABLE[_n] = (_at, _at + _w)
    _at += _w
NTABLE = _at
WORK = 5008 + NTABLE


def make_tables():
    f = np.float32
    small = np.zeros((128, NSMALL), f)

    def put(arr, spans, name, value):
        a, b = spans[name]
        value = np.asarray(value, f).reshape(len(value), -1)
        arr[:value.shape[0], a:b] = value

    put(small, SMALL, "ident", np.eye(128))
    put(small, SMALL, "two_i", 2 * np.eye(C))
    put(small, SMALL, "dup_i", np.concatenate([np.eye(C)] * 2, 1))
    put(small, SMALL, "rho", np.tile(np.array(rho_schedule())[None], (128, 1)))
    put(small, SMALL, "basis", HAAR @ HAAR.T)
    put(small, SMALL, "ones", np.ones((128, C)))
    put(small, SMALL, "half_pow", np.full((128, 2 * UT), 0.5))
    put(small, SMALL, "neg_half_pow", np.full((128, NT), -0.5))
    put(small, SMALL, "rank", np.tile(np.arange(E, 0, -1)[None], (128, 1)))

    table = np.zeros((128, NTABLE), f)
    t = np.arange(TP)[:, None] + TP * np.arange(TT)[None, :]
    real = t < SEQ
    half = C // 2
    inv_freq = (1.0 / 10000.0 ** (np.arange(half, dtype=f) / half)).astype(f)
    ang = t.astype(f)[..., None] * inv_freq
    put(table, TABLE, "cos", np.cos(ang) * real[..., None])
    put(table, TABLE, "sin", np.sin(ang) * real[..., None])
    ends = STARTS[1:] + [SEQ]
    seg = np.searchsorted(STARTS, t, side="right") - 1
    onehot = (seg[..., None] == np.arange(NSEG)) & real[..., None]
    put(table, TABLE, "seg", onehot)
    sums = np.zeros((TP, TT, NSUM))
    for j in range(TT):
        sums[:, j, j + 1:TT] = 1
    sums *= real[..., None]
    sums[:, :, TT:] = onehot[:, :, :NF]
    put(table, TABLE, "sums", sums)
    count = np.ones((TP, TT, NV))
    for j in range(NF):
        count[:, :, j] = np.clip(t - STARTS[j], 0, ends[j] - STARTS[j]) * real
    put(table, TABLE, "count", count)
    put(table, TABLE, "absent", np.where(count > 0, 0.0, -1e30))
    put(table, TABLE, "before", (np.arange(NF) < seg[..., None]) & real[..., None])
    put(table, TABLE, "own", onehot[:, :, :NF])
    n = np.where(real, t + 1, 1).astype(f)
    put(table, TABLE, "inv_n", 1 / n)
    put(table, TABLE, "root_n", 1 / np.sqrt(n))
    prefix = np.zeros((TP + 1, TP))
    prefix[:TP] = np.triu(np.ones((TP, TP)), 1)
    prefix[TP] = 1
    put(table, TABLE, "prefix", prefix)
    seg_rows = np.zeros((NSEG, TT, TP), f)
    seg_rows[:] = onehot.transpose(2, 1, 0)
    return small, table, seg_rows.reshape(NSEG, TT * TP)


def is_zero(m):
    return isinstance(m, int) and m == 0


def build(nc, pair, txt, tok_w1, tok_b1, tok_w2, tok_b2, tok_w3, tok_b3, wq, wq_t, wv, wo_t,
          gate_w, gate_b, ffn_w1, ffn_b1, ffn_w2, ffn_b2, small, table, seg_rows, out):
    ctx = ExitStack()
    with ctx:
        def sb(name, cols, dt=F32):
            return ctx.enter_context(nc.sbuf_tensor(name, [128, cols], dt))

        def sem(name):
            return ctx.enter_context(nc.semaphore(name))

        h = sb("h", NT * C)
        vx = sb("vx", 2 * NT * C)
        stack = sb("stack", 4 * XH_IMG + UN, F32R)
        work = sb("work", WORK)
        wts = sb("wts", 3584, F32R)
        w3_sb = sb("w3_sb", CHUNKS * C)
        small_sb = sb("small_sb", NSMALL)
        bias = sb("bias", 1 + CHUNKS + E + C + E)
        stat = sb("stat", 3 * NT + 4 * UT)
        nrm = sb("nrm", 5 * NT)
        seg_q = sb("seg_q", B * 2 * NSEG)
        seg_v = sb("seg_v", B * NSUM)
        ps = ctx.enter_context(nc.psum_tensor("ps", [128, 8, 512], F32))

        def sm(name, rows=128):
            a, b = SMALL[name]
            return small_sb[0:rows, a:b]

        tb0 = WORK - NTABLE

        def tab(name, rows=TP):
            a, b = TABLE[name]
            return work[0:rows, tb0 + a:tb0 + b]

        def grid(ap, inner):
            return ap.rearrange("p (t c) -> p t c", c=inner)

        ident = sm("ident")
        b1_sb = bias[:, 0:1]
        b2_sb = bias[:, 1:1 + CHUNKS]
        eb1_sb = bias[:, 6:6 + E]
        b3_sb = bias[0:TP, 14:14 + C]
        gb_sb = bias[0:TP, 78:78 + E]

        pin = work[:, tb0:tb0 + 9 * C]
        xa = vx[:, 0:B * XA_IMG]
        xh = stack[:, 0:B * XH_IMG]
        hl = stack[:, B * XH_IMG:B * XH_IMG + UN]
        gates = work[:, 0:CHUNKS * UN]
        gated = work[:, CHUNKS * UN:2 * CHUNKS * UN]
        w1_raw = work[:, 0:9 * 128]
        w2_raw = work[:, 9 * 128:14 * 128]
        w1h, w1l = wts[:, 0:1152], wts[:, 1152:2304]
        w2h, w2l = wts[:, 2304:2944], wts[:, 2944:3584]
        qkvh, qkvl = wts[:, 0:192], wts[:, 192:384]
        gwh, gwl = wts[:, 2048:2056], wts[:, 2056:2064]
        hid = work[:, 4480:4480 + UN]
        a_in, a_t = pin[0:C, 8 * C:9 * C], pin[0:C, 0:C]
        a_tt = pin[0:C, 0:2 * C]
        xtx = pin[0:C, 2 * C:4 * C]
        xt, xx = xtx[:, 0:C], xtx[:, C:2 * C]
        resid = pin[0:C, 4 * C:5 * C]
        wv_sb = pin[0:C, 5 * C:7 * C]
        wo_sb = pin[0:C, 7 * C:8 * C]
        rowsum, rowmax, bound, bound_inv = (stat[0:C, i:i + 1] for i in range(4))

        vals = vx[:, 0:NT * C]
        xc = vx[0:TP, NT * C:2 * NT * C]
        sq = {ln: [work[0:TP, a + i * 1856:a + (i + 1) * 1856] for i in range(2)]
              for ln, a in (("ln1_", 0), ("ln2_", tb0))}
        nmean, vare, rstd = (stat[0:TP, i * NT:(i + 1) * NT] for i in range(3))
        xn = [work[0:TP, i * 256:(i + 1) * 256] for i in range(2)]
        qkv = [grid(work[0:TP, 512 + i * 768:512 + (i + 1) * 768], 192) for i in range(2)]
        prod = grid(work[0:TP, 2048:2816], 192)
        mcos = work[0:TP, 2816:3328].rearrange("p (t g d) -> p t g d", g=4, d=32)
        msin = work[0:TP, 3328:3840].rearrange("p (t g d) -> p t g d", g=4, d=32)
        rot = [work[0:TP, 3840 + i * 512:3840 + (i + 1) * 512] for i in range(2)]
        inv_u = [stat[0:TP, 3 * NT + i * 8:3 * NT + (i + 1) * 8] for i in range(2)]
        segw = [work[0:TP, 4864 + i * 72:4864 + (i + 1) * 72] for i in range(2)]
        assert 5008 <= tb0
        tok_hl = [stack[0:TP, i * 512:(i + 1) * 512] for i in range(2)]
        tok_t = [stack[:, 1024 + i * UN:1024 + (i + 1) * UN] for i in range(2)]
        dots = nrm[0:TP, 0:3 * NT]
        inv = nrm[0:TP, 3 * NT:5 * NT]

        NR = TT * B * NV
        segr = vx[0:NSEG, NT * C:NT * C + TT * TP]
        val, dev, sqv, ex = (vx[0:TP, NT * C + TT * TP + i * NR:NT * C + TT * TP + (i + 1) * NR] for i in range(4))
        ks0 = work[0:C, 0:72]
        qk9 = work[0:NSEG, 72:108]
        bq9 = work[0:NSEG, 108:144]
        far9 = work[0:NSEG, 144:144 + B * NF]
        vpick = work[0:C, 176:176 + 128]
        vseg = work[0:B * NF, 304:560]
        carry = work[0:TT, 560:816]
        mean1, mean2, mean3, den = (work[0:TP, 816 + i * 116:816 + (i + 1) * 116] for i in range(4))
        wown, wdiag = (work[0:TP, 1280 + i * 116:1280 + (i + 1) * 116] for i in range(2))
        dwt = work[0:TP, 1512:1512 + TT * B * NF]
        dwr = [work[0:TP, 2440 + i * 32:2440 + (i + 1) * 32] for i in range(2)]
        dwT = [work[0:B * NF, 2504 + i * TP:2504 + (i + 1) * TP] for i in range(2)]
        far_part = [work[0:TP, 2728 + i * 256:2728 + (i + 1) * 256] for i in range(2)]
        self_part = [work[0:TP, 3240 + i * 256:3240 + (i + 1) * 256] for i in range(2)]

        all_t = stack[:, 0:NU * UN]
        hl2 = [work[0:TP, 512 + i * 512:512 + (i + 1) * 512] for i in range(2)]
        logit_s = [work[0:E, 1536 + i * UN:1536 + (i + 1) * UN] for i in range(2)]
        ew1_raw = work[:, 2432:2432 + 1024]
        ew2_sb = work[:, 3456:3456 + 512]
        gw_raw = work[:, 3968:3976]
        eb2_blk = work[:, 3976:3976 + 1024]
        ew1h, ew1l = wts[:, 0:1024], wts[:, 1024:2048]
        g0 = NT * C
        logit = vx[0:TP, 6400:6400 + 928]
        prob, pick, keep, cand, last_p = (vx[0:TP, g0 + i * 928:g0 + (i + 1) * 928] for i in range(5))
        cw = vx[0:TP, g0 + 5 * 928:g0 + 6 * 928]
        cw_t = vx[:, 0:8 * TP]
        gtop, gsum = stat[0:TP, 0:NT], stat[0:TP, NT:2 * NT]
        act_g = [vx[:, 1024 + i * UN:1024 + (i + 1) * UN] for i in range(4)]
        wy = vx[0:TP, 3072:3072 + 2048]
        wsum = vx[0:TP, 5120:5376]

        carry_rows = nc.dram_tensor("carry_rows", [B, TT, C], F32, kind="Internal").ap()

        names = """d_small d_tokw d_img0 d_img1 d_img2 d_img3 d_txt d_pin d_table d_segr d_rows d_carry d_ffnw d_ffn2 d_out
        z_text w_split x_hi x_up x_lo h1_ps h1_relu h1_step hl_ready s_ps s_sig u_ready o_ps o_out
        p_init p_chain x_ready p_ps r_ready xn_ps w_ps w_hi w_ready
        ln1_mean ln1_xc ln1_sq ln1_s2 ln1_var ln1_rstd ln1_m ln2_mean ln2_xc ln2_sq ln2_s2 ln2_var ln2_rstd ln2_m
        q_xn q_hi q_lo q_tps q_t q_ps q_sb q_v q_sq q_qk q_dots q_root q_rooteps q_inv q_invs q_segw q_cos q_sin q_rot1 q_rot2
        q_sums q_acc
        f_ps f_sb f_dve f_far f_carry f_vsb f_exp f_pow f_mean f_dw f_pool
        y_dwr y_dps y_dwt y_ps y_far y_self y_self2 y_mix y_sum y_h
        g_xn g_hi g_lo g_tps g_t g_ps g_sb g_lps g_logit g_w g_whi g_ew g_dve g_exp g_cwps g_cwt g_bps g_bias
        e_h e_g e_y e_used e_red e_out""".split()
        s = {n: sem(n) for n in names}

        block = ctx.enter_context(nc.Block())
        groups = range(B)
        GT = TT
        d_img = [s["d_img0"], s["d_img1"], s["d_img2"], s["d_img3"]]

        def tiles(buf, start, n, inner=C):
            return grid(buf[:, bass.ds(start * inner, n * inner)], inner)

        def window(buf, lo, hi, off):
            return buf[lo:hi, bass.ds(off, STEP)].rearrange("p (r w) -> p r w", w=PW)[:, :, 0:HW]

        def tile_major(buf, width):
            return buf.rearrange("p (t c) -> p t c", c=width)

        def spread(ap, n):
            return ap.unsqueeze(2).to_broadcast([ap.shape[0], ap.shape[1], n])

        def rope_table(name, r, text):
            if text:
                return tab(name)[:, TI * 32:TT * 32].unsqueeze(1).unsqueeze(1).to_broadcast([TP, UT, 4, 32])
            return tab(name)[:, bass.ds(r * 32, UT * 32)].rearrange("p (t d) -> p t d", d=32).unsqueeze(2)\
                .to_broadcast([TP, UT, 4, 32])

        def rows_of(buf, j, text):
            if text:
                return tiles(buf[0:TP, :], B * TI, B)
            return buf[0:TP, 0:B * TI * C].rearrange("p (b t c) -> p b t c", b=B, c=C)[:, :, bass.ds(j, 1), :]\
                .rearrange("p b o c -> p b (o c)")

        @block.sync
        def _(sp):
            sp.dma_start(small_sb[:, :], small).then_inc(s["d_small"], 16)
            sp.dma_start(w1_raw, tok_w1).then_inc(s["d_tokw"], 16)
            sp.dma_start(w2_raw, tok_w2).then_inc(s["d_tokw"], 16)
            sp.dma_start(xa[:, 0:XA_IMG], pair[0]).then_inc(s["d_img0"], 16)
            sp.dma_start(b1_sb, tok_b1).then_inc(s["d_tokw"], 16)
            sp.dma_start(b2_sb, tok_b2).then_inc(s["d_tokw"], 16)
            sp.dma_start(w3_sb[:, :], tok_w3).then_inc(s["d_tokw"], 16)
            sp.dma_start(b3_sb, tok_b3).then_inc(s["d_tokw"], 16)
            sp.dma_start(eb1_sb, ffn_b1).then_inc(s["d_tokw"], 16)
            sp.dma_start(gb_sb, gate_b).then_inc(s["d_tokw"], 16)
            sp.dma_start(a_in, wq).then_inc(s["d_pin"], 16)
            sp.dma_start(a_tt, wq_t).then_inc(s["d_pin"], 16)
            sp.dma_start(wv_sb, wv).then_inc(s["d_pin"], 16)
            sp.dma_start(wo_sb, wo_t).then_inc(s["d_pin"], 16)
            for b in range(1, B):
                sp.dma_start(xa[:, b * XA_IMG:(b + 1) * XA_IMG], pair[b]).then_inc(d_img[b], 16)
            sp.wait_ge(s["z_text"], 1)
            for b in range(B):
                k = B * TI + b
                sp.dma_start(h[0:TXT, k * C:(k + 1) * C], txt[b]).then_inc(s["d_txt"], 16)
            sp.wait_ge(s["o_ps"], UNITS)
            sp.wait_ge(s["w_ps"], 1)
            sp.dma_start(work[:, tb0:tb0 + NTABLE], table).then_inc(s["d_table"], 16)
            sp.wait_ge(s["q_xn"], NU)
            sp.dma_start(segr, seg_rows).then_inc(s["d_segr"], 16)
            sp.wait_ge(s["f_carry"], 1)
            sp.dma_start(carry_rows.rearrange("b t c -> t b c"), carry.rearrange("t (b c) -> t b c", c=C))\
              .then_inc(s["d_rows"], 16)
            sp.wait_ge(s["d_rows"], 16)
            crow = vals[TP:TP + 1, :]
            sp.dma_start(crow[:, 0:B * TI * C].rearrange("o (b k) -> o b k", b=B),
                         carry_rows[:, 0:TI, :].rearrange("(o b) t c -> o b (t c)", o=1)).then_inc(s["d_carry"], 16)
            sp.dma_start(crow[:, B * TI * C:NT * C].rearrange("o (b c) -> o b c", b=B),
                         carry_rows[:, TI:TT, :].rearrange("(o b) t c -> o b (t c)", o=1)).then_inc(s["d_carry"], 16)
            sp.wait_ge(s["y_h"], TT)
            sp.wait_ge(s["y_ps"], TT)
            sp.dma_start(gw_raw, gate_w).then_inc(s["d_ffnw"], 16)
            sp.dma_start(ew1_raw, ffn_w1).then_inc(s["d_ffnw"], 16)
            sp.dma_start(ew2_sb, ffn_w2).then_inc(s["d_ffn2"], 16)
            sp.dma_start(eb2_blk, ffn_b2).then_inc(s["d_ffn2"], 16)
            out_rows = out.rearrange("b s c -> (b s) c")
            with sp.Fori(0, UNITS) as m:
                sp.wait_ge(s["e_out"], m + 1)
                b = m // UPI
                dst = out_rows[bass.ds(m * UN + b * TXT, UN), :].rearrange("(t p) c -> p t c", p=TP)
                sp.dma_start(dst, tiles(h[0:TP, :], m * UT, UT)).then_inc(s["d_out"], 16)
            sp.wait_ge(s["e_out"], NU)
            for b in range(B):
                k = B * TI + b
                sp.dma_start(out[b, HW * HW:SEQ, :], h[0:TXT, k * C:(k + 1) * C]).then_inc(s["d_out"], 16)
            sp.wait_ge(s["d_out"], 16 * (UNITS + B))

        def ln_vector(eng, ln):
            for g in groups:
                a = slice(g * GT, (g + 1) * GT)
                eng.tensor_reduce(nmean[:, a], tile_major(h[0:TP, g * GT * C:(g + 1) * GT * C], C), AX.X,
                                  ALU.add).then_inc(s[ln + "m"], 1)
            for g in groups:
                a = slice(g * GT, (g + 1) * GT)
                eng.wait_ge(s[ln + "m"], g + 1)
                eng.tensor_scalar(nmean[:, a], nmean[:, a], -1.0 / C, None, ALU.mult).then_inc(s[ln + "mean"], 1)
            for g in groups:
                a = slice(g * GT, (g + 1) * GT)
                eng.wait_ge(s[ln + "sq"], g + 1)
                eng.tensor_reduce(vare[:, a], tile_major(sq[ln][g % 2], C), AX.X, ALU.add).then_inc(s[ln + "s2"], 1)
                eng.wait_ge(s[ln + "s2"], g + 1)
                eng.tensor_scalar(vare[:, a], vare[:, a], 1.0 / C, EPS_LN, ALU.mult, ALU.add)\
                   .then_inc(s[ln + "var"], 1)

        def ln_pool(eng, ln):
            for g in groups:
                a = slice(g * GT, (g + 1) * GT)
                c = slice(g * GT * C, (g + 1) * GT * C)
                eng.wait_ge(s[ln + "mean"], g + 1)
                eng.tensor_tensor(tile_major(xc[:, c], C), tile_major(h[0:TP, c], C), spread(nmean[:, a], C),
                                  ALU.add).then_inc(s[ln + "xc"], 1)
            for g in groups:
                a = slice(g * GT, (g + 1) * GT)
                eng.wait_ge(s[ln + "var"], g + 1)
                eng.tensor_tensor(rstd[:, a], vare[:, a], sm("neg_half_pow", TP)[:, a], ALU.pow)\
                   .then_inc(s[ln + "rstd"], 1)

        def ln_scalar(eng, ln):
            for g in groups:
                c = slice(g * GT * C, (g + 1) * GT * C)
                eng.wait_ge(s[ln + "xc"], g + 1)
                if g >= 2:
                    eng.wait_ge(s[ln + "s2"], g - 1)
                eng.activation(sq[ln][g % 2], xc[:, c], ACT.Square).then_inc(s[ln + "sq"], 1)

        def in_pairs(eng, body):
            body(0, 0, True)
            body(1, 1, True)
            with eng.Fori(1, NU // 2) as i:
                body(2 * i, 0, False)
                body(2 * i + 1, 1, False)
            body(NU - 1, 0, False)

        @block.tensor
        def _(pe):
            def conv(off, last=False):
                n = 0
                for w in (w1h, w1l):
                    for tap in range(9):
                        mm = pe.matmul(ps[:, 0, 0:UN], w[:, tap * 128:(tap + 1) * 128],
                                       window(xh, 0, 128, off + (tap // 3) * PW + tap % 3),
                                       start=(n == 0), stop=(n == 17))
                        n += 1
                mm.then_inc(s["h1_ps"], 1)

            pe.wait_ge(s["d_pin"], 64)
            pe.wait_ge(s["d_small"], 16)
            pe.matmul(ps[0:C, 7, 0:C], a_t, a_t, start=True, stop=True).then_inc(s["p_init"], 1)
            pe.wait_ge(s["p_chain"], 1)
            pe.transpose(ps[0:1, 7, 64:128], rowsum, ident[0:C, 0:C]).then_inc(s["p_init"], 1)
            pe.wait_ge(s["p_chain"], 2)
            pe.matmul(ps[0:C, 7, 128:129], sm("ones", 1)[:, 0:C], rowmax[0:1, :], start=True, stop=True)\
              .then_inc(s["p_init"], 1)

            pe.wait_ge(s["w_split"], 4)
            pe.wait_ge(s["x_hi"], 1)
            pe.wait_ge(s["x_lo"], 1)
            conv(0)

            def unit(n, last):
                pe.wait_ge(s["hl_ready"], n + 1)
                for k in range(CHUNKS):
                    pe.matmul(ps[:, 1 + k, 0:UN], w2h[:, k * 128:(k + 1) * 128], hl, start=True, stop=False)
                    pe.matmul(ps[:, 1 + k, 0:UN], w2l[:, k * 128:(k + 1) * 128], hl, start=False, stop=True)\
                      .then_inc(s["s_ps"], 1)
                pe.wait_ge(s["x_ready"], n + 1)
                pe.matmul(ps[:, 7, 0:C], a_tt, xx, start=True, stop=True).then_inc(s["p_ps"], 1)
                if not last:
                    b = (n + 1) // UPI
                    pe.wait_ge(s["x_hi"], b + 1)
                    pe.wait_ge(s["x_lo"], b + 1)
                    conv((n + 1) * STEP + b * (XH_IMG - UPI * STEP))
                pe.wait_ge(s["r_ready"], n + 1)
                pe.matmul(ps[:, 7, 128:192], xtx, resid, start=True, stop=True)
                pe.matmul(ps[0:C, 7, 64:128], resid, xt, start=True, stop=True)\
                  .then_inc(s["xn_ps"], 1)
                pe.wait_ge(s["u_ready"], CHUNKS * n + CHUNKS)
                for t in range(UT):
                    for k in range(CHUNKS):
                        mm = pe.matmul(ps[0:TP, 6, t * C:(t + 1) * C],
                                       gated[:, k * UN + t * TP:k * UN + (t + 1) * TP],
                                       w3_sb[:, k * C:(k + 1) * C], start=(k == 0), stop=(k == CHUNKS - 1))
                mm.then_inc(s["o_ps"], 1)

            with pe.Fori(0, UNITS - 1) as n:
                unit(n, False)
            unit(UNITS - 1, True)

            pe.wait_ge(s["x_ready"], UNITS + 1)
            pe.matmul(ps[:, 0, 0:C], sm("dup_i", C), a_in, start=True, stop=True)
            pe.matmul(ps[:, 0, C:2 * C], sm("dup_i", C), xt, start=True, stop=True)
            pe.matmul(ps[:, 0, 2 * C:3 * C], wv_sb, wo_sb, start=True, stop=True).then_inc(s["w_ps"], 1)

            def project(m, p, first):
                pe.wait_ge(s["q_lo"], m + 1)
                if not first:
                    pe.wait_ge(s["q_t"], m - 1)
                for t in range(UT):
                    mm = pe.transpose(ps[:, 1 + p, t * TP:(t + 1) * TP],
                                      tok_hl[p][:, t * 128:(t + 1) * 128].bitcast(F32), ident[0:TP, 0:TP])
                mm.then_inc(s["q_tps"], 1)
                pe.wait_ge(s["q_t"], m + 1)
                if is_zero(m):
                    pe.wait_ge(s["w_ready"], 1)
                else:
                    pe.wait_ge(s["q_sb"], m)
                for t in range(UT):
                    for n, w in enumerate((qkvh, qkvl)):
                        mm = pe.matmul(ps[0:TP, 3 + t // 2, t % 2 * 192:t % 2 * 192 + 192],
                                       tok_t[p][:, t * TP:(t + 1) * TP], w, start=(n == 0), stop=(n == 1))
                mm.then_inc(s["q_ps"], 1)

            def sums(m, p, first, text=False):
                pe.wait_ge(s["q_rot2"], m + 1)
                pe.wait_ge(s["q_rot1"], m + 1)
                pe.wait_ge(s["q_segw"], m + 1)
                if not is_zero(m):
                    pe.wait_ge(s["q_acc"], 2 * m)
                r = TI if text else m % UPI * UT
                for t in range(UT):
                    o = ps[:, 5, t * 18:(t + 1) * 18] if text else ps[:, 5, 0:18]
                    pe.matmul(o, rot[p][:, t * 128:(t + 1) * 128], segw[p][:, t * 18:(t + 1) * 18],
                              start=(text or t == 0), stop=(text or t == UT - 1))
                for t in range(UT):
                    j = r if text else r + t
                    o = ps[0:C, 6, t * NSUM:(t + 1) * NSUM] if text else ps[0:C, 6, 0:NSUM]
                    mm = pe.matmul(o, qkv[p][:, t, 128:192], tab("sums")[:, bass.ds(j * NSUM, NSUM)],
                                   start=(text or t == 0), stop=(text or t == UT - 1))
                mm.then_inc(s["q_sums"], 1)

            pe.wait_ge(s["d_table"], 16)
            project(0, 0, True)
            project(1, 1, True)
            sums(0, 0, True)
            project(2, 0, False)
            sums(1, 1, True)
            with pe.Fori(1, NU // 2 - 1) as i:
                project(2 * i + 1, 1, False)
                sums(2 * i, 0, False)
                project(2 * i + 2, 0, False)
                sums(2 * i + 1, 1, False)
            m = NU - 3
            project(m + 1, 1, False)
            sums(m, 0, False)
            project(m + 2, 0, False)
            sums(m + 1, 1, False)
            sums(NU - 1, 0, False, text=True)

            pe.wait_ge(s["q_acc"], 2 * NU)
            pe.matmul(ps[0:C, 0, 0:72], ident[:, C:128], seg_q[:, :], start=True, stop=True)\
              .then_inc(s["f_ps"], 1)
            pe.wait_ge(s["f_sb"], 1)
            for b in range(B):
                mm = pe.matmul(ps[0:NSEG, 1, b * NSEG:(b + 1) * NSEG], seg_q[0:C, b * 18:b * 18 + NSEG],
                               ks0[:, b * 18 + NSEG:(b + 1) * 18], start=True, stop=True)
            mm.then_inc(s["f_ps"], 1)
            pe.wait_ge(s["f_sb"], 2)
            for b in range(B):
                mm = pe.matmul(ps[0:NSEG, 2, b * NSEG:(b + 1) * NSEG], qk9[:, b * NSEG:(b + 1) * NSEG],
                               sm("basis", NSEG), start=True, stop=True)
            mm.then_inc(s["f_ps"], 1)
            pe.wait_ge(s["f_sb"], 3)
            for b in range(B):
                mm = pe.matmul(ps[0:NSEG, 0, b * NF:(b + 1) * NF], bq9[:, b * NSEG:(b + 1) * NSEG],
                               sm("basis", NSEG)[:, 0:NF], start=True, stop=True)
            mm.then_inc(s["f_ps"], 1)
            for b in range(B):
                mm = pe.transpose(ps[0:TT, 3, b * C:(b + 1) * C], seg_v[0:C, b * NSUM:b * NSUM + TT], ident[0:C, 0:C])
            mm.then_inc(s["f_ps"], 1)
            pe.wait_ge(s["f_vsb"], 1)
            for b in range(B):
                mm = pe.matmul(ps[0:B * NF, 4, b * C:(b + 1) * C], vpick[:, b * 32:(b + 1) * 32], ident[0:C, 0:C],
                               start=True, stop=True)
            mm.then_inc(s["f_ps"], 1)
            pe.wait_ge(s["f_sb"], 4)
            pe.wait_ge(s["d_segr"], 16)
            for j in range(TT):
                mm = pe.matmul(ps[0:TP, 5 + j // 16, j % 16 * 32:j % 16 * 32 + 32], segr[:, j * TP:(j + 1) * TP],
                               far9, start=True, stop=True)
            mm.then_inc(s["f_far"], 1)

            pe.wait_ge(s["f_vsb"], 2)
            pe.wait_ge(s["d_carry"], 32)

            def attend(j, p, first, text=False):
                pe.wait_ge(s["y_dwr"], j + 1)
                if not first:
                    pe.wait_ge(s["y_sum"], j - 1)
                pe.transpose(ps[0:B * NF, p, 0:TP], dwr[p], ident[0:TP, 0:TP]).then_inc(s["y_dps"], 1)
                v = (tiles(vals[0:TP + 1, :], B * TI, B) if text else
                     vals[0:TP + 1, 0:B * TI * C].rearrange("p (b t c) -> p b t c", b=B, c=C)[:, :, bass.ds(j, 1), :]
                     .rearrange("p b o c -> p b (o c)"))
                pe.matmul(ps[0:TP, 2 + p, 0:256], tab("prefix", TP + 1), v, start=True, stop=True)
                pe.wait_ge(s["y_dwt"], j + 1)
                pe.matmul(ps[0:TP, 4 + p, 0:256], dwT[p], vseg, start=True, stop=True).then_inc(s["y_ps"], 1)

            attend(0, 0, True)
            attend(1, 1, True)
            with pe.Fori(1, TI // 2) as i:
                attend(2 * i, 0, False)
                attend(2 * i + 1, 1, False)
            attend(TI, 0, False, text=True)

            def route(m, p, first):
                pe.wait_ge(s["g_lo"], m + 1)
                if not first:
                    pe.wait_ge(s["g_t"], m - 1)
                for t in range(UT):
                    mm = pe.transpose(ps[:, p, t * TP:(t + 1) * TP], hl2[p][:, t * 128:(t + 1) * 128],
                                      ident[0:TP, 0:TP])
                mm.then_inc(s["g_tps"], 1)
                pe.wait_ge(s["g_t"], m + 1)
                if is_zero(m):
                    pe.wait_ge(s["g_w"], 1)
                if not first:
                    pe.wait_ge(s["g_sb"], m - 1)
                for n, w in enumerate((gwh, gwl)):
                    mm = pe.matmul(ps[0:E, 2 + p, 0:UN], w, all_t[:, bass.ds(m * UN, UN)],
                                   start=(n == 0), stop=(n == 1))
                mm.then_inc(s["g_ps"], 1)
                pe.wait_ge(s["g_sb"], m + 1)
                if not first:
                    pe.wait_ge(s["g_logit"], m - 1)
                for t in range(UT):
                    mm = pe.matmul(ps[0:TP, 4 + p, t * E:(t + 1) * E], logit_s[p][:, t * TP:(t + 1) * TP],
                                   ident[0:E, 0:E], start=True, stop=True)
                mm.then_inc(s["g_lps"], 1)

            in_pairs(pe, route)

            pe.wait_ge(s["g_cwps"], 1)
            for g in range(8):
                n = min(16, NT - 16 * g)
                mm = pe.transpose(ps[0:n * E, 6 + g // 4, g % 4 * TP:(g % 4 + 1) * TP],
                                  cw[:, g * 128:g * 128 + n * E], ident[0:TP, 0:TP])
            mm.then_inc(s["g_cwt"], 1)
            pe.wait_ge(s["d_ffn2"], 32)
            pe.wait_ge(s["g_cwt"], 2)
            for g in range(15):
                n = min(8, NT - 8 * g)
                k = min(16, NT - 16 * (g // 2)) * E
                if g >= 4:
                    pe.wait_ge(s["g_bias"], g - 3)
                pe.matmul(ps[0:TP, g % 4, 0:n * C], cw_t[0:k, g // 2 * TP:(g // 2 + 1) * TP],
                          eb2_blk[0:k, g % 2 * 512:g % 2 * 512 + n * C], start=True, stop=True)\
                  .then_inc(s["g_bps"], 1)

            pe.wait_ge(s["g_ew"], 1)
            pe.wait_ge(s["g_bias"], 15)

            def hidden(m, e):
                pe.matmul(ps[:, e % 4, 0:UN], ew1h[:, e * HID:(e + 1) * HID], all_t[:, bass.ds(m * UN, UN)],
                          start=True, stop=False)
                pe.matmul(ps[:, e % 4, 0:UN], ew1l[:, e * HID:(e + 1) * HID], all_t[:, bass.ds(m * UN, UN)],
                          start=False, stop=True).then_inc(s["e_h"], 1)

            def experts(m, first, last):
                for e in range(E):
                    if e < E - 2:
                        hidden(m, e + 2)
                    elif not last:
                        hidden(m + 1, e + 2 - E)
                    if e % 4 == 0 and not first:
                        pe.wait_ge(s["e_used"], 2 * m + e // 4 - 1)
                    pe.wait_ge(s["e_g"], E * m + e + 1)
                    for t in range(UT):
                        col = t % 2 * 256 + e % 4 * C
                        mm = pe.matmul(ps[0:TP, 4 + e // 4 * 2 + t // 2, col:col + C], act_g[e % 4][:, t * TP:(t + 1) * TP],
                                       ew2_sb[:, e * C:(e + 1) * C], start=True, stop=True)
                    if e % 4 == 3:
                        mm.then_inc(s["e_y"], 1)

            hidden(0, 0)
            hidden(0, 1)
            experts(0, True, False)
            with pe.Fori(1, NU - 1) as m:
                experts(m, False, False)
            experts(NU - 1, False, True)

        @block.scalar
        def _(act):
            for b in range(B):
                act.wait_ge(d_img[b], 16)
                act.activation(xh[0:C, b * XH_IMG:b * XH_IMG + PW * PW],
                               xa[0:C, b * XA_IMG + PW:b * XA_IMG + PW + PW * PW], ACT.Copy).then_inc(s["x_hi"], 1)
                if b == 0:
                    act.wait_ge(s["h1_ps"], 1)
                    act.wait_ge(s["d_tokw"], 128)
                    act.activation(hid, ps[:, 0, 0:UN], ACT.Relu, bias=b1_sb).then_inc(s["h1_relu"], 1)

            def gates_of(n):
                for k in range(CHUNKS):
                    act.wait_ge(s["s_ps"], CHUNKS * n + k + 1)
                    act.activation(gates[:, k * UN:(k + 1) * UN], ps[:, 1 + k, 0:UN], ACT.Sigmoid,
                                   bias=b2_sb[:, k:k + 1]).then_inc(s["s_sig"], 1)

            with act.Fori(0, UNITS - 1) as n:
                gates_of(n)
                act.wait_ge(s["h1_ps"], n + 2)
                act.activation(hid, ps[:, 0, 0:UN], ACT.Relu, bias=b1_sb).then_inc(s["h1_relu"], 1)
            gates_of(UNITS - 1)

            ln_scalar(act, "ln1_")

            def front(m, p, first):
                act.wait_ge(s["q_xn"], m + 1)
                if not first:
                    act.wait_ge(s["q_tps"], m - 1)
                hi = tile_major(tok_hl[p], 128)[:, :, 0:C]
                act.activation(hi, tile_major(xn[p], C), ACT.Copy).then_inc(s["q_hi"], 1)
                act.wait_ge(s["q_tps"], m + 1)
                if not first:
                    act.wait_ge(s["q_ps"], m - 1)
                act.activation(tok_t[p], ps[:, 1 + p, 0:UN], ACT.Copy).then_inc(s["q_t"], 1)

            def back(m, p, first):
                act.wait_ge(s["q_ps"], m + 1)
                if not first:
                    act.wait_ge(s["q_sums"], m - 1)
                    act.wait_ge(s["q_v"], m - 1)
                act.activation(qkv[p].rearrange("p (b t) c -> p b (t c)", b=2), ps[0:TP, 3:5, 0:384], ACT.Copy)\
                   .then_inc(s["q_sb"], 1)
                act.wait_ge(s["q_sb"], m + 1)
                if not is_zero(m):
                    act.wait_ge(s["q_dots"], m)
                act.activation(prod[:, :, 0:128], qkv[p][:, :, 0:128], ACT.Square).then_inc(s["q_sq"], 1)

            front(0, 0, True)
            front(1, 1, True)
            back(0, 0, True)
            front(2, 0, False)
            back(1, 1, True)
            with act.Fori(1, NU // 2 - 1) as i:
                front(2 * i + 1, 1, False)
                back(2 * i, 0, False)
                front(2 * i + 2, 0, False)
                back(2 * i + 1, 1, False)
            m = NU - 3
            front(m + 1, 1, False)
            back(m, 0, False)
            front(m + 2, 0, False)
            back(m + 1, 1, False)
            back(NU - 1, 0, False)

            act.wait_ge(s["f_exp"], 1)
            act.activation(ex, dev, ACT.Exp).then_inc(s["f_exp"], 1)

            def turned(j, p, first):
                act.wait_ge(s["y_dps"], j + 1)
                if not first:
                    act.wait_ge(s["y_ps"], j - 1)
                act.activation(dwT[p], ps[0:B * NF, p, 0:TP], ACT.Copy).then_inc(s["y_dwt"], 1)

            turned(0, 0, True)
            turned(1, 1, True)
            with act.Fori(1, TI // 2) as i:
                turned(2 * i, 0, False)
                turned(2 * i + 1, 1, False)
            turned(TI, 0, False)

            ln_scalar(act, "ln2_")

            def route_hi(m, p, first):
                act.wait_ge(s["g_xn"], m + 1)
                if not first:
                    act.wait_ge(s["g_tps"], m - 1)
                hi = tile_major(hl2[p], 128)[:, :, 0:C].bitcast(F32R)
                act.activation(hi, tile_major(xn[p], C), ACT.Copy).then_inc(s["g_hi"], 1)

            def route_t(m, p, first):
                act.wait_ge(s["g_tps"], m + 1)
                act.activation(all_t[:, bass.ds(m * UN, UN)], ps[:, p, 0:UN], ACT.Copy).then_inc(s["g_t"], 1)
                act.wait_ge(s["g_ps"], m + 1)
                if not first:
                    act.wait_ge(s["g_lps"], m - 1)
                act.activation(logit_s[p], ps[0:E, 2 + p, 0:UN], ACT.Copy).then_inc(s["g_sb"], 1)

            def both(m, p, first):
                route_hi(m, p, first)
                route_t(m, p, first)

            in_pairs(act, both)

            act.wait_ge(s["g_exp"], 1)
            act.activation(prob, pick, ACT.Exp).then_inc(s["g_exp"], 1)

            act.wait_ge(s["g_bias"], 15)
            with act.Fori(0, NU) as m:
                for e in range(E):
                    act.wait_ge(s["e_h"], E * m + e + 1)
                    act.activation(act_g[e % 4], ps[:, e % 4, 0:UN], ACT.Gelu, bias=eb1_sb[:, e:e + 1])\
                       .then_inc(s["e_g"], 1)

        @block.gpsimd
        def _(pool):
            pool.memset(h[0:TP, B * TI * C:NT * C], 0.0).then_inc(s["z_text"], 1)
            pool.wait_ge(s["z_text"], 1)
            for b in range(1, B):
                pool.wait_ge(s["x_up"], b + 1)
                up = xh[C:128, b * XH_IMG:b * XH_IMG + PW * PW]
                pool.tensor_tensor(up, xa[C:128, b * XA_IMG:b * XA_IMG + PW * PW], up.bitcast(F32),
                                   ALU.subtract).then_inc(s["x_lo"], 1)

            pool.wait_ge(s["x_lo"], B)
            pool.wait_ge(s["d_txt"], 64)
            ln_pool(pool, "ln1_")
            pool.wait_ge(s["d_table"], 16)

            def qkv_pool(m, p, first, text=False):
                pool.wait_ge(s["q_hi"], m + 1)
                t3 = tile_major(tok_hl[p], 128)
                pool.tensor_tensor(t3[:, :, C:128], tile_major(xn[p], C), t3[:, :, 0:C].bitcast(F32),
                                   ALU.subtract).then_inc(s["q_lo"], 1)

            def qkv_pool2(m, p, first, text=False):
                r = TI if text else m % UPI * UT
                pool.wait_ge(s["q_sb"], m + 1)
                pool.tensor_copy(tiles(vals[0:TP, :], m * UT, UT), qkv[p][:, :, 128:192]).then_inc(s["q_v"], 1)
                if not is_zero(m):
                    pool.wait_ge(s["q_dots"], m)
                pool.tensor_tensor(prod[:, :, 128:192], qkv[p][:, :, 0:64], qkv[p][:, :, 64:128], ALU.mult)\
                    .then_inc(s["q_qk"], 1)
                if not is_zero(m):
                    pool.wait_ge(s["q_rot2"], m)
                cos = rope_table("cos", r, text)
                pool.tensor_tensor(mcos, qkv[p][:, :, 0:128].rearrange("p t (g d) -> p t g d", d=32), cos,
                                   ALU.mult).then_inc(s["q_cos"], 1)
                pool.wait_ge(s["q_dots"], m + 1)
                d = tiles(dots, m * UT, UT, 3)[:, :, 0:2]
                if not first:
                    pool.wait_ge(s["q_invs"], m - 1)
                pool.tensor_tensor(inv_u[p].rearrange("p (t c) -> p t c", c=2), d, sm("half_pow", TP)[:, 0:2 * UT].rearrange("p (t c) -> p t c", c=2),
                                   ALU.pow).then_inc(s["q_root"], 1)

            qkv_pool(0, 0, True)
            qkv_pool(1, 1, True)
            qkv_pool2(0, 0, True)
            qkv_pool(2, 0, False)
            qkv_pool2(1, 1, True)
            with pool.Fori(1, NU // 2 - 1) as i:
                qkv_pool(2 * i + 1, 1, False)
                qkv_pool2(2 * i, 0, False)
                qkv_pool(2 * i + 2, 0, False)
                qkv_pool2(2 * i + 1, 1, False)
            m = NU - 3
            qkv_pool(m + 1, 1, False)
            qkv_pool2(m, 0, False)
            qkv_pool(m + 2, 0, False)
            qkv_pool2(m + 1, 1, False)
            qkv_pool2(NU - 1, 0, False, text=True)

            pool.wait_ge(s["f_pow"], 1)
            pool.tensor_tensor(mean3, mean2, sm("neg_half_pow", TP), ALU.pow).then_inc(s["f_pow"], 1)

            pool.wait_ge(s["f_dw"], 1)

            def self_of(j, p, first, text=False):
                if not first:
                    pool.wait_ge(s["y_dps"], j - 1)
                pool.tensor_copy(dwr[p], dwt[:, bass.ds(j * 32, 32)]).then_inc(s["y_dwr"], 1)
                if not first:
                    pool.wait_ge(s["y_h"], j - 1)
                pool.tensor_tensor(grid(self_part[p], C), rows_of(vals, j, text), spread(wdiag[:, bass.ds(j * B, B)], C),
                                   ALU.mult).then_inc(s["y_self"], 1)
                pool.wait_ge(s["y_self"], j + 1)
                pool.tensor_tensor(grid(self_part[p], C), grid(self_part[p], C), rows_of(h, j, text), ALU.add)\
                    .then_inc(s["y_self2"], 1)

            self_of(0, 0, True)
            self_of(1, 1, True)
            with pool.Fori(1, TI // 2) as i:
                self_of(2 * i, 0, False)
                self_of(2 * i + 1, 1, False)
            self_of(TI, 0, False, text=True)

            pool.wait_ge(s["y_h"], TT)
            ln_pool(pool, "ln2_")

            def route_lo(m, p, first):
                pool.wait_ge(s["g_hi"], m + 1)
                t3 = tile_major(hl2[p], 128)
                pool.tensor_tensor(t3[:, :, C:128], tile_major(xn[p], C), t3[:, :, 0:C], ALU.subtract)\
                    .then_inc(s["g_lo"], 1)

            in_pairs(pool, route_lo)

        @block.vector
        def _(dve):
            dve.wait_ge(s["d_tokw"], 128)
            for n, (hi, lo, raw) in enumerate(((w1h, w1l, w1_raw), (w2h, w2l, w2_raw))):
                dve.tensor_copy(hi, raw).then_inc(s["w_split"], 1)
                dve.wait_ge(s["w_split"], 2 * n + 1)
                dve.tensor_tensor(lo, raw, hi.bitcast(F32), ALU.subtract).then_inc(s["w_split"], 1)
            for b in range(B):
                dve.wait_ge(d_img[b], 16)
                up = xh[C:128, b * XH_IMG:b * XH_IMG + PW * PW]
                src = xa[C:128, b * XA_IMG:b * XA_IMG + PW * PW]
                dve.tensor_copy(up, src).then_inc(s["x_up"], 1)
                if b == 0:
                    dve.wait_ge(s["x_up"], 1)
                    dve.tensor_tensor(up, src, up.bitcast(F32), ALU.subtract).then_inc(s["x_lo"], 1)
                    dve.wait_ge(s["p_init"], 1)
                    dve.tensor_reduce(rowsum, ps[0:C, 7, 0:C], AX.X, ALU.add, apply_absolute_value=True)\
                       .then_inc(s["p_chain"], 1)
                    dve.wait_ge(s["p_init"], 2)
                    dve.tensor_reduce(rowmax[0:1, :], ps[0:1, 7, 64:128], AX.X, ALU.max).then_inc(s["p_chain"], 1)
                    dve.wait_ge(s["p_init"], 3)
                    dve.tensor_scalar(bound, ps[0:C, 7, 128:129], 1e-30, None, ALU.max).then_inc(s["p_chain"], 1)
                    dve.wait_ge(s["p_chain"], 3)
                    dve.reciprocal(bound_inv, bound).then_inc(s["p_chain"], 1)
                    dve.wait_ge(s["p_chain"], 4)
                    dve.tensor_scalar(xx, a_t, bound_inv, None, ALU.mult)
                    dve.tensor_scalar(xt, a_in, bound_inv, None, ALU.mult).then_inc(s["x_ready"], 1)

            def split_hidden(n):
                dve.wait_ge(s["h1_relu"], n + 1)
                dve.tensor_copy(hl, hid).then_inc(s["h1_step"], 1)
                dve.wait_ge(s["h1_step"], n + 1)
                dve.tensor_tensor(hl[C:128, :], hid[C:128, :], hl[C:128, :].bitcast(F32), ALU.subtract)\
                   .then_inc(s["hl_ready"], 1)

            split_hidden(0)

            def tokenizer(n, last):
                off = n * STEP + (n // UPI) * (XA_IMG - UPI * STEP)
                for k in range(CHUNKS):
                    dve.wait_ge(s["s_sig"], CHUNKS * n + k + 1)
                    g3 = gates[:, k * UN:(k + 1) * UN].rearrange("p (r w) -> p r w", w=HW)
                    u3 = gated[:, k * UN:(k + 1) * UN].rearrange("p (r w) -> p r w", w=HW)
                    if k < 3:
                        dve.tensor_tensor(u3, g3, window(xa, 0, 128, off + PW + k), ALU.mult)\
                           .then_inc(s["u_ready"], 1)
                    elif k == 3:
                        dve.tensor_tensor(u3[0:C], g3[0:C], window(xa, 0, C, off + 3 * PW), ALU.mult)
                        dve.tensor_tensor(u3[C:128], g3[C:128], window(xa, C, 128, off + 2 * PW + 1), ALU.mult)\
                           .then_inc(s["u_ready"], 1)
                    else:
                        dve.tensor_tensor(u3, g3, window(xa, 0, 128, off + 3 * PW + 2), ALU.mult)\
                           .then_inc(s["u_ready"], 1)
                    if k == 1:
                        dve.wait_ge(s["p_ps"], n + 1)
                        dve.tensor_scalar(resid, ps[0:C, 7, 0:C], sm("rho", C)[:, bass.ds(n, 1)], None, ALU.mult)\
                           .then_inc(s["p_chain"], 1)
                        dve.wait_ge(s["p_chain"], n + 5)
                        dve.tensor_tensor(resid, sm("two_i", C), resid, ALU.subtract).then_inc(s["r_ready"], 1)
                if not last:
                    split_hidden(n + 1)
                dve.wait_ge(s["xn_ps"], n + 1)
                dve.tensor_scalar(xtx, ps[0:C, 7, 64:192], sm("rho", C)[:, bass.ds(n, 1)], None, ALU.mult)\
                   .then_inc(s["x_ready"], 1)
                dve.wait_ge(s["o_ps"], n + 1)
                dve.tensor_tensor(tiles(h[0:TP, :], n * UT, UT), grid(ps[0:TP, 6, 0:UT * C], C),
                                  b3_sb.unsqueeze(1).to_broadcast([TP, UT, C]), ALU.add).then_inc(s["o_out"], 1)

            with dve.Fori(0, UNITS - 1) as n:
                tokenizer(n, False)
            tokenizer(UNITS - 1, True)

            dve.wait_ge(s["w_ps"], 1)
            dve.tensor_copy(qkvh, ps[:, 0, 0:192]).then_inc(s["w_hi"], 1)
            dve.wait_ge(s["w_hi"], 1)
            dve.tensor_tensor(qkvl, ps[:, 0, 0:192], qkvh.bitcast(F32), ALU.subtract).then_inc(s["w_ready"], 1)

            dve.wait_ge(s["o_out"], UNITS)
            dve.wait_ge(s["d_txt"], 64)
            ln_vector(dve, "ln1_")
            dve.wait_ge(s["ln1_rstd"], B)
            dve.wait_ge(s["d_table"], 16)

            def normed(m, p, first, names=("q_xn", "q_lo")):
                if not first:
                    dve.wait_ge(s[names[1]], m - 1)
                dve.tensor_tensor(tile_major(xn[p], C), tiles(xc, m * UT, UT), spread(rstd[:, bass.ds(m * UT, UT)], C),
                                  ALU.mult).then_inc(s[names[0]], 1)

            def rotate(m, p, first, text=False):
                r = TI if text else m % UPI * UT
                dve.wait_ge(s["q_sb"], m + 1)
                if not is_zero(m):
                    dve.wait_ge(s["q_rot2"], m)
                dve.tensor_tensor(msin, qkv[p][:, :, 0:128].rearrange("p t (g d) -> p t g d", d=32),
                                  rope_table("sin", r, text), ALU.mult).then_inc(s["q_sin"], 1)
                dve.wait_ge(s["q_sq"], m + 1)
                dve.wait_ge(s["q_qk"], m + 1)
                dve.tensor_reduce(tiles(dots, m * UT, UT, 3), prod.rearrange("p t (g c) -> p t g c", c=C), AX.X,
                                  ALU.add).then_inc(s["q_dots"], 1)
                dve.wait_ge(s["q_cos"], m + 1)
                dve.wait_ge(s["q_sin"], m + 1)
                if not first:
                    dve.wait_ge(s["q_sums"], m - 1)
                ro = rot[p].rearrange("p (t q g d) -> p t q g d", q=2, g=2, d=32)
                mc = mcos.rearrange("p t (q g) d -> p t q g d", g=2)
                ms = msin.rearrange("p t (q g) d -> p t q g d", g=2)
                dve.tensor_tensor(ro[:, :, :, 0], mc[:, :, :, 0], ms[:, :, :, 1], ALU.subtract).then_inc(s["q_rot1"], 1)
                dve.tensor_tensor(ro[:, :, :, 1], ms[:, :, :, 0], mc[:, :, :, 1], ALU.add).then_inc(s["q_rot2"], 1)
                dve.wait_ge(s["q_root"], m + 1)
                i2 = inv_u[p]
                dve.tensor_scalar(i2, i2, EPS_L2, None, ALU.add).then_inc(s["q_rooteps"], 1)
                dve.wait_ge(s["q_rooteps"], m + 1)
                dve.reciprocal(i2, i2).then_inc(s["q_inv"], 1)
                dve.wait_ge(s["q_inv"], m + 1)
                if text:
                    ind = tab("seg")[:, TI * NSEG:TT * NSEG].unsqueeze(1).unsqueeze(1).to_broadcast([TP, UT, 2, NSEG])
                else:
                    ind = tab("seg")[:, bass.ds(r * NSEG, UT * NSEG)].rearrange("p (t g) -> p t g", g=NSEG)\
                        .unsqueeze(2).to_broadcast([TP, UT, 2, NSEG])
                dve.tensor_tensor(segw[p].rearrange("p (t q g) -> p t q g", q=2, g=NSEG), ind,
                                  inv_u[p].rearrange("p (t c) -> p t c", c=2).unsqueeze(3)
                                  .to_broadcast([TP, UT, 2, NSEG]), ALU.mult).then_inc(s["q_segw"], 1)
                dve.tensor_copy(inv[:, bass.ds(m * UT * 2, UT * 2)], i2).then_inc(s["q_invs"], 1)

            def gather(m, text=False):
                dve.wait_ge(s["q_sums"], m + 1)
                if not is_zero(m):
                    dve.wait_ge(s["q_acc"], 2 * m)
                if text:
                    for q, src in ((seg_q[:, :], ps[:, 5, 0:72]), (seg_v[0:C, :], ps[0:C, 6, 0:B * NSUM])):
                        dve.tensor_tensor(q, q, src, ALU.add).then_inc(s["q_acc"], 1)
                    return
                b = m // UPI
                for q, src, w in ((seg_q[:, :], ps[:, 5, 0:18], 18), (seg_v[0:C, :], ps[0:C, 6, 0:NSUM], NSUM)):
                    dst = q[:, bass.ds(b * w, w)]
                    dve.tensor_tensor(dst, dst, src, ALU.add).then_inc(s["q_acc"], 1)

            dve.memset(seg_q[:, :], 0.0)
            dve.memset(seg_v[:, :], 0.0).then_inc(s["f_dve"], 1)
            dve.wait_ge(s["f_dve"], 1)
            normed(0, 0, True)
            normed(1, 1, True)
            rotate(0, 0, True)
            normed(2, 0, False)
            rotate(1, 1, True)
            gather(0)
            with dve.Fori(1, NU // 2 - 1) as i:
                normed(2 * i + 1, 1, False)
                rotate(2 * i, 0, False)
                gather(2 * i - 1)
                normed(2 * i + 2, 0, False)
                rotate(2 * i + 1, 1, False)
                gather(2 * i)
            m = NU - 3
            normed(m + 1, 1, False)
            rotate(m, 0, False)
            gather(m - 1)
            normed(m + 2, 0, False)
            rotate(m + 1, 1, False)
            gather(m)
            rotate(NU - 1, 0, False, text=True)
            gather(m + 1)
            gather(NU - 1, text=True)

            dve.memset(vpick, 0.0).then_inc(s["f_dve"], 1)
            dve.wait_ge(s["q_acc"], 2 * NU)
            dve.wait_ge(s["f_dve"], 2)
            for b in range(B):
                ins = dve.tensor_copy(vpick[:, b * 32 + b * NF:b * 32 + (b + 1) * NF],
                                      seg_v[0:C, b * NSUM + TT:(b + 1) * NSUM])
            ins.then_inc(s["f_vsb"], 1)
            for n, (dst, src) in enumerate(((ks0, ps[0:C, 0, 0:72]), (qk9, ps[0:NSEG, 1, 0:B * NSEG]),
                                            (bq9, ps[0:NSEG, 2, 0:B * NSEG]))):
                dve.wait_ge(s["f_ps"], n + 1)
                dve.tensor_copy(dst, src).then_inc(s["f_sb"], 1)
            dve.wait_ge(s["f_ps"], 4)
            dve.tensor_scalar(far9, ps[0:NSEG, 0, 0:B * NF], SCALE, None, ALU.mult).then_inc(s["f_sb"], 1)
            dve.wait_ge(s["f_ps"], 5)
            dve.tensor_copy(carry, ps[0:TT, 3, 0:B * C]).then_inc(s["f_carry"], 1)
            dve.wait_ge(s["f_ps"], 6)
            dve.tensor_copy(vseg, ps[0:B * NF, 4, 0:B * C]).then_inc(s["f_vsb"], 1)

            step = [2]

            def then(ins):
                step[0] += 1
                ins.then_inc(s["f_dve"], 1)
                dve.wait_ge(s["f_dve"], step[0])

            v4 = val.rearrange("p (t b j) -> p t b j", b=B, j=NV)
            d3 = dots.rearrange("p (t c) -> p t c", c=3)[:, :, 2]
            i3 = inv.rearrange("p (t c) -> p t c", c=2)
            then(dve.tensor_tensor(mean1, i3[:, :, 0], i3[:, :, 1], ALU.mult))
            then(dve.scalar_tensor_tensor(out=mean2, in0=d3, scalar=SCALE, in1=mean1, op0=ALU.mult, op1=ALU.mult))
            dve.tensor_copy(v4[:, 0:TI, :, NF], mean2[:, 0:B * TI].rearrange("p (b t) -> p t b", b=B))
            dve.tensor_copy(v4[:, TI, :, NF], mean2[:, B * TI:NT])
            dve.wait_ge(s["f_far"], 1)
            dve.tensor_copy(v4[:, 0:16, :, 0:NF],
                            ps[0:TP, 5, :].rearrange("p (t b j) -> p t b j", b=B, j=NF))
            then(dve.tensor_copy(v4[:, 16:TT, :, 0:NF],
                                 ps[0:TP, 6, 0:(TT - 16) * 32].rearrange("p (t b j) -> p t b j", b=B, j=NF)))

            def rows(ap):
                return ap.rearrange("p (t b j) -> p t b j", b=B, j=NV)

            def flat(ap):
                return ap.rearrange("p (n j) -> p n j", j=NV)

            def per_pos(name, width):
                return tab(name).rearrange("p (t j) -> p t j", j=width).unsqueeze(2).to_broadcast([TP, TT, B, width])

            def per_row(ap):
                return ap.unsqueeze(2).to_broadcast([TP, NT, NV])

            def by_pos(ap):
                return ap.rearrange("p (t b) -> p t b", b=B)

            inv_n = tab("inv_n").unsqueeze(2).to_broadcast([TP, TT, B])
            root_n = tab("root_n").unsqueeze(2).unsqueeze(2).to_broadcast([TP, TT, B, NV])
            then(dve.tensor_tensor(v4, v4, root_n, ALU.mult))
            then(dve.tensor_tensor(rows(sqv), v4, per_pos("count", NV), ALU.mult))
            then(dve.tensor_reduce(mean1, flat(sqv), AX.X, ALU.add))
            then(dve.tensor_tensor(by_pos(mean1), by_pos(mean1), inv_n, ALU.mult))
            then(dve.tensor_tensor(flat(dev), flat(val), per_row(mean1), ALU.subtract))
            then(dve.tensor_tensor(sqv, dev, dev, ALU.mult))
            then(dve.tensor_tensor(rows(sqv), rows(sqv), per_pos("count", NV), ALU.mult))
            then(dve.tensor_reduce(mean1, flat(sqv), AX.X, ALU.add))
            then(dve.tensor_tensor(by_pos(mean2), by_pos(mean1), inv_n, ALU.mult))
            dve.tensor_scalar(mean2, mean2, EPS_VAR, None, ALU.max).then_inc(s["f_pow"], 1)
            dve.wait_ge(s["f_pow"], 2)
            then(dve.tensor_tensor(flat(dev), flat(dev), per_row(mean3), ALU.mult))
            then(dve.tensor_tensor(rows(dev), rows(dev), per_pos("absent", NV), ALU.add))
            then(dve.tensor_reduce(mean1, flat(dev), AX.X, ALU.max))
            dve.tensor_tensor(flat(dev), flat(dev), per_row(mean1), ALU.subtract).then_inc(s["f_exp"], 1)
            dve.wait_ge(s["f_exp"], 2)
            then(dve.tensor_tensor(rows(sqv), rows(ex), per_pos("count", NV), ALU.mult))
            then(dve.tensor_reduce(mean1, flat(sqv), AX.X, ALU.add))
            then(dve.reciprocal(den, mean1))
            then(dve.tensor_tensor(flat(val), flat(ex), per_row(den), ALU.mult))
            then(dve.tensor_tensor(rows(sqv)[:, :, :, 0:NF], v4[:, :, :, 0:NF], per_pos("own", NF), ALU.mult))
            then(dve.tensor_reduce(wown, flat(sqv)[:, :, 0:NF], AX.X, ALU.add))
            then(dve.tensor_copy(wdiag, flat(val)[:, :, NF]))
            d4 = dwt.rearrange("p (t b j) -> p t b j", b=B, j=NF)
            then(dve.tensor_tensor(dwt.rearrange("p (n j) -> p n j", j=NF), flat(val)[:, :, 0:NF],
                                   wown.unsqueeze(2).to_broadcast([TP, NT, NF]), ALU.subtract))
            dve.tensor_tensor(d4, d4, per_pos("before", NF), ALU.mult).then_inc(s["f_dw"], 1)

            def mix(j, p, first, text=False):
                dve.wait_ge(s["y_ps"], j + 1)
                if not first:
                    dve.wait_ge(s["y_h"], j - 1)
                dve.tensor_tensor(grid(far_part[p], C), grid(ps[0:TP, 2 + p, 0:256], C),
                                  spread(wown[:, bass.ds(j * B, B)], C), ALU.mult).then_inc(s["y_far"], 1)
                dve.wait_ge(s["y_far"], j + 1)
                dve.tensor_tensor(far_part[p], far_part[p], ps[0:TP, 4 + p, 0:256], ALU.add).then_inc(s["y_sum"], 1)
                dve.wait_ge(s["y_sum"], j + 1)
                dve.wait_ge(s["y_self2"], j + 1)
                dve.tensor_tensor(rows_of(h, j, text), grid(far_part[p], C), grid(self_part[p], C), ALU.add)\
                   .then_inc(s["y_h"], 1)

            mix(0, 0, True)
            mix(1, 1, True)
            with dve.Fori(1, TI // 2) as i:
                mix(2 * i, 0, False)
                mix(2 * i + 1, 1, False)
            mix(TI, 0, False, text=True)

            dve.wait_ge(s["y_h"], TT)
            ln_vector(dve, "ln2_")
            dve.wait_ge(s["ln2_rstd"], B)
            dve.wait_ge(s["d_ffnw"], 32)
            dve.tensor_copy(gwh, gw_raw)
            dve.tensor_copy(ew1h, ew1_raw).then_inc(s["g_whi"], 1)
            dve.wait_ge(s["g_whi"], 1)
            dve.tensor_tensor(ew1l, ew1_raw, ew1h.bitcast(F32), ALU.subtract).then_inc(s["g_ew"], 1)
            dve.tensor_tensor(gwl, gw_raw, gwh.bitcast(F32), ALU.subtract).then_inc(s["g_w"], 1)
            dve.wait_ge(s["g_w"], 1)

            def read_logits(m, p):
                dve.wait_ge(s["g_lps"], m + 1)
                dve.tensor_tensor(tiles(logit, m * UT, UT, E), grid(ps[0:TP, 4 + p, 0:UT * E], E),
                                  gb_sb.unsqueeze(1).to_broadcast([TP, UT, E]), ALU.add).then_inc(s["g_logit"], 1)

            names = ("g_xn", "g_lo")
            normed(0, 0, True, names)
            normed(1, 1, True, names)
            with dve.Fori(1, NU // 2) as i:
                normed(2 * i, 0, False, names)
                read_logits(2 * i - 2, 0)
                normed(2 * i + 1, 1, False, names)
                read_logits(2 * i - 1, 1)
            normed(NU - 1, 0, False, names)
            read_logits(NU - 3, 0)
            read_logits(NU - 2, 1)
            read_logits(NU - 1, 0)

            gstep = [0]

            def then2(ins):
                gstep[0] += 1
                ins.then_inc(s["g_dve"], 1)
                dve.wait_ge(s["g_dve"], gstep[0])

            def g3(ap):
                return grid(ap, E)

            def each(ap):
                return spread(ap, E)

            dve.wait_ge(s["g_logit"], NU)
            then2(dve.tensor_reduce(gtop, g3(logit), AX.X, ALU.max))
            dve.tensor_tensor(g3(pick), g3(logit), each(gtop), ALU.subtract).then_inc(s["g_exp"], 1)
            dve.wait_ge(s["g_exp"], 2)
            then2(dve.tensor_reduce(gsum, g3(prob), AX.X, ALU.add))
            then2(dve.reciprocal(gsum, gsum))
            then2(dve.tensor_tensor(g3(prob), g3(prob), each(gsum), ALU.mult))
            rank = sm("rank", TP).unsqueeze(1).to_broadcast([TP, NT, E])
            then2(dve.tensor_copy(last_p, prob))
            for n in range(2):
                then2(dve.tensor_reduce(gtop, g3(last_p), AX.X, ALU.max))
                then2(dve.tensor_tensor(g3(cand), g3(last_p), each(gtop), ALU.is_ge))
                then2(dve.tensor_tensor(g3(cand), g3(cand), rank, ALU.mult))
                then2(dve.tensor_reduce(gtop, g3(cand), AX.X, ALU.max))
                then2(dve.tensor_tensor(g3(pick if n else keep), g3(cand), each(gtop), ALU.is_equal))
                if n == 0:
                    then2(dve.scalar_tensor_tensor(out=last_p, in0=keep, scalar=-2.0, in1=last_p, op0=ALU.mult,
                                                   op1=ALU.add))
            then2(dve.tensor_tensor(keep, keep, pick, ALU.add))
            dve.tensor_tensor(cw, prob, keep, ALU.mult).then_inc(s["g_cwps"], 1)
            dve.wait_ge(s["g_cwps"], 1)
            dve.wait_ge(s["g_cwt"], 1)
            for g in range(2):
                n = 4 - g
                dve.tensor_copy(cw_t[:, 4 * g * TP:(4 * g + n) * TP], ps[:, 6 + g, 0:n * TP])
            dve.tensor_copy(cw_t[0:4 * E, 7 * TP:8 * TP], ps[0:4 * E, 7, 3 * TP:4 * TP]).then_inc(s["g_cwt"], 1)
            for g in range(15):
                n = min(8, NT - 8 * g)
                dve.wait_ge(s["g_bps"], g + 1)
                hg = h[0:TP, g * 512:g * 512 + n * C]
                dve.tensor_tensor(hg, hg, ps[0:TP, g % 4, 0:n * C], ALU.add).then_inc(s["g_bias"], 1)
            dve.wait_ge(s["g_bias"], 15)

            wy4 = wy.rearrange("p (t e c) -> p t e c", e=E, c=C)

            with dve.Fori(0, NU) as m:
                for hf in range(2):
                    dve.wait_ge(s["e_y"], 2 * m + hf + 1)
                    w = tiles(cw, m * UT, UT, E)[:, :, 4 * hf:4 * hf + 4].unsqueeze(3).to_broadcast([TP, UT, 4, C])
                    y = ps[0:TP, 4 + 2 * hf:6 + 2 * hf, :].rearrange("p b (t e c) -> p (b t) e c", e=4, c=C)
                    dve.tensor_tensor(wy4[:, :, 4 * hf:4 * hf + 4], y, w, ALU.mult).then_inc(s["e_used"], 1)
                dve.wait_ge(s["e_used"], 2 * m + 2)
                dve.tensor_reduce(grid(wsum, C), wy4.rearrange("p t e c -> p t c e"), AX.X, ALU.add)\
                   .then_inc(s["e_red"], 1)
                dve.wait_ge(s["e_red"], m + 1)
                hm = h[0:TP, bass.ds(m * UT * C, UT * C)]
                dve.tensor_tensor(hm, hm, wsum, ALU.add).then_inc(s["e_out"], 1)


_INS = ["pair", "txt", "tok_w1", "tok_b1", "tok_w2", "tok_b2", "tok_w3", "tok_b3", "wq", "wq_t", "wv", "wo_t",
        "gate_w", "gate_b", "ffn_w1", "ffn_b1", "ffn_w2", "ffn_b2", "small", "table", "seg_rows"]


def kernel(**inputs):
    import numpy as _np
    import concourse.bacc as _bacc
    from concourse import mybir as _mybir
    from concourse.bass_utils import run_bass_kernel_spmd as _run

    f = _np.float32
    x = _np.asarray(inputs["x"])
    pad = _np.zeros((B, C, PW, PW), x.dtype)
    pad[:, :, 1:-1, 1:-1] = x
    pad = pad.reshape(B, C, PW * PW)
    pair = _np.zeros((B, 128, XA_IMG), x.dtype)
    pair[:, :C, PW:PW + PW * PW] = pad
    pair[:, C:, :PW * PW] = pad

    pairs = [(0, 3), (1, 4), (2, 5), (6, 7), (8, None)]
    w1 = _np.asarray(inputs["L0_tok_W1"]).reshape(C, 9, C)
    w1 = _np.concatenate([_np.concatenate([w1, w1], 2)] * 2, 0).reshape(128, 9 * 128)
    w2_src = _np.asarray(inputs["L0_tok_W2"]).reshape(C, C, 9)
    b2_src = _np.asarray(inputs["L0_tok_b2"]).reshape(C, 9)
    w3_src = _np.asarray(inputs["L0_tok_W3"]).reshape(C, 9, C)
    w2 = _np.zeros((C, CHUNKS, 2, C), x.dtype)
    b2 = _np.zeros((2, C, CHUNKS), x.dtype)
    w3 = _np.zeros((2, C, CHUNKS, C), x.dtype)
    for k, taps in enumerate(pairs):
        for j, tap in enumerate(taps):
            if tap is not None:
                w2[:, k, j] = w2_src[:, :, tap]
                b2[j, :, k] = b2_src[:, tap]
                w3[j, :, k] = w3_src[:, tap]
    w2 = _np.concatenate([w2.reshape(C, -1)] * 2, 0)
    b1 = _np.asarray(inputs["L0_tok_b1"])
    wv = _np.asarray(inputs["L0_attn_W_V"])
    gw = _np.asarray(inputs["L0_ffn_gate_w"])
    fw1 = _np.asarray(inputs["L0_ffn_W1"]).transpose(1, 0, 2).reshape(C, E * HID)
    fb2 = _np.asarray(inputs["L0_ffn_b2"])
    blk = _np.zeros((16, E, 16, C), x.dtype)
    for i in range(16):
        blk[i, :, i] = fb2
    small, table, seg_rows = make_tables()
    data = {
        "pair": pair, "txt": inputs["txt"], "tok_w1": w1, "tok_b1": _np.concatenate([b1, b1])[:, None],
        "tok_w2": w2, "tok_b2": b2.reshape(128, CHUNKS), "tok_w3": w3.reshape(128, CHUNKS * C),
        "tok_b3": _np.tile(_np.asarray(inputs["L0_tok_b3"])[None], (TP, 1)),
        "wq": inputs["L0_attn_W_Q"], "wq_t": _np.concatenate([_np.asarray(inputs["L0_attn_W_Q"]).T] * 2, 1),
        "wv": _np.concatenate([wv, wv], 1), "wo_t": _np.asarray(inputs["L0_attn_W_O"]).T,
        "gate_w": _np.concatenate([gw, gw], 0), "gate_b": _np.tile(_np.asarray(inputs["L0_ffn_gate_b"])[None], (TP, 1)),
        "ffn_w1": _np.concatenate([fw1, fw1], 0), "ffn_b1": _np.asarray(inputs["L0_ffn_b1"]).T,
        "ffn_w2": _np.asarray(inputs["L0_ffn_W2"]).transpose(1, 0, 2).reshape(HID, E * C),
        "ffn_b2": blk.reshape(128, 16 * C), "small": small, "table": table, "seg_rows": seg_rows,
    }

    nc = _bacc.Bacc("TRN2", target_bir_lowering=False, num_devices=1)
    arrays, args = {}, []
    for name in _INS:
        a = _np.ascontiguousarray(data[name])
        arrays[f"in_{name}_dram"] = a
        args.append(nc.dram_tensor(f"in_{name}_dram", a.shape, _mybir.dt.from_np(a.dtype), kind="ExternalInput").ap())
    args.append(nc.dram_tensor("out_0_dram", (B, SEQ, C), _mybir.dt.from_np(_np.dtype("float32")),
                               kind="ExternalOutput").ap())
    build(nc, *args)
    r = _run(nc, [arrays], core_ids=[0])
    return r.results[0]["out_0_dram"]
```

```python
from contextlib import ExitStack

import numpy as np

import concourse.bass as bass
from concourse import mybir

ALU = mybir.AluOpType
ACT = mybir.ActivationFunctionType
AX = mybir.AxisListType
F32 = mybir.dt.float32
F32R = mybir.dt.float32r

B, C, HW, TXT = 4, 64, 56, 77
PW = HW + 2
SEQ = HW * HW + TXT
TP = 2 * HW
UR = 8
UN = UR * HW
UT = UN // TP
UPI = HW // UR
UNITS = B * UPI
TI = UPI * UT
TT = TI + 1
NT = B * TT
NU = NT // UT
XA_IMG = 3424
XH_IMG = 3368
STEP = UR * PW
CHUNKS = 5
E, HID = 8, 128
LEVELS = 3
EPS_LN, EPS_L2, EPS_VAR = 1e-5, 1e-8, 1e-6
SCALE = 1.0 / 8.0
PSTEPS = UNITS


def haar_rows():
    cols = []
    for j in range(LEVELS):
        bc = 2 ** j
        bs = SEQ // bc
        half = bs // 2
        for k in range(bc):
            v = np.zeros(SEQ)
            v[k * bs:k * bs + half] = 1 / np.sqrt(half)
            v[k * bs + half:(k + 1) * bs] = -1 / np.sqrt(half)
            cols.append(v)
    w = np.stack(cols, 1)
    starts = [0] + [t for t in range(1, SEQ) if (w[t] != w[t - 1]).any()]
    return starts, w[starts]


STARTS, HAAR = haar_rows()
NSEG = len(STARTS)
NF = NSEG - 1
NV = NF + 1
NSUM = TT + NF


def rho_schedule():
    low, out = 1e-9, []
    while low < 1 - 1e-7:
        r = 2 / (1 + low)
        out.append(r)
        low = 1 - (1 - r * low) ** 2
    return out + [1.0] * (PSTEPS - len(out))


SMALL = {}
TABLE = {}
_at = 0
for _n, _w in (("ident", 128), ("two_i", C), ("dup_i", 128), ("rho", PSTEPS), ("basis", NSEG), ("ones", C),
               ("rank", E)):
    SMALL[_n] = (_at, _at + _w)
    _at += _w
NSMALL = _at
_at = 0
for _n, _w in (("cos", TT * 32), ("sin", TT * 32), ("sums", TT * NSUM), ("seg", TT * NSEG), ("count", TT * NV),
               ("absent", TT * NV), ("before", TT * NF), ("own", TT * NF), ("inv_n", TT), ("root_n", TT),
               ("prefix", TP)):
    TABLE[_n] = (_at, _at + _w)
    _at += _w
NTABLE = _at
WORK = 5008 + NTABLE


def make_tables():
    f = np.float32
    small = np.zeros((128, NSMALL), f)

    def put(arr, spans, name, value):
        a, b = spans[name]
        value = np.asarray(value, f).reshape(len(value), -1)
        arr[:value.shape[0], a:b] = value

    put(small, SMALL, "ident", np.eye(128))
    put(small, SMALL, "two_i", 2 * np.eye(C))
    put(small, SMALL, "dup_i", np.concatenate([np.eye(C)] * 2, 1))
    put(small, SMALL, "rho", np.tile(np.array(rho_schedule())[None], (128, 1)))
    put(small, SMALL, "basis", HAAR @ HAAR.T)
    put(small, SMALL, "ones", np.ones((128, C)))
    put(small, SMALL, "rank", np.tile(np.arange(E, 0, -1)[None], (128, 1)))

    table = np.zeros((128, NTABLE), f)
    t = np.arange(TP)[:, None] + TP * np.arange(TT)[None, :]
    real = t < SEQ
    half = C // 2
    inv_freq = (1.0 / 10000.0 ** (np.arange(half, dtype=f) / half)).astype(f)
    ang = t.astype(f)[..., None] * inv_freq
    put(table, TABLE, "cos", np.cos(ang) * real[..., None])
    put(table, TABLE, "sin", np.sin(ang) * real[..., None])
    ends = STARTS[1:] + [SEQ]
    seg = np.searchsorted(STARTS, t, side="right") - 1
    onehot = (seg[..., None] == np.arange(NSEG)) & real[..., None]
    put(table, TABLE, "seg", onehot)
    sums = np.zeros((TP, TT, NSUM))
    for j in range(TT):
        sums[:, j, j + 1:TT] = 1
    sums *= real[..., None]
    sums[:, :, TT:] = onehot[:, :, :NF]
    put(table, TABLE, "sums", sums)
    count = np.ones((TP, TT, NV))
    for j in range(NF):
        count[:, :, j] = np.clip(t - STARTS[j], 0, ends[j] - STARTS[j]) * real
    put(table, TABLE, "count", count)
    put(table, TABLE, "absent", np.where(count > 0, 0.0, -1e30))
    put(table, TABLE, "before", (np.arange(NF) < seg[..., None]) & real[..., None])
    put(table, TABLE, "own", onehot[:, :, :NF])
    n = np.where(real, t + 1, 1).astype(f)
    put(table, TABLE, "inv_n", 1 / n)
    put(table, TABLE, "root_n", 1 / np.sqrt(n))
    prefix = np.zeros((TP + 1, TP))
    prefix[:TP] = np.triu(np.ones((TP, TP)), 1)
    prefix[TP] = 1
    put(table, TABLE, "prefix", prefix)
    seg_rows = np.zeros((NSEG, TT, TP), f)
    seg_rows[:] = onehot.transpose(2, 1, 0)
    return small, table, seg_rows.reshape(NSEG, TT * TP)


def is_zero(m):
    return isinstance(m, int) and m == 0


def build(nc, pair, txt, tok_w1, tok_b1, tok_w2, tok_b2, tok_w3, tok_b3, wq, wq_t, wv, wo_t,
          gate_w, gate_b, ffn_w1, ffn_b1, ffn_w2, ffn_b2, small, table, seg_rows, out):
    ctx = ExitStack()
    with ctx:
        def sb(name, cols, dt=F32):
            return ctx.enter_context(nc.sbuf_tensor(name, [128, cols], dt))

        def sem(name):
            return ctx.enter_context(nc.semaphore(name))

        h = sb("h", NT * C)
        vx = sb("vx", 2 * NT * C)
        stack = sb("stack", 4 * XH_IMG + UN, F32R)
        work = sb("work", WORK)
        wts = sb("wts", 3584, F32R)
        w3_sb = sb("w3_sb", CHUNKS * C)
        small_sb = sb("small_sb", NSMALL)
        bias = sb("bias", 1 + CHUNKS + E + C + E)
        stat = sb("stat", 10 * NT + 1)
        nrm = sb("nrm", 3 * NT + 64)
        seg_q = sb("seg_q", B * 2 * NSEG)
        seg_v = sb("seg_v", B * NSUM)
        ps = ctx.enter_context(nc.psum_tensor("ps", [128, 8, 512], F32))

        def sm(name, rows=128):
            a, b = SMALL[name]
            return small_sb[0:rows, a:b]

        tb0 = WORK - NTABLE

        def tab(name, rows=TP):
            a, b = TABLE[name]
            return work[0:rows, tb0 + a:tb0 + b]

        def grid(ap, inner):
            return ap.rearrange("p (t c) -> p t c", c=inner)

        ident = sm("ident")
        b1_sb = bias[:, 0:1]
        b2_sb = bias[:, 1:1 + CHUNKS]
        eb1_sb = bias[:, 6:6 + E]
        b3_sb = bias[0:TP, 14:14 + C]
        gb_sb = bias[0:TP, 78:78 + E]

        pin = work[:, tb0:tb0 + 9 * C]
        xa = vx[:, 0:B * XA_IMG]
        xh = stack[:, 0:B * XH_IMG]
        hl = stack[:, B * XH_IMG:B * XH_IMG + UN]
        gates = work[:, 0:CHUNKS * UN]
        gated = work[:, CHUNKS * UN:2 * CHUNKS * UN]
        w1_raw = work[:, 0:9 * 128]
        w2_raw = work[:, 9 * 128:14 * 128]
        w1h, w1l = wts[:, 0:1152], wts[:, 1152:2304]
        w2h, w2l = wts[:, 2304:2944], wts[:, 2944:3584]
        qkvh, qkvl = wts[:, 0:256], wts[:, 256:512]
        gwh, gwl = wts[:, 2048:2056], wts[:, 2056:2064]
        hid = work[:, 4480:4480 + UN]
        a_in, a_t = pin[0:C, 8 * C:9 * C], pin[0:C, 0:C]
        a_tt = pin[0:C, 0:2 * C]
        xtx = pin[0:C, 2 * C:4 * C]
        xt, xx = xtx[:, 0:C], xtx[:, C:2 * C]
        resid = pin[0:C, 4 * C:5 * C]
        wv_sb = pin[0:C, 5 * C:7 * C]
        wo_sb = pin[0:C, 7 * C:8 * C]
        tiny = stat[:, 10 * NT:10 * NT + 1]
        rowsum, rowmax, bound, bound_inv = (stat[0:C, i:i + 1] for i in range(4))

        vals = vx[:, 0:NT * C]
        mean, vare, rstd, tmp_n = (stat[0:TP, i * NT:(i + 1) * NT] for i in range(4))
        bn = stat[0:TP, 4 * NT:10 * NT]
        xn = [work[0:TP, i * 256:(i + 1) * 256] for i in range(2)]
        qkv = [grid(work[0:TP, 512 + i * 768:512 + (i + 1) * 768], 192) for i in range(2)]
        m0 = NT * C + TT * TP
        prod = [grid(vx[0:TP, m0 + i * 768:m0 + (i + 1) * 768], 192) for i in range(2)]
        mcos, msin = ([vx[0:TP, m0 + 1536 + (2 * n + i) * 512:m0 + 1536 + (2 * n + i + 1) * 512]
                       .rearrange("p (t g d) -> p t g d", g=4, d=32) for i in range(2)] for n in range(2))
        assert m0 + 1536 + 2048 <= 2 * NT * C
        rot = [work[0:TP, 3840 + i * 512:3840 + (i + 1) * 512] for i in range(2)]
        unit_n = nrm[0:TP, 3 * NT:3 * NT + 64]
        root_u = [unit_n[:, i * 8:(i + 1) * 8] for i in range(2)]
        inv_u = [unit_n[:, 16 + i * 8:24 + i * 8] for i in range(2)]
        tmp_u = unit_n[:, 32:40]
        dots_u = [unit_n[:, 40 + i * 12:52 + i * 12].rearrange("p (t c) -> p t c", c=3) for i in range(2)]
        segw = [work[0:TP, 4864 + i * 72:4864 + (i + 1) * 72] for i in range(2)]
        assert 5008 <= tb0
        tok_hl = [stack[0:TP, i * 512:(i + 1) * 512] for i in range(2)]
        tok_t = [stack[:, 1024 + i * UN:1024 + (i + 1) * UN] for i in range(2)]
        inv = nrm[0:TP, 0:2 * NT]
        dot_qk = nrm[0:TP, 2 * NT:3 * NT]

        NR = TT * B * NV
        segr = vx[0:NSEG, NT * C:NT * C + TT * TP]
        val, dev, sqv, ex = (vx[0:TP, NT * C + TT * TP + i * NR:NT * C + TT * TP + (i + 1) * NR] for i in range(4))
        ks0 = work[0:C, 0:72]
        qk9 = work[0:NSEG, 72:108]
        bq9 = work[0:NSEG, 108:144]
        far9 = work[0:NSEG, 144:144 + B * NF]
        vpick = work[0:C, 176:176 + 128]
        vseg = work[0:B * NF, 304:560]
        carry = work[0:TT, 560:816]
        mean1, mean2, mean3, den = (work[0:TP, 816 + i * 116:816 + (i + 1) * 116] for i in range(4))
        wown, wdiag = (work[0:TP, 1280 + i * 116:1280 + (i + 1) * 116] for i in range(2))
        dwt = work[0:TP, 1512:1512 + TT * B * NF]
        dwr = [work[0:TP, 2440 + i * 32:2440 + (i + 1) * 32] for i in range(2)]
        dwT = [work[0:B * NF, 2504 + i * TP:2504 + (i + 1) * TP] for i in range(2)]
        far_part = [work[0:TP, 2728 + i * 256:2728 + (i + 1) * 256] for i in range(2)]
        self_part = [work[0:TP, 3240 + i * 256:3240 + (i + 1) * 256] for i in range(2)]

        all_t = stack[:, 0:NU * UN]
        hl2 = [work[0:TP, 512 + i * 512:512 + (i + 1) * 512] for i in range(2)]
        logit_s = [work[0:E, 1536 + i * UN:1536 + (i + 1) * UN] for i in range(2)]
        ew1_raw = work[:, 2432:2432 + 1024]
        ew2_sb = work[:, 3456:3456 + 512]
        gw_raw = work[:, 3968:3976]
        eb2_blk = work[:, 3976:3976 + 1024]
        ew1h, ew1l = wts[:, 0:1024], wts[:, 1024:2048]
        g0 = NT * C
        logit = vx[0:TP, 6400:6400 + 928]
        prob, pick, keep, cand, last_p = (vx[0:TP, g0 + i * 928:g0 + (i + 1) * 928] for i in range(5))
        cw = vx[0:TP, g0 + 5 * 928:g0 + 6 * 928]
        cw_t = vx[:, 0:8 * TP]
        gtop, gsum = stat[0:TP, 0:NT], stat[0:TP, NT:2 * NT]
        act_g = [vx[:, 1024 + i * UN:1024 + (i + 1) * UN] for i in range(4)]
        wy = vx[0:TP, 3072:3072 + 2048]
        wsum = vx[0:TP, 5120:5376]

        carry_rows = nc.dram_tensor("carry_rows", [B, TT, C], F32, kind="Internal").ap()

        names = """d_small d_tokw d_img0 d_img1 d_img2 d_img3 d_txt d_pin d_table d_segr d_rows d_carry d_ffnw d_ffn2 d_out
        z_text w_split x_hi x_up x_lo h1_ps h1_relu h1_step hl_ready s_ps s_sig u_ready o_ps o_out
        p_init p_chain x_ready p_ps r_ready xn_ps w_ps w_hi w_ready
        ln1 ln1_root ln2 ln2_root ln_bn
        q_cen q_xn q_hi q_lo q_tps q_t q_ps q_sb q_sq q_qk q_dots q_root q_small q_invs q_segw q_cos q_sin q_rot
        q_rsum q_vsum q_racc q_vacc
        f_ps f_sb f_dve f_far f_carry f_vsb f_exp f_pow f_mean f_dw f_pool
        y_dwr y_dps y_dwt y_ps y_far y_self y_self2 y_mix y_sum y_h
        g_cen g_xn g_hi g_lo g_tps g_t g_ps g_sb g_lps g_logit g_w g_whi g_ew g_dve g_exp g_cwps g_cwt g_bps g_bias
        e_h e_g e_y e_used e_red e_out""".split()
        s = {n: sem(n) for n in names}

        block = ctx.enter_context(nc.Block())
        d_img = [s["d_img0"], s["d_img1"], s["d_img2"], s["d_img3"]]

        def tiles(buf, start, n, inner=C):
            return grid(buf[:, bass.ds(start * inner, n * inner)], inner)

        def window(buf, lo, hi, off):
            return buf[lo:hi, bass.ds(off, STEP)].rearrange("p (r w) -> p r w", w=PW)[:, :, 0:HW]

        def tile_major(buf, width):
            return buf.rearrange("p (t c) -> p t c", c=width)

        def spread(ap, n):
            return ap.unsqueeze(2).to_broadcast([ap.shape[0], ap.shape[1], n])

        def rope_table(name, r, text):
            if text:
                return tab(name)[:, TI * 32:TT * 32].unsqueeze(1).unsqueeze(1).to_broadcast([TP, UT, 4, 32])
            return tab(name)[:, bass.ds(r * 32, UT * 32)].rearrange("p (t d) -> p t d", d=32).unsqueeze(2)\
                .to_broadcast([TP, UT, 4, 32])

        def rows_of(buf, j, text):
            if text:
                return tiles(buf[0:TP, :], B * TI, B)
            return buf[0:TP, 0:B * TI * C].rearrange("p (b t c) -> p b t c", b=B, c=C)[:, :, bass.ds(j, 1), :]\
                .rearrange("p b o c -> p b (o c)")

        @block.sync
        def _(sp):
            sp.dma_start(small_sb[:, :], small).then_inc(s["d_small"], 16)
            sp.dma_start(w1_raw, tok_w1).then_inc(s["d_tokw"], 16)
            sp.dma_start(w2_raw, tok_w2).then_inc(s["d_tokw"], 16)
            sp.dma_start(xa[:, 0:XA_IMG], pair[0]).then_inc(s["d_img0"], 16)
            sp.dma_start(b1_sb, tok_b1).then_inc(s["d_tokw"], 16)
            sp.dma_start(b2_sb, tok_b2).then_inc(s["d_tokw"], 16)
            sp.dma_start(w3_sb[:, :], tok_w3).then_inc(s["d_tokw"], 16)
            sp.dma_start(b3_sb, tok_b3).then_inc(s["d_tokw"], 16)
            sp.dma_start(eb1_sb, ffn_b1).then_inc(s["d_tokw"], 16)
            sp.dma_start(gb_sb, gate_b).then_inc(s["d_tokw"], 16)
            sp.dma_start(a_in, wq).then_inc(s["d_pin"], 16)
            sp.dma_start(a_tt, wq_t).then_inc(s["d_pin"], 16)
            sp.dma_start(wv_sb, wv).then_inc(s["d_pin"], 16)
            sp.dma_start(wo_sb, wo_t).then_inc(s["d_pin"], 16)
            for b in range(1, B):
                sp.dma_start(xa[:, b * XA_IMG:(b + 1) * XA_IMG], pair[b]).then_inc(d_img[b], 16)
            sp.wait_ge(s["z_text"], 1)
            for b in range(B):
                k = B * TI + b
                sp.dma_start(h[0:TXT, k * C:(k + 1) * C], txt[b]).then_inc(s["d_txt"], 16)
            sp.wait_ge(s["o_ps"], UNITS)
            sp.wait_ge(s["w_ps"], 1)
            sp.dma_start(work[:, tb0:tb0 + NTABLE], table).then_inc(s["d_table"], 16)
            sp.wait_ge(s["q_xn"], NU)
            sp.dma_start(segr, seg_rows).then_inc(s["d_segr"], 16)
            sp.wait_ge(s["f_carry"], 1)
            sp.dma_start(carry_rows.rearrange("b t c -> t b c"), carry.rearrange("t (b c) -> t b c", c=C))\
              .then_inc(s["d_rows"], 16)
            sp.wait_ge(s["d_rows"], 16)
            crow = vals[TP:TP + 1, :]
            sp.dma_start(crow[:, 0:B * TI * C].rearrange("o (b k) -> o b k", b=B),
                         carry_rows[:, 0:TI, :].rearrange("(o b) t c -> o b (t c)", o=1)).then_inc(s["d_carry"], 16)
            sp.dma_start(crow[:, B * TI * C:NT * C].rearrange("o (b c) -> o b c", b=B),
                         carry_rows[:, TI:TT, :].rearrange("(o b) t c -> o b (t c)", o=1)).then_inc(s["d_carry"], 16)
            sp.wait_ge(s["y_h"], TT)
            sp.wait_ge(s["y_ps"], TT)
            sp.dma_start(gw_raw, gate_w).then_inc(s["d_ffnw"], 16)
            sp.dma_start(ew1_raw, ffn_w1).then_inc(s["d_ffnw"], 16)
            sp.dma_start(ew2_sb, ffn_w2).then_inc(s["d_ffn2"], 16)
            sp.dma_start(eb2_blk, ffn_b2).then_inc(s["d_ffn2"], 16)
            out_rows = out.rearrange("b s c -> (b s) c")
            with sp.Fori(0, UNITS) as m:
                sp.wait_ge(s["e_out"], m + 1)
                b = m // UPI
                dst = out_rows[bass.ds(m * UN + b * TXT, UN), :].rearrange("(t p) c -> p t c", p=TP)
                sp.dma_start(dst, tiles(h[0:TP, :], m * UT, UT)).then_inc(s["d_out"], 16)
            sp.wait_ge(s["e_out"], NU)
            for b in range(B):
                k = B * TI + b
                sp.dma_start(out[b, HW * HW:SEQ, :], h[0:TXT, k * C:(k + 1) * C]).then_inc(s["d_out"], 16)
            sp.wait_ge(s["d_out"], 16 * (UNITS + B))

        def wait(eng, name, value):
            if not (isinstance(value, int) and value <= 0):
                eng.wait_ge(s[name], value)

        def pipeline(eng, body, units, lead, lag):
            first = lag + 3 + (lag + 3) % 2
            pairs = (units - lead - first) // 2
            end = first + 2 * pairs
            for i in range(-lead, first):
                body(i, i % 2, lambda u: 0 <= u < units)
            with eng.Fori(first // 2, end // 2) as j:
                body(2 * j, 0, lambda u: True)
                body(2 * j + 1, 1, lambda u: True)
            for i in range(end, units + lag):
                body(i, i % 2, lambda u: 0 <= u < units)

        def tile_stats(eng, k):
            return eng.bn_stats(bn[:, bass.ds(k * 6, 6)], h[0:TP, bass.ds(k * C, C)])

        def norm_stats(eng, name, step0):
            count = [step0]

            def then(ins):
                count[0] += 1
                ins.then_inc(s[name], 1)
                eng.wait_ge(s[name], count[0])

            b6 = bn.rearrange("p (t c) -> p t c", c=6)
            then(eng.tensor_tensor(mean, b6[:, :, 1], b6[:, :, 4], ALU.add))
            then(eng.tensor_scalar(mean, mean, 0.5, None, ALU.mult))
            then(eng.tensor_tensor(vare, b6[:, :, 2], b6[:, :, 5], ALU.add))
            then(eng.tensor_tensor(rstd, b6[:, :, 1], b6[:, :, 4], ALU.subtract))
            then(eng.tensor_tensor(rstd, rstd, rstd, ALU.mult))
            then(eng.scalar_tensor_tensor(out=vare, in0=rstd, scalar=C / 4.0, in1=vare, op0=ALU.mult, op1=ALU.add))
            eng.tensor_scalar(vare, vare, 1.0 / C, EPS_LN, ALU.mult, ALU.add).then_inc(s[name], 1)
            eng.wait_ge(s[name + "_root"], 1)
            count[0] += 1
            then(eng.reciprocal(rstd, rstd))
            then(eng.tensor_tensor(tmp_n, rstd, rstd, ALU.mult))
            then(eng.tensor_tensor(tmp_n, tmp_n, vare, ALU.mult))
            then(eng.tensor_scalar(tmp_n, tmp_n, -0.5, 1.5, ALU.mult, ALU.add))
            then(eng.tensor_tensor(rstd, rstd, tmp_n, ALU.mult))

        @block.tensor
        def _(pe):
            def conv(off, last=False):
                n = 0
                for w in (w1h, w1l):
                    for tap in range(9):
                        mm = pe.matmul(ps[:, 0, 0:UN], w[:, tap * 128:(tap + 1) * 128],
                                       window(xh, 0, 128, off + (tap // 3) * PW + tap % 3),
                                       start=(n == 0), stop=(n == 17))
                        n += 1
                mm.then_inc(s["h1_ps"], 1)

            pe.wait_ge(s["w_split"], 4)
            pe.wait_ge(s["x_hi"], 1)
            pe.wait_ge(s["x_lo"], 1)
            conv(0)

            pe.wait_ge(s["d_pin"], 64)
            pe.wait_ge(s["d_small"], 16)
            pe.matmul(ps[0:C, 7, 0:C], a_t, a_t, start=True, stop=True).then_inc(s["p_init"], 1)
            pe.wait_ge(s["p_chain"], 1)
            pe.transpose(ps[0:1, 7, 64:128], rowsum, ident[0:C, 0:C]).then_inc(s["p_init"], 1)
            pe.wait_ge(s["p_chain"], 2)
            pe.matmul(ps[0:C, 7, 128:129], sm("ones", 1)[:, 0:C], rowmax[0:1, :], start=True, stop=True)\
              .then_inc(s["p_init"], 1)

            def unit(n, last):
                pe.wait_ge(s["hl_ready"], n + 1)
                for k in range(CHUNKS):
                    pe.matmul(ps[:, 1 + k, 0:UN], w2h[:, k * 128:(k + 1) * 128], hl, start=True, stop=False)
                    pe.matmul(ps[:, 1 + k, 0:UN], w2l[:, k * 128:(k + 1) * 128], hl, start=False, stop=True)\
                      .then_inc(s["s_ps"], 1)
                pe.wait_ge(s["x_ready"], n + 1)
                pe.matmul(ps[:, 7, 0:C], a_tt, xx, start=True, stop=True).then_inc(s["p_ps"], 1)
                if not last:
                    b = (n + 1) // UPI
                    pe.wait_ge(s["x_hi"], b + 1)
                    pe.wait_ge(s["x_lo"], b + 1)
                    conv((n + 1) * STEP + b * (XH_IMG - UPI * STEP))
                pe.wait_ge(s["r_ready"], n + 1)
                pe.matmul(ps[:, 7, 128:192], xtx, resid, start=True, stop=True)
                pe.matmul(ps[0:C, 7, 64:128], resid, xt, start=True, stop=True)\
                  .then_inc(s["xn_ps"], 1)
                pe.wait_ge(s["u_ready"], CHUNKS * n + CHUNKS)
                for t in range(UT):
                    for k in range(CHUNKS):
                        mm = pe.matmul(ps[0:TP, 6, t * C:(t + 1) * C],
                                       gated[:, k * UN + t * TP:k * UN + (t + 1) * TP],
                                       w3_sb[:, k * C:(k + 1) * C], start=(k == 0), stop=(k == CHUNKS - 1))
                mm.then_inc(s["o_ps"], 1)

            with pe.Fori(0, UNITS - 1) as n:
                unit(n, False)
            unit(UNITS - 1, True)

            pe.wait_ge(s["x_ready"], UNITS + 1)
            pe.matmul(ps[:, 0, 0:C], sm("dup_i", C), a_in, start=True, stop=True)
            pe.matmul(ps[:, 0, C:2 * C], sm("dup_i", C), xt, start=True, stop=True)
            pe.matmul(ps[:, 0, 2 * C:3 * C], wv_sb, wo_sb, start=True, stop=True)
            pe.matmul(ps[:, 0, 3 * C:4 * C], wv_sb, wo_sb, start=True, stop=True).then_inc(s["w_ps"], 1)

            def attention(i, p, live):
                q = 1 - p
                if live(i + 1):
                    m = i + 1
                    wait(pe, "q_t", m + 1)
                    if is_zero(m):
                        pe.wait_ge(s["w_ready"], 1)
                    wait(pe, "q_sb", m)
                    for t in range(UT):
                        for n, w in enumerate((qkvh, qkvl)):
                            mm = pe.matmul(ps[0:TP, 3 + t // 2, t % 2 * 256:t % 2 * 256 + 256],
                                           tok_t[q][:, t * TP:(t + 1) * TP], w, start=(n == 0), stop=(n == 1))
                    mm.then_inc(s["q_ps"], 1)
                if live(i - 2):
                    m = i - 2
                    text = isinstance(m, int) and m == NU - 1
                    wait(pe, "q_rot", m + 1)
                    wait(pe, "q_segw", m + 1)
                    wait(pe, "q_racc", m - 1)
                    for t in range(UT):
                        o = ps[:, 5 + 2 * p, t * 18:(t + 1) * 18] if text else ps[:, 5 + 2 * p, 0:18]
                        mm = pe.matmul(o, rot[p][:, t * 128:(t + 1) * 128], segw[p][:, t * 18:(t + 1) * 18],
                                       start=(text or t == 0), stop=(text or t == UT - 1))
                    mm.then_inc(s["q_rsum"], 1)
                if live(i + 2):
                    m = i + 2
                    wait(pe, "q_lo", m + 1)
                    wait(pe, "q_t", m - 1)
                    for t in range(UT):
                        mm = pe.transpose(ps[:, 1 + p, t * TP:(t + 1) * TP],
                                          tok_hl[p][:, t * 128:(t + 1) * 128].bitcast(F32), ident[0:TP, 0:TP])
                    mm.then_inc(s["q_tps"], 1)
                if live(i):
                    m = i
                    text = isinstance(m, int) and m == NU - 1
                    r = TI if text else m % UPI * UT
                    wait(pe, "q_sb", m + 1)
                    wait(pe, "q_vacc", m - 1)
                    for t in range(UT):
                        j = r if text else r + t
                        o = ps[0:C, 6 * p, t * NSUM:(t + 1) * NSUM] if text else ps[0:C, 6 * p, 0:NSUM]
                        mm = pe.matmul(o, qkv[p][:, t, 128:192], tab("sums")[:, bass.ds(j * NSUM, NSUM)],
                                       start=(text or t == 0), stop=(text or t == UT - 1))
                    mm.then_inc(s["q_vsum"], 1)

            pe.wait_ge(s["d_table"], 16)
            pipeline(pe, attention, NU, 2, 3)

            pe.wait_ge(s["q_racc"], NU)
            pe.wait_ge(s["q_vacc"], NU)
            pe.matmul(ps[0:C, 0, 0:72], ident[:, C:128], seg_q[:, :], start=True, stop=True)\
              .then_inc(s["f_ps"], 1)
            pe.wait_ge(s["f_sb"], 1)
            for b in range(B):
                mm = pe.matmul(ps[0:NSEG, 1, b * NSEG:(b + 1) * NSEG], seg_q[0:C, b * 18:b * 18 + NSEG],
                               ks0[:, b * 18 + NSEG:(b + 1) * 18], start=True, stop=True)
            mm.then_inc(s["f_ps"], 1)
            pe.wait_ge(s["f_sb"], 2)
            for b in range(B):
                mm = pe.matmul(ps[0:NSEG, 2, b * NSEG:(b + 1) * NSEG], qk9[:, b * NSEG:(b + 1) * NSEG],
                               sm("basis", NSEG), start=True, stop=True)
            mm.then_inc(s["f_ps"], 1)
            pe.wait_ge(s["f_sb"], 3)
            for b in range(B):
                mm = pe.matmul(ps[0:NSEG, 0, b * NF:(b + 1) * NF], bq9[:, b * NSEG:(b + 1) * NSEG],
                               sm("basis", NSEG)[:, 0:NF], start=True, stop=True)
            mm.then_inc(s["f_ps"], 1)
            for b in range(B):
                mm = pe.transpose(ps[0:TT, 3, b * C:(b + 1) * C], seg_v[0:C, b * NSUM:b * NSUM + TT], ident[0:C, 0:C])
            mm.then_inc(s["f_ps"], 1)
            pe.wait_ge(s["f_vsb"], 1)
            for b in range(B):
                mm = pe.matmul(ps[0:B * NF, 4, b * C:(b + 1) * C], vpick[:, b * 32:(b + 1) * 32], ident[0:C, 0:C],
                               start=True, stop=True)
            mm.then_inc(s["f_ps"], 1)
            pe.wait_ge(s["f_sb"], 4)
            pe.wait_ge(s["d_segr"], 16)
            for j in range(TT):
                mm = pe.matmul(ps[0:TP, 5 + j // 16, j % 16 * 32:j % 16 * 32 + 32], segr[:, j * TP:(j + 1) * TP],
                               far9, start=True, stop=True)
            mm.then_inc(s["f_far"], 1)

            pe.wait_ge(s["f_vsb"], 2)
            pe.wait_ge(s["d_carry"], 32)

            def attend(i, p, live):
                q = 1 - p
                if live(i + 1):
                    wait(pe, "y_dwr", i + 2)
                    wait(pe, "y_dwt", i)
                    pe.transpose(ps[0:B * NF, q, 0:TP], dwr[q], ident[0:TP, 0:TP]).then_inc(s["y_dps"], 1)
                if live(i):
                    text = isinstance(i, int) and i == TI
                    wait(pe, "y_sum", i - 1)
                    v = (tiles(vals[0:TP + 1, :], B * TI, B) if text else
                         vals[0:TP + 1, 0:B * TI * C].rearrange("p (b t c) -> p b t c", b=B, c=C)
                         [:, :, bass.ds(i, 1), :].rearrange("p b o c -> p b (o c)"))
                    pe.matmul(ps[0:TP, 2 + p, 0:256], tab("prefix", TP + 1), v, start=True, stop=True)
                    wait(pe, "y_dwt", i + 1)
                    pe.matmul(ps[0:TP, 4 + p, 0:256], dwT[p], vseg, start=True, stop=True).then_inc(s["y_ps"], 1)

            pipeline(pe, attend, TT, 2, 2)

            def route(i, p, live):
                q = 1 - p
                if live(i + 1):
                    m = i + 1
                    wait(pe, "g_lo", m + 1)
                    wait(pe, "g_t", m - 1)
                    for t in range(UT):
                        mm = pe.transpose(ps[:, q, t * TP:(t + 1) * TP], hl2[q][:, t * 128:(t + 1) * 128],
                                          ident[0:TP, 0:TP])
                    mm.then_inc(s["g_tps"], 1)
                if live(i - 1):
                    m = i - 1
                    wait(pe, "g_sb", m + 1)
                    wait(pe, "g_logit", m - 1)
                    for t in range(UT):
                        mm = pe.matmul(ps[0:TP, 4 + q, t * E:(t + 1) * E], logit_s[q][:, t * TP:(t + 1) * TP],
                                       ident[0:E, 0:E], start=True, stop=True)
                    mm.then_inc(s["g_lps"], 1)
                if live(i):
                    wait(pe, "g_t", i + 1)
                    if is_zero(i):
                        pe.wait_ge(s["g_w"], 1)
                    wait(pe, "g_sb", i - 1)
                    for n, w in enumerate((gwh, gwl)):
                        mm = pe.matmul(ps[0:E, 2 + p, 0:UN], w, all_t[:, bass.ds(i * UN, UN)],
                                       start=(n == 0), stop=(n == 1))
                    mm.then_inc(s["g_ps"], 1)

            pipeline(pe, route, NU, 2, 2)

            pe.wait_ge(s["g_cwps"], 1)
            for g in range(8):
                n = min(16, NT - 16 * g)
                mm = pe.transpose(ps[0:n * E, 6 + g // 4, g % 4 * TP:(g % 4 + 1) * TP],
                                  cw[:, g * 128:g * 128 + n * E], ident[0:TP, 0:TP])
            mm.then_inc(s["g_cwt"], 1)
            pe.wait_ge(s["d_ffn2"], 32)
            pe.wait_ge(s["g_cwt"], 2)
            for g in range(15):
                n = min(8, NT - 8 * g)
                k = min(16, NT - 16 * (g // 2)) * E
                if g >= 4:
                    pe.wait_ge(s["g_bias"], g - 3)
                pe.matmul(ps[0:TP, g % 4, 0:n * C], cw_t[0:k, g // 2 * TP:(g // 2 + 1) * TP],
                          eb2_blk[0:k, g % 2 * 512:g % 2 * 512 + n * C], start=True, stop=True)\
                  .then_inc(s["g_bps"], 1)

            pe.wait_ge(s["g_ew"], 1)
            pe.wait_ge(s["g_bias"], 15)

            def hidden(m, e):
                pe.matmul(ps[:, e % 4, 0:UN], ew1h[:, e * HID:(e + 1) * HID], all_t[:, bass.ds(m * UN, UN)],
                          start=True, stop=False)
                pe.matmul(ps[:, e % 4, 0:UN], ew1l[:, e * HID:(e + 1) * HID], all_t[:, bass.ds(m * UN, UN)],
                          start=False, stop=True).then_inc(s["e_h"], 1)

            def experts(m, first, last):
                for e in range(E):
                    if e < E - 2:
                        hidden(m, e + 2)
                    elif not last:
                        hidden(m + 1, e + 2 - E)
                    if e % 4 == 0 and not first:
                        pe.wait_ge(s["e_used"], 2 * m + e // 4 - 1)
                    pe.wait_ge(s["e_g"], E * m + e + 1)
                    for t in range(UT):
                        col = t % 2 * 256 + e % 4 * C
                        mm = pe.matmul(ps[0:TP, 4 + e // 4 * 2 + t // 2, col:col + C], act_g[e % 4][:, t * TP:(t + 1) * TP],
                                       ew2_sb[:, e * C:(e + 1) * C], start=True, stop=True)
                    if e % 4 == 3:
                        mm.then_inc(s["e_y"], 1)

            hidden(0, 0)
            hidden(0, 1)
            experts(0, True, False)
            with pe.Fori(1, NU - 1) as m:
                experts(m, False, False)
            experts(NU - 1, False, True)

        @block.scalar
        def _(act):
            def round_image(b):
                act.wait_ge(d_img[b], 16)
                act.activation(xh[0:C, b * XH_IMG:b * XH_IMG + PW * PW],
                               xa[0:C, b * XA_IMG + PW:b * XA_IMG + PW + PW * PW], ACT.Copy).then_inc(s["x_hi"], 1)

            def hidden_layer(n):
                act.wait_ge(s["h1_ps"], n + 1)
                act.activation(hid, ps[:, 0, 0:UN], ACT.Relu, bias=b1_sb).then_inc(s["h1_relu"], 1)

            def gates_of(n):
                for k in range(CHUNKS):
                    act.wait_ge(s["s_ps"], CHUNKS * n + k + 1)
                    act.activation(gates[:, k * UN:(k + 1) * UN], ps[:, 1 + k, 0:UN], ACT.Sigmoid,
                                   bias=b2_sb[:, k:k + 1]).then_inc(s["s_sig"], 1)

            act.wait_ge(s["d_small"], 16)
            act.activation(tiny, sm("two_i")[:, 0:1], ACT.Sigmoid)
            round_image(0)
            act.wait_ge(s["d_tokw"], 128)
            hidden_layer(0)
            for b in range(B):
                gates_of(b * UPI)
                hidden_layer(b * UPI + 1)
                if b + 1 < B:
                    round_image(b + 1)
                with act.Fori(b * UPI + 1, (b + 1) * UPI - (b == B - 1)) as n:
                    gates_of(n)
                    hidden_layer(n + 1)
            gates_of(UNITS - 1)

            act.wait_ge(s["ln1"], 7)
            act.activation(rstd, vare, ACT.Sqrt).then_inc(s["ln1_root"], 1)

            def attention(i, p, live):
                q = 1 - p
                if live(i - 1):
                    wait(act, "q_dots", i)
                    wait(act, "q_invs", i - 2)
                    act.activation(root_u[q].rearrange("p (t c) -> p t c", c=2), dots_u[q][:, :, 0:2], ACT.Sqrt)\
                       .then_inc(s["q_root"], 1)
                if live(i + 1):
                    m = i + 1
                    wait(act, "q_tps", m + 1)
                    wait(act, "q_ps", m - 1)
                    act.activation(tok_t[q], ps[:, 1 + q, 0:UN], ACT.Copy).then_inc(s["q_t"], 1)
                if live(i):
                    wait(act, "q_sb", i + 1)
                    wait(act, "q_dots", i - 1)
                    act.activation(prod[p][:, :, 0:128], qkv[p][:, :, 0:128], ACT.Square).then_inc(s["q_sq"], 1)
                if live(i + 2):
                    m = i + 2
                    wait(act, "q_xn", m + 1)
                    wait(act, "q_tps", m - 1)
                    act.activation(tile_major(tok_hl[p], 128)[:, :, 0:C], tile_major(xn[p], C), ACT.Copy)\
                       .then_inc(s["q_hi"], 1)
                if live(i + 1):
                    m = i + 1
                    ps_u = ps[0:TP, 3:5, :].rearrange("p b (t c) -> p b t c", c=256)
                    wait(act, "q_ps", m + 1)
                    wait(act, "q_vsum", m - 1)
                    wait(act, "q_rot", m - 1)
                    act.activation(qkv[q].rearrange("p (b t) c -> p b t c", b=2), ps_u[:, :, :, 0:192], ACT.Copy)
                    act.activation(vals[0:TP, bass.ds(m * UT * C, UT * C)].rearrange("p (b t c) -> p b t c", b=2, c=C),
                                   ps_u[:, :, :, 128:192], ACT.Copy).then_inc(s["q_sb"], 1)

            pipeline(act, attention, NU, 2, 3)

            act.wait_ge(s["f_pow"], 1)
            act.activation(mean3, mean2, ACT.Sqrt).then_inc(s["f_pow"], 1)
            act.wait_ge(s["f_exp"], 1)
            act.activation(ex, dev, ACT.Exp).then_inc(s["f_exp"], 1)

            act.wait_ge(s["f_dw"], 1)

            def attend(i, p, live):
                q = 1 - p
                if live(i + 1):
                    wait(act, "y_dps", i + 2)
                    wait(act, "y_ps", i)
                    act.activation(dwT[q], ps[0:B * NF, q, 0:TP], ACT.Copy).then_inc(s["y_dwt"], 1)
                if live(i + 2):
                    wait(act, "y_dps", i + 1)
                    act.activation(dwr[p], dwt[:, bass.ds((i + 2) * 32, 32)], ACT.Copy).then_inc(s["y_dwr"], 1)

            pipeline(act, attend, TT, 2, 2)

            act.wait_ge(s["ln2"], 7)
            act.activation(rstd, vare, ACT.Sqrt).then_inc(s["ln2_root"], 1)

            def route(i, p, live):
                q = 1 - p
                if live(i + 1):
                    wait(act, "g_tps", i + 2)
                    act.activation(all_t[:, bass.ds((i + 1) * UN, UN)], ps[:, q, 0:UN], ACT.Copy)\
                       .then_inc(s["g_t"], 1)
                if live(i + 2):
                    wait(act, "g_xn", i + 3)
                    wait(act, "g_tps", i + 1)
                    act.activation(tile_major(hl2[p], 128)[:, :, 0:C].bitcast(F32R), tile_major(xn[p], C), ACT.Copy)\
                       .then_inc(s["g_hi"], 1)
                if live(i):
                    wait(act, "g_ps", i + 1)
                    wait(act, "g_lps", i - 1)
                    act.activation(logit_s[p], ps[0:E, 2 + p, 0:UN], ACT.Copy).then_inc(s["g_sb"], 1)

            pipeline(act, route, NU, 2, 2)

            act.wait_ge(s["g_exp"], 1)
            act.activation(prob, pick, ACT.Exp).then_inc(s["g_exp"], 1)
            act.activation(tiny, sm("two_i")[:, 0:1], ACT.Gelu)

            act.wait_ge(s["g_bias"], 15)
            with act.Fori(0, NU) as m:
                for e in range(E):
                    act.wait_ge(s["e_h"], E * m + e + 1)
                    act.activation(act_g[e % 4], ps[:, e % 4, 0:UN], ACT.Gelu, bias=eb1_sb[:, e:e + 1])\
                       .then_inc(s["e_g"], 1)

        @block.gpsimd
        def _(pool):
            pool.memset(h[0:TP, B * TI * C:NT * C], 0.0).then_inc(s["z_text"], 1)
            pool.wait_ge(s["z_text"], 1)
            for b in range(1, B):
                pool.wait_ge(s["x_up"], b + 1)
                up = xh[C:128, b * XH_IMG:b * XH_IMG + PW * PW]
                pool.tensor_tensor(up, xa[C:128, b * XA_IMG:b * XA_IMG + PW * PW], up.bitcast(F32),
                                   ALU.subtract).then_inc(s["x_lo"], 1)

            pool.wait_ge(s["x_lo"], B)
            pool.wait_ge(s["d_table"], 16)

            def attention(i, p, live):
                if live(i):
                    text = isinstance(i, int) and i == NU - 1
                    wait(pool, "q_sb", i + 1)
                    wait(pool, "q_dots", i - 1)
                    pool.tensor_tensor(prod[p][:, :, 128:192], qkv[p][:, :, 0:64], qkv[p][:, :, 64:128], ALU.mult)\
                        .then_inc(s["q_qk"], 1)
                    wait(pool, "q_rot", i - 1)
                    pool.tensor_tensor(mcos[p], qkv[p][:, :, 0:128].rearrange("p t (g d) -> p t g d", d=32),
                                       rope_table("cos", TI if text else i % UPI * UT, text), ALU.mult)\
                        .then_inc(s["q_cos"], 1)
                if live(i + 2):
                    wait(pool, "q_hi", i + 3)
                    t3 = tile_major(tok_hl[p], 128)
                    pool.tensor_tensor(t3[:, :, C:128], tile_major(xn[p], C), t3[:, :, 0:C].bitcast(F32),
                                       ALU.subtract).then_inc(s["q_lo"], 1)

            pipeline(pool, attention, NU, 2, 3)

            pool.wait_ge(s["f_dw"], 1)

            def attend(i, p, live):
                if live(i):
                    text = isinstance(i, int) and i == TI
                    wait(pool, "y_h", i - 1)
                    pool.tensor_tensor(grid(self_part[p], C), rows_of(vals, i, text),
                                       spread(wdiag[:, bass.ds(i * B, B)], C), ALU.mult).then_inc(s["y_self"], 1)
                    wait(pool, "y_self", i + 1)
                    pool.tensor_tensor(grid(self_part[p], C), grid(self_part[p], C), rows_of(h, i, text), ALU.add)\
                        .then_inc(s["y_self2"], 1)

            pipeline(pool, attend, TT, 2, 2)

            def route(i, p, live):
                if live(i + 2):
                    wait(pool, "g_hi", i + 3)
                    t3 = tile_major(hl2[p], 128)
                    pool.tensor_tensor(t3[:, :, C:128], tile_major(xn[p], C), t3[:, :, 0:C], ALU.subtract)\
                        .then_inc(s["g_lo"], 1)

            pipeline(pool, route, NU, 2, 2)

        @block.vector
        def _(dve):
            dve.wait_ge(s["d_tokw"], 128)
            for n, (hi, lo, raw) in enumerate(((w1h, w1l, w1_raw), (w2h, w2l, w2_raw))):
                dve.tensor_copy(hi, raw).then_inc(s["w_split"], 1)
                dve.wait_ge(s["w_split"], 2 * n + 1)
                dve.tensor_tensor(lo, raw, hi.bitcast(F32), ALU.subtract).then_inc(s["w_split"], 1)
            def split_image(b):
                dve.wait_ge(d_img[b], 16)
                up = xh[C:128, b * XH_IMG:b * XH_IMG + PW * PW]
                src = xa[C:128, b * XA_IMG:b * XA_IMG + PW * PW]
                dve.tensor_copy(up, src).then_inc(s["x_up"], 1)
                if b == 0:
                    dve.wait_ge(s["x_up"], 1)
                    dve.tensor_tensor(up, src, up.bitcast(F32), ALU.subtract).then_inc(s["x_lo"], 1)

            split_image(0)

            def split_hidden(n):
                dve.wait_ge(s["h1_relu"], n + 1)
                dve.tensor_copy(hl, hid).then_inc(s["h1_step"], 1)
                dve.wait_ge(s["h1_step"], n + 1)
                dve.tensor_tensor(hl[C:128, :], hid[C:128, :], hl[C:128, :].bitcast(F32), ALU.subtract)\
                   .then_inc(s["hl_ready"], 1)

            split_hidden(0)
            dve.wait_ge(s["p_init"], 1)
            dve.tensor_reduce(rowsum, ps[0:C, 7, 0:C], AX.X, ALU.add, apply_absolute_value=True)\
               .then_inc(s["p_chain"], 1)
            dve.wait_ge(s["p_init"], 2)
            dve.tensor_reduce(rowmax[0:1, :], ps[0:1, 7, 64:128], AX.X, ALU.max).then_inc(s["p_chain"], 1)
            dve.wait_ge(s["p_init"], 3)
            dve.tensor_scalar(bound, ps[0:C, 7, 128:129], 1e-30, None, ALU.max).then_inc(s["p_chain"], 1)
            dve.wait_ge(s["p_chain"], 3)
            dve.reciprocal(bound_inv, bound).then_inc(s["p_chain"], 1)
            dve.wait_ge(s["p_chain"], 4)
            dve.tensor_scalar(xx, a_t, bound_inv, None, ALU.mult)
            dve.tensor_scalar(xt, a_in, bound_inv, None, ALU.mult).then_inc(s["x_ready"], 1)

            def tokenizer(n, last):
                off = n * STEP + (n // UPI) * (XA_IMG - UPI * STEP)
                for k in range(CHUNKS):
                    dve.wait_ge(s["s_sig"], CHUNKS * n + k + 1)
                    g3 = gates[:, k * UN:(k + 1) * UN].rearrange("p (r w) -> p r w", w=HW)
                    u3 = gated[:, k * UN:(k + 1) * UN].rearrange("p (r w) -> p r w", w=HW)
                    if k < 3:
                        dve.tensor_tensor(u3, g3, window(xa, 0, 128, off + PW + k), ALU.mult)\
                           .then_inc(s["u_ready"], 1)
                    elif k == 3:
                        dve.tensor_tensor(u3[0:C], g3[0:C], window(xa, 0, C, off + 3 * PW), ALU.mult)
                        dve.tensor_tensor(u3[C:128], g3[C:128], window(xa, C, 128, off + 2 * PW + 1), ALU.mult)\
                           .then_inc(s["u_ready"], 1)
                    else:
                        dve.tensor_tensor(u3, g3, window(xa, 0, 128, off + 3 * PW + 2), ALU.mult)\
                           .then_inc(s["u_ready"], 1)
                    if k == 1:
                        dve.wait_ge(s["p_ps"], n + 1)
                        dve.tensor_scalar(resid, ps[0:C, 7, 0:C], sm("rho", C)[:, bass.ds(n, 1)], None, ALU.mult)\
                           .then_inc(s["p_chain"], 1)
                        dve.wait_ge(s["p_chain"], n + 5)
                        dve.tensor_tensor(resid, sm("two_i", C), resid, ALU.subtract).then_inc(s["r_ready"], 1)
                if not last:
                    split_hidden(n + 1)
                dve.wait_ge(s["xn_ps"], n + 1)
                dve.tensor_scalar(xtx, ps[0:C, 7, 64:192], sm("rho", C)[:, bass.ds(n, 1)], None, ALU.mult)\
                   .then_inc(s["x_ready"], 1)
                wait(dve, "o_out", n)
                dve.wait_ge(s["o_ps"], n + 1)
                dve.tensor_tensor(tiles(h[0:TP, :], n * UT, UT), grid(ps[0:TP, 6, 0:UT * C], C),
                                  b3_sb.unsqueeze(1).to_broadcast([TP, UT, C]), ALU.add).then_inc(s["o_out"], 1)

            def stats_of(n):
                for t in range(UT):
                    tile_stats(dve, n * UT + t)

            for b in range(B):
                tokenizer(b * UPI, False)
                if b:
                    stats_of(b * UPI - 1)
                if b + 1 < B:
                    split_image(b + 1)
                with dve.Fori(b * UPI + 1, (b + 1) * UPI - (b == B - 1)) as n:
                    tokenizer(n, False)
                    stats_of(n - 1)
            tokenizer(UNITS - 1, True)
            stats_of(UNITS - 2)

            dve.wait_ge(s["w_ps"], 1)
            dve.tensor_copy(qkvh, ps[:, 0, 0:256]).then_inc(s["w_hi"], 1)
            dve.wait_ge(s["w_hi"], 1)
            dve.tensor_tensor(qkvl, ps[:, 0, 0:256], qkvh.bitcast(F32), ALU.subtract).then_inc(s["w_ready"], 1)

            dve.wait_ge(s["o_out"], UNITS)
            dve.wait_ge(s["d_txt"], 64)
            stats_of(UNITS - 1)
            for b in range(B - 1):
                tile_stats(dve, B * TI + b)
            tile_stats(dve, NT - 1).then_inc(s["ln_bn"], 1)
            dve.wait_ge(s["ln_bn"], 1)
            norm_stats(dve, "ln1", 0)
            dve.wait_ge(s["d_table"], 16)

            def centre(m, p, step, taken):
                wait(dve, taken, m - 1)
                dve.tensor_tensor(grid(xn[p], C), tiles(h[0:TP, :], m * UT, UT), spread(mean[:, bass.ds(m * UT, UT)], C),
                                  ALU.subtract).then_inc(s[step], 1)

            def scale(m, p, step, ready):
                wait(dve, step, m + 1)
                dve.tensor_tensor(grid(xn[p], C), grid(xn[p], C), spread(rstd[:, bass.ds(m * UT, UT)], C),
                                  ALU.mult).then_inc(s[ready], 1)

            def attention(i, p, live):
                q = 1 - p

                def refine(n):
                    if not live(i - 1):
                        return
                    m = i - 1
                    r0, r1, r2 = root_u[q], inv_u[q], tmp_u
                    if n:
                        wait(dve, "q_small", 6 * m + n)
                    if n == 0:
                        wait(dve, "q_root", m + 1)
                        ins = dve.tensor_scalar(r2, r0, 1e-18, None, ALU.add)
                    elif n == 1 or n == 5:
                        ins = dve.reciprocal(r1, r2)
                    elif n == 2:
                        ins = dve.tensor_tensor(r2.rearrange("p (t c) -> p t c", c=2), dots_u[q][:, :, 0:2],
                                                r1.rearrange("p (t c) -> p t c", c=2), ALU.mult)
                    elif n == 3:
                        ins = dve.tensor_tensor(r2, r2, r0, ALU.add)
                    else:
                        ins = dve.tensor_scalar(r2, r2, 0.5, EPS_L2, ALU.mult, ALU.add)
                    ins.then_inc(s["q_small"], 1)

                if live(i + 2):
                    centre(i + 2, p, "q_cen", "q_lo")
                for m, name, used, sums, src, w in (
                        (i - 3, "q_racc", "q_rsum", seg_q[:, :], ps[:, 5 + 2 * q], 18),
                        (i - 1, "q_vacc", "q_vsum", seg_v[0:C, :], ps[0:C, 6 * q], NSUM)):
                    if live(m):
                        wait(dve, used, m + 1)
                        wait(dve, name, m)
                        last = isinstance(m, int) and m == NU - 1
                        dst = sums if last else sums[:, bass.ds(m // UPI * w, w)]
                        dve.tensor_tensor(dst, dst, src[:, 0:B * w] if last else src[:, 0:w], ALU.add)\
                           .then_inc(s[name], 1)
                if live(i + 2):
                    scale(i + 2, p, "q_cen", "q_xn")
                refine(0)
                text = isinstance(i, int) and i == NU - 1
                if live(i):
                    wait(dve, "q_sb", i + 1)
                    wait(dve, "q_rot", i - 1)
                    dve.tensor_tensor(msin[p], qkv[p][:, :, 0:128].rearrange("p t (g d) -> p t g d", d=32),
                                      rope_table("sin", TI if text else i % UPI * UT, text), ALU.mult)\
                       .then_inc(s["q_sin"], 1)
                refine(1)
                if live(i):
                    wait(dve, "q_sq", i + 1)
                    wait(dve, "q_qk", i + 1)
                    dve.tensor_reduce(dots_u[p], prod[p].rearrange("p t (g c) -> p t g c", c=C), AX.X,
                                      ALU.add).then_inc(s["q_dots"], 1)
                refine(2)
                ro = rot[p].rearrange("p (t q g d) -> p t q g d", q=2, g=2, d=32)
                mc = mcos[p].rearrange("p t (q g) d -> p t q g d", g=2)
                ms = msin[p].rearrange("p t (q g) d -> p t q g d", g=2)
                if live(i):
                    wait(dve, "q_cos", i + 1)
                    wait(dve, "q_sin", i + 1)
                    wait(dve, "q_rsum", i - 1)
                    dve.tensor_tensor(ro[:, :, :, 0], mc[:, :, :, 0], ms[:, :, :, 1], ALU.subtract)
                refine(3)
                if live(i):
                    dve.tensor_tensor(ro[:, :, :, 1], ms[:, :, :, 0], mc[:, :, :, 1], ALU.add)\
                       .then_inc(s["q_rot"], 1)
                refine(4)
                if live(i - 1):
                    m = i - 1
                    last = isinstance(m, int) and m == NU - 1
                    dve.tensor_copy(dot_qk[:, bass.ds(m * UT, UT)], dots_u[q][:, :, 2])
                    refine(5)
                    wait(dve, "q_small", 6 * m + 6)
                    wait(dve, "q_rsum", m - 1)
                    if last:
                        ind = tab("seg")[:, TI * NSEG:TT * NSEG].unsqueeze(1).unsqueeze(1)\
                            .to_broadcast([TP, UT, 2, NSEG])
                    else:
                        ind = tab("seg")[:, bass.ds(m % UPI * UT * NSEG, UT * NSEG)]\
                            .rearrange("p (t g) -> p t g", g=NSEG).unsqueeze(2).to_broadcast([TP, UT, 2, NSEG])
                    dve.tensor_tensor(segw[q].rearrange("p (t q g) -> p t q g", q=2, g=NSEG), ind,
                                      inv_u[q].rearrange("p (t c) -> p t c", c=2).unsqueeze(3)
                                      .to_broadcast([TP, UT, 2, NSEG]), ALU.mult).then_inc(s["q_segw"], 1)
                    dve.tensor_copy(inv[:, bass.ds(m * UT * 2, UT * 2)], inv_u[q]).then_inc(s["q_invs"], 1)

            dve.memset(seg_q[:, :], 0.0)
            dve.memset(seg_v[:, :], 0.0).then_inc(s["f_dve"], 1)
            dve.wait_ge(s["f_dve"], 1)
            pipeline(dve, attention, NU, 2, 3)

            dve.memset(vpick, 0.0).then_inc(s["f_dve"], 1)
            dve.wait_ge(s["q_racc"], NU)
            dve.wait_ge(s["q_vacc"], NU)
            dve.wait_ge(s["f_dve"], 2)
            for b in range(B):
                ins = dve.tensor_copy(vpick[:, b * 32 + b * NF:b * 32 + (b + 1) * NF],
                                      seg_v[0:C, b * NSUM + TT:(b + 1) * NSUM])
            ins.then_inc(s["f_vsb"], 1)
            for n, (dst, src) in enumerate(((ks0, ps[0:C, 0, 0:72]), (qk9, ps[0:NSEG, 1, 0:B * NSEG]),
                                            (bq9, ps[0:NSEG, 2, 0:B * NSEG]))):
                dve.wait_ge(s["f_ps"], n + 1)
                dve.tensor_copy(dst, src).then_inc(s["f_sb"], 1)
            dve.wait_ge(s["f_ps"], 4)
            dve.tensor_scalar(far9, ps[0:NSEG, 0, 0:B * NF], SCALE, None, ALU.mult).then_inc(s["f_sb"], 1)
            dve.wait_ge(s["f_ps"], 5)
            dve.tensor_copy(carry, ps[0:TT, 3, 0:B * C]).then_inc(s["f_carry"], 1)
            dve.wait_ge(s["f_ps"], 6)
            dve.tensor_copy(vseg, ps[0:B * NF, 4, 0:B * C]).then_inc(s["f_vsb"], 1)

            step = [2]

            def then(ins):
                step[0] += 1
                ins.then_inc(s["f_dve"], 1)
                dve.wait_ge(s["f_dve"], step[0])

            v4 = val.rearrange("p (t b j) -> p t b j", b=B, j=NV)
            d3 = dot_qk
            i3 = inv.rearrange("p (t c) -> p t c", c=2)
            then(dve.tensor_tensor(mean1, i3[:, :, 0], i3[:, :, 1], ALU.mult))
            then(dve.scalar_tensor_tensor(out=mean2, in0=d3, scalar=SCALE, in1=mean1, op0=ALU.mult, op1=ALU.mult))
            dve.tensor_copy(v4[:, 0:TI, :, NF], mean2[:, 0:B * TI].rearrange("p (b t) -> p t b", b=B))
            dve.tensor_copy(v4[:, TI, :, NF], mean2[:, B * TI:NT])
            dve.wait_ge(s["f_far"], 1)
            dve.tensor_copy(v4[:, 0:16, :, 0:NF],
                            ps[0:TP, 5, :].rearrange("p (t b j) -> p t b j", b=B, j=NF))
            then(dve.tensor_copy(v4[:, 16:TT, :, 0:NF],
                                 ps[0:TP, 6, 0:(TT - 16) * 32].rearrange("p (t b j) -> p t b j", b=B, j=NF)))

            def rows(ap):
                return ap.rearrange("p (t b j) -> p t b j", b=B, j=NV)

            def flat(ap):
                return ap.rearrange("p (n j) -> p n j", j=NV)

            def per_pos(name, width):
                return tab(name).rearrange("p (t j) -> p t j", j=width).unsqueeze(2).to_broadcast([TP, TT, B, width])

            def per_row(ap):
                return ap.unsqueeze(2).to_broadcast([TP, NT, NV])

            def by_pos(ap):
                return ap.rearrange("p (t b) -> p t b", b=B)

            inv_n = tab("inv_n").unsqueeze(2).to_broadcast([TP, TT, B])
            root_n = tab("root_n").unsqueeze(2).unsqueeze(2).to_broadcast([TP, TT, B, NV])
            then(dve.tensor_tensor(v4, v4, root_n, ALU.mult))
            then(dve.tensor_tensor(rows(sqv), v4, per_pos("count", NV), ALU.mult))
            then(dve.tensor_reduce(mean1, flat(sqv), AX.X, ALU.add))
            then(dve.tensor_tensor(by_pos(mean1), by_pos(mean1), inv_n, ALU.mult))
            then(dve.tensor_tensor(flat(dev), flat(val), per_row(mean1), ALU.subtract))
            then(dve.tensor_tensor(sqv, dev, dev, ALU.mult))
            then(dve.tensor_tensor(rows(sqv), rows(sqv), per_pos("count", NV), ALU.mult))
            then(dve.tensor_reduce(mean1, flat(sqv), AX.X, ALU.add))
            then(dve.tensor_tensor(by_pos(mean2), by_pos(mean1), inv_n, ALU.mult))
            dve.tensor_scalar(mean2, mean2, EPS_VAR, None, ALU.max).then_inc(s["f_pow"], 1)
            dve.wait_ge(s["f_pow"], 2)
            then(dve.reciprocal(mean3, mean3))
            then(dve.tensor_tensor(mean1, mean3, mean3, ALU.mult))
            then(dve.tensor_tensor(mean1, mean1, mean2, ALU.mult))
            then(dve.tensor_scalar(mean1, mean1, -0.5, 1.5, ALU.mult, ALU.add))
            then(dve.tensor_tensor(mean3, mean3, mean1, ALU.mult))
            then(dve.tensor_tensor(flat(dev), flat(dev), per_row(mean3), ALU.mult))
            then(dve.tensor_tensor(rows(dev), rows(dev), per_pos("absent", NV), ALU.add))
            then(dve.tensor_reduce(mean1, flat(dev), AX.X, ALU.max))
            dve.tensor_tensor(flat(dev), flat(dev), per_row(mean1), ALU.subtract).then_inc(s["f_exp"], 1)
            dve.wait_ge(s["f_exp"], 2)
            then(dve.tensor_tensor(rows(sqv), rows(ex), per_pos("count", NV), ALU.mult))
            then(dve.tensor_reduce(mean1, flat(sqv), AX.X, ALU.add))
            then(dve.reciprocal(den, mean1))
            then(dve.tensor_tensor(flat(val), flat(ex), per_row(den), ALU.mult))
            then(dve.tensor_tensor(rows(sqv)[:, :, :, 0:NF], v4[:, :, :, 0:NF], per_pos("own", NF), ALU.mult))
            then(dve.tensor_reduce(wown, flat(sqv)[:, :, 0:NF], AX.X, ALU.add))
            then(dve.tensor_copy(wdiag, flat(val)[:, :, NF]))
            d4 = dwt.rearrange("p (t b j) -> p t b j", b=B, j=NF)
            then(dve.tensor_tensor(dwt.rearrange("p (n j) -> p n j", j=NF), flat(val)[:, :, 0:NF],
                                   wown.unsqueeze(2).to_broadcast([TP, NT, NF]), ALU.subtract))
            dve.tensor_tensor(d4, d4, per_pos("before", NF), ALU.mult).then_inc(s["f_dw"], 1)

            def attend(i, p, live):
                if live(i):
                    text = isinstance(i, int) and i == TI
                    wait(dve, "y_ps", i + 1)
                    wait(dve, "y_h", i - 1)
                    dve.tensor_tensor(grid(far_part[p], C), grid(ps[0:TP, 2 + p, 0:256], C),
                                      spread(wown[:, bass.ds(i * B, B)], C), ALU.mult).then_inc(s["y_far"], 1)
                    wait(dve, "y_far", i + 1)
                    dve.tensor_tensor(far_part[p], far_part[p], ps[0:TP, 4 + p, 0:256], ALU.add).then_inc(s["y_sum"], 1)
                    wait(dve, "y_sum", i + 1)
                    wait(dve, "y_self2", i + 1)
                    dve.tensor_tensor(rows_of(h, i, text), grid(far_part[p], C), grid(self_part[p], C), ALU.add)\
                       .then_inc(s["y_h"], 1)
                if live(i - 2):
                    if not live(i):
                        wait(dve, "y_h", i - 1)
                    for b in range(B):
                        tile_stats(dve, b * TI + i - 2)

            pipeline(dve, attend, TI, 2, 2)
            dve.wait_ge(s["y_h"], TI)
            attend(TI, TI % 2, lambda u: u == TI)
            dve.wait_ge(s["y_h"], TT)
            for b in range(B - 1):
                tile_stats(dve, B * TI + b)
            tile_stats(dve, NT - 1).then_inc(s["ln_bn"], 1)
            dve.wait_ge(s["ln_bn"], 2)
            norm_stats(dve, "ln2", 0)
            dve.wait_ge(s["d_ffnw"], 32)
            dve.tensor_copy(gwh, gw_raw)
            dve.tensor_copy(ew1h, ew1_raw).then_inc(s["g_whi"], 1)
            dve.wait_ge(s["g_whi"], 1)
            dve.tensor_tensor(ew1l, ew1_raw, ew1h.bitcast(F32), ALU.subtract).then_inc(s["g_ew"], 1)
            dve.tensor_tensor(gwl, gw_raw, gwh.bitcast(F32), ALU.subtract).then_inc(s["g_w"], 1)
            dve.wait_ge(s["g_w"], 1)

            def read_logits(m, p):
                dve.wait_ge(s["g_lps"], m + 1)
                dve.tensor_tensor(tiles(logit, m * UT, UT, E), grid(ps[0:TP, 4 + p, 0:UT * E], E),
                                  gb_sb.unsqueeze(1).to_broadcast([TP, UT, E]), ALU.add).then_inc(s["g_logit"], 1)

            def route(i, p, live):
                if live(i + 2):
                    centre(i + 2, p, "g_cen", "g_lo")
                if live(i - 2):
                    read_logits(i - 2, p)
                if live(i + 2):
                    scale(i + 2, p, "g_cen", "g_xn")

            pipeline(dve, route, NU, 2, 2)

            gstep = [0]

            def then2(ins):
                gstep[0] += 1
                ins.then_inc(s["g_dve"], 1)
                dve.wait_ge(s["g_dve"], gstep[0])

            def g3(ap):
                return grid(ap, E)

            def each(ap):
                return spread(ap, E)

            dve.wait_ge(s["g_logit"], NU)
            then2(dve.tensor_reduce(gtop, g3(logit), AX.X, ALU.max))
            dve.tensor_tensor(g3(pick), g3(logit), each(gtop), ALU.subtract).then_inc(s["g_exp"], 1)
            dve.wait_ge(s["g_exp"], 2)
            then2(dve.tensor_reduce(gsum, g3(prob), AX.X, ALU.add))
            then2(dve.reciprocal(gsum, gsum))
            then2(dve.tensor_tensor(g3(prob), g3(prob), each(gsum), ALU.mult))
            rank = sm("rank", TP).unsqueeze(1).to_broadcast([TP, NT, E])
            then2(dve.tensor_copy(last_p, prob))
            for n in range(2):
                then2(dve.tensor_reduce(gtop, g3(last_p), AX.X, ALU.max))
                then2(dve.tensor_tensor(g3(cand), g3(last_p), each(gtop), ALU.is_ge))
                then2(dve.tensor_tensor(g3(cand), g3(cand), rank, ALU.mult))
                then2(dve.tensor_reduce(gtop, g3(cand), AX.X, ALU.max))
                then2(dve.tensor_tensor(g3(pick if n else keep), g3(cand), each(gtop), ALU.is_equal))
                if n == 0:
                    then2(dve.scalar_tensor_tensor(out=last_p, in0=keep, scalar=-2.0, in1=last_p, op0=ALU.mult,
                                                   op1=ALU.add))
            then2(dve.tensor_tensor(keep, keep, pick, ALU.add))
            dve.tensor_tensor(cw, prob, keep, ALU.mult).then_inc(s["g_cwps"], 1)
            dve.wait_ge(s["g_cwps"], 1)
            dve.wait_ge(s["g_cwt"], 1)
            for g in range(2):
                n = 4 - g
                dve.tensor_copy(cw_t[:, 4 * g * TP:(4 * g + n) * TP], ps[:, 6 + g, 0:n * TP])
            dve.tensor_copy(cw_t[0:4 * E, 7 * TP:8 * TP], ps[0:4 * E, 7, 3 * TP:4 * TP]).then_inc(s["g_cwt"], 1)
            for g in range(15):
                n = min(8, NT - 8 * g)
                dve.wait_ge(s["g_bps"], g + 1)
                hg = h[0:TP, g * 512:g * 512 + n * C]
                dve.tensor_tensor(hg, hg, ps[0:TP, g % 4, 0:n * C], ALU.add).then_inc(s["g_bias"], 1)
            dve.wait_ge(s["g_bias"], 15)

            wy4 = wy.rearrange("p (t e c) -> p t e c", e=E, c=C)

            with dve.Fori(0, NU) as m:
                for hf in range(2):
                    dve.wait_ge(s["e_y"], 2 * m + hf + 1)
                    w = tiles(cw, m * UT, UT, E)[:, :, 4 * hf:4 * hf + 4].unsqueeze(3).to_broadcast([TP, UT, 4, C])
                    y = ps[0:TP, 4 + 2 * hf:6 + 2 * hf, :].rearrange("p b (t e c) -> p (b t) e c", e=4, c=C)
                    dve.tensor_tensor(wy4[:, :, 4 * hf:4 * hf + 4], y, w, ALU.mult).then_inc(s["e_used"], 1)
                dve.wait_ge(s["e_used"], 2 * m + 2)
                dve.tensor_reduce(grid(wsum, C), wy4.rearrange("p t e c -> p t c e"), AX.X, ALU.add)\
                   .then_inc(s["e_red"], 1)
                dve.wait_ge(s["e_red"], m + 1)
                hm = h[0:TP, bass.ds(m * UT * C, UT * C)]
                dve.tensor_tensor(hm, hm, wsum, ALU.add).then_inc(s["e_out"], 1)


_INS = ["pair", "txt", "tok_w1", "tok_b1", "tok_w2", "tok_b2", "tok_w3", "tok_b3", "wq", "wq_t", "wv", "wo_t",
        "gate_w", "gate_b", "ffn_w1", "ffn_b1", "ffn_w2", "ffn_b2", "small", "table", "seg_rows"]


def kernel(**inputs):
    import numpy as _np
    import concourse.bacc as _bacc
    from concourse import mybir as _mybir
    from concourse.bass_utils import run_bass_kernel_spmd as _run

    f = _np.float32
    x = _np.asarray(inputs["x"])
    pad = _np.zeros((B, C, PW, PW), x.dtype)
    pad[:, :, 1:-1, 1:-1] = x
    pad = pad.reshape(B, C, PW * PW)
    pair = _np.zeros((B, 128, XA_IMG), x.dtype)
    pair[:, :C, PW:PW + PW * PW] = pad
    pair[:, C:, :PW * PW] = pad

    pairs = [(0, 3), (1, 4), (2, 5), (6, 7), (8, None)]
    w1 = _np.asarray(inputs["L0_tok_W1"]).reshape(C, 9, C)
    w1 = _np.concatenate([_np.concatenate([w1, w1], 2)] * 2, 0).reshape(128, 9 * 128)
    w2_src = _np.asarray(inputs["L0_tok_W2"]).reshape(C, C, 9)
    b2_src = _np.asarray(inputs["L0_tok_b2"]).reshape(C, 9)
    w3_src = _np.asarray(inputs["L0_tok_W3"]).reshape(C, 9, C)
    w2 = _np.zeros((C, CHUNKS, 2, C), x.dtype)
    b2 = _np.zeros((2, C, CHUNKS), x.dtype)
    w3 = _np.zeros((2, C, CHUNKS, C), x.dtype)
    for k, taps in enumerate(pairs):
        for j, tap in enumerate(taps):
            if tap is not None:
                w2[:, k, j] = w2_src[:, :, tap]
                b2[j, :, k] = b2_src[:, tap]
                w3[j, :, k] = w3_src[:, tap]
    w2 = _np.concatenate([w2.reshape(C, -1)] * 2, 0)
    b1 = _np.asarray(inputs["L0_tok_b1"])
    wv = _np.asarray(inputs["L0_attn_W_V"])
    gw = _np.asarray(inputs["L0_ffn_gate_w"])
    fw1 = _np.asarray(inputs["L0_ffn_W1"]).transpose(1, 0, 2).reshape(C, E * HID)
    fb2 = _np.asarray(inputs["L0_ffn_b2"])
    blk = _np.zeros((16, E, 16, C), x.dtype)
    for i in range(16):
        blk[i, :, i] = fb2
    small, table, seg_rows = make_tables()
    data = {
        "pair": pair, "txt": inputs["txt"], "tok_w1": w1, "tok_b1": _np.concatenate([b1, b1])[:, None],
        "tok_w2": w2, "tok_b2": b2.reshape(128, CHUNKS), "tok_w3": w3.reshape(128, CHUNKS * C),
        "tok_b3": _np.tile(_np.asarray(inputs["L0_tok_b3"])[None], (TP, 1)),
        "wq": inputs["L0_attn_W_Q"], "wq_t": _np.concatenate([_np.asarray(inputs["L0_attn_W_Q"]).T] * 2, 1),
        "wv": _np.concatenate([wv, wv], 1), "wo_t": _np.asarray(inputs["L0_attn_W_O"]).T,
        "gate_w": _np.concatenate([gw, gw], 0), "gate_b": _np.tile(_np.asarray(inputs["L0_ffn_gate_b"])[None], (TP, 1)),
        "ffn_w1": _np.concatenate([fw1, fw1], 0), "ffn_b1": _np.asarray(inputs["L0_ffn_b1"]).T,
        "ffn_w2": _np.asarray(inputs["L0_ffn_W2"]).transpose(1, 0, 2).reshape(HID, E * C),
        "ffn_b2": blk.reshape(128, 16 * C), "small": small, "table": table, "seg_rows": seg_rows,
    }

    nc = _bacc.Bacc("TRN2", target_bir_lowering=False, num_devices=1)
    arrays, args = {}, []
    for name in _INS:
        a = _np.ascontiguousarray(data[name])
        arrays[f"in_{name}_dram"] = a
        args.append(nc.dram_tensor(f"in_{name}_dram", a.shape, _mybir.dt.from_np(a.dtype), kind="ExternalInput").ap())
    args.append(nc.dram_tensor("out_0_dram", (B, SEQ, C), _mybir.dt.from_np(_np.dtype("float32")),
                               kind="ExternalOutput").ap())
    build(nc, *args)
    r = _run(nc, [arrays], core_ids=[0])
    return r.results[0]["out_0_dram"]
```

```python
from contextlib import ExitStack

import numpy as np

import concourse.bass as bass
from concourse import mybir

ALU = mybir.AluOpType
ACT = mybir.ActivationFunctionType
AX = mybir.AxisListType
F32 = mybir.dt.float32
F32R = mybir.dt.float32r

B, C, HW, TXT = 4, 64, 56, 77
PW = HW + 2
SEQ = HW * HW + TXT
TP = 2 * HW
UR = 8
UN = UR * HW
UT = UN // TP
UPI = HW // UR
UNITS = B * UPI
TI = UPI * UT
TT = TI + 1
NT = B * TT
NU = NT // UT
XA_IMG = 3424
XH_IMG = 3368
STEP = UR * PW
PIECES = 5
PIECE = -(-PW * PW // PIECES)
CHUNKS = 5
E, HID = 8, 128
EARLY = 4
WARM_UP = 18
GROUPS = -(-NT // 8)
BATCHES = [list(range(g, min(g + 4, GROUPS))) for g in range(0, GROUPS, 4)]
GROUP_SPANS = [(0, NT // 8, 64), (NT // 8, GROUPS, NT % 8 * E)]
LEVELS = 3
EPS_LN, EPS_L2, EPS_VAR = 1e-5, 1e-8, 1e-6
SCALE = 1.0 / 8.0
PSTEPS = UNITS


def haar_rows():
    cols = []
    for j in range(LEVELS):
        bc = 2 ** j
        bs = SEQ // bc
        half = bs // 2
        for k in range(bc):
            v = np.zeros(SEQ)
            v[k * bs:k * bs + half] = 1 / np.sqrt(half)
            v[k * bs + half:(k + 1) * bs] = -1 / np.sqrt(half)
            cols.append(v)
    w = np.stack(cols, 1)
    starts = [0] + [t for t in range(1, SEQ) if (w[t] != w[t - 1]).any()]
    return starts, w[starts]


STARTS, HAAR = haar_rows()
NSEG = len(STARTS)
NF = NSEG - 1
NV = NF + 1
NSUM = TT + NF


def rho_schedule():
    low, out = 1e-9, []
    while low < 1 - 1e-7:
        r = 2 / (1 + low)
        out.append(r)
        low = 1 - (1 - r * low) ** 2
    return out + [1.0] * (PSTEPS - len(out))


SMALL = {}
TABLE = {}
_at = 0
for _n, _w in (("ident", 128), ("two_i", C), ("dup_i", 128), ("sum_i", C), ("rho", PSTEPS), ("basis", NSEG), ("ones", C),
               ("rank", E)):
    SMALL[_n] = (_at, _at + _w)
    _at += _w
NSMALL = _at
_at = 0
for _n, _w in (("cos", TT * 32), ("sin", TT * 32), ("sums", TT * NSUM), ("seg", TT * NSEG), ("count", TT * NV),
               ("absent", TT * NV), ("before", TT * NF), ("own", TT * NF), ("inv_n", TT), ("root_n", TT),
               ("prefix", TP)):
    TABLE[_n] = (_at, _at + _w)
    _at += _w
NTABLE = _at
WORK = 5008 + NTABLE


def make_tables():
    f = np.float32
    small = np.zeros((128, NSMALL), f)

    def put(arr, spans, name, value):
        a, b = spans[name]
        value = np.asarray(value, f).reshape(len(value), -1)
        arr[:value.shape[0], a:b] = value

    put(small, SMALL, "ident", np.eye(128))
    put(small, SMALL, "two_i", 2 * np.eye(C))
    put(small, SMALL, "dup_i", np.concatenate([np.eye(C)] * 2, 1))
    put(small, SMALL, "sum_i", np.concatenate([np.eye(C)] * 2, 0))
    put(small, SMALL, "rho", np.tile(np.array(rho_schedule())[None], (128, 1)))
    put(small, SMALL, "basis", HAAR @ HAAR.T)
    put(small, SMALL, "ones", np.ones((128, C)))
    put(small, SMALL, "rank", np.tile(np.arange(E, 0, -1)[None], (128, 1)))

    table = np.zeros((128, NTABLE), f)
    t = np.arange(TP)[:, None] + TP * np.arange(TT)[None, :]
    real = t < SEQ
    half = C // 2
    inv_freq = (1.0 / 10000.0 ** (np.arange(half, dtype=f) / half)).astype(f)
    ang = t.astype(f)[..., None] * inv_freq
    put(table, TABLE, "cos", np.cos(ang) * real[..., None])
    put(table, TABLE, "sin", np.sin(ang) * real[..., None])
    ends = STARTS[1:] + [SEQ]
    seg = np.searchsorted(STARTS, t, side="right") - 1
    onehot = (seg[..., None] == np.arange(NSEG)) & real[..., None]
    put(table, TABLE, "seg", onehot)
    sums = np.zeros((TP, TT, NSUM))
    for j in range(TT):
        sums[:, j, j + 1:TT] = 1
    sums *= real[..., None]
    sums[:, :, TT:] = onehot[:, :, :NF]
    put(table, TABLE, "sums", sums)
    count = np.ones((TP, TT, NV))
    for j in range(NF):
        count[:, :, j] = np.clip(t - STARTS[j], 0, ends[j] - STARTS[j]) * real
    put(table, TABLE, "count", count)
    put(table, TABLE, "absent", np.where(count > 0, 0.0, -1e30))
    put(table, TABLE, "before", (np.arange(NF) < seg[..., None]) & real[..., None])
    put(table, TABLE, "own", onehot[:, :, :NF])
    n = np.where(real, t + 1, 1).astype(f)
    put(table, TABLE, "inv_n", 1 / n)
    put(table, TABLE, "root_n", 1 / np.sqrt(n))
    prefix = np.zeros((TP + 1, TP))
    prefix[:TP] = np.triu(np.ones((TP, TP)), 1)
    prefix[TP] = 1
    put(table, TABLE, "prefix", prefix)
    seg_rows = np.zeros((NSEG, TT, TP), f)
    seg_rows[:] = onehot.transpose(2, 1, 0)
    return small, table, seg_rows.reshape(NSEG, TT * TP)


def is_zero(m):
    return isinstance(m, int) and m == 0


def build(nc, pair, txt, tok_w1, tok_b1, tok_w2, tok_b2, tok_w3, tok_b3, wq, wq_t, wv, wo_t,
          gate_w, gate_b, ffn_w1, ffn_b1, ffn_w2, ffn_b2, small, table, seg_rows, out):
    ctx = ExitStack()
    with ctx:
        def sb(name, cols, dt=F32):
            return ctx.enter_context(nc.sbuf_tensor(name, [128, cols], dt))

        def sem(name):
            return ctx.enter_context(nc.semaphore(name))

        h = sb("h", NT * C)
        vx = sb("vx", 2 * NT * C)
        stack = sb("stack", 4 * XH_IMG + UN, F32R)
        work = sb("work", WORK)
        wts = sb("wts", 3584, F32R)
        w3_sb = sb("w3_sb", CHUNKS * C)
        small_sb = sb("small_sb", NSMALL)
        bias = sb("bias", 1 + CHUNKS + E + C + E)
        stat = sb("stat", 10 * NT + 1)
        nrm = sb("nrm", 3 * NT + 64)
        seg_q = sb("seg_q", B * 2 * NSEG)
        seg_v = sb("seg_v", B * NSUM)
        ps = ctx.enter_context(nc.psum_tensor("ps", [128, 8, 512], F32))

        def sm(name, rows=128):
            a, b = SMALL[name]
            return small_sb[0:rows, a:b]

        tb0 = WORK - NTABLE

        def tab(name, rows=TP):
            a, b = TABLE[name]
            return work[0:rows, tb0 + a:tb0 + b]

        def grid(ap, inner):
            return ap.rearrange("p (t c) -> p t c", c=inner)

        ident = sm("ident")
        b1_sb = bias[:, 0:1]
        b2_sb = bias[:, 1:1 + CHUNKS]
        eb1_sb = bias[:, 6:6 + E]
        b3_sb = bias[0:TP, 14:14 + C]
        gb_sb = bias[0:TP, 78:78 + E]

        pin = work[:, tb0:tb0 + 9 * C]
        xa = vx[:, 0:B * XA_IMG]
        xh = stack[:, 0:2 * XH_IMG]
        ghi = stack[:, 2 * XH_IMG:2 * XH_IMG + CHUNKS * UN]
        glo = stack[:, 2 * XH_IMG + CHUNKS * UN:2 * XH_IMG + 2 * CHUNKS * UN]
        w3_at = 2 * XH_IMG + 2 * CHUNKS * UN
        w3hl = stack[:, w3_at:w3_at + CHUNKS * 128].rearrange("p (k c) -> p k c", c=128)
        assert PW * PW <= PIECES * PIECE <= XH_IMG
        hl = stack[:, B * XH_IMG:B * XH_IMG + UN]
        gates = work[:, 0:CHUNKS * UN]
        gated = work[:, CHUNKS * UN:2 * CHUNKS * UN]
        w1_raw = work[:, 0:9 * 128]
        w2_raw = work[:, 9 * 128:14 * 128]
        w1h, w1l = wts[:, 0:1152], wts[:, 1152:2304]
        w2h, w2l = wts[:, 2304:2944], wts[:, 2944:3584]
        qkvh, qkvl = wts[:, 0:256], wts[:, 256:512]
        gwhl = wts[:, 2048:2048 + 2 * E]
        hid = work[:, 4480:4480 + UN]
        turned = work[:, tb0 + 9 * C:tb0 + 9 * C + UN]
        a_in, a_t = pin[0:C, 8 * C:9 * C], pin[0:C, 0:C]
        a_tt = pin[0:C, 0:2 * C]
        xtx = pin[0:C, 2 * C:4 * C]
        xt, xx = xtx[:, 0:C], xtx[:, C:2 * C]
        resid = pin[0:C, 4 * C:5 * C]
        wv_sb = pin[0:C, 5 * C:7 * C]
        wo_sb = pin[0:C, 7 * C:8 * C]
        tiny = stat[:, 10 * NT:10 * NT + 1]
        rowsum, rowmax, bound, bound_inv = (stat[0:C, i:i + 1] for i in range(4))

        vals = vx[:, 0:NT * C]
        mean, vare, rstd, tmp_n = (stat[0:TP, i * NT:(i + 1) * NT] for i in range(4))
        bn = stat[0:TP, 4 * NT:10 * NT]
        xn = [work[0:TP, i * 256:(i + 1) * 256] for i in range(2)]
        qkv = [grid(work[0:TP, 512 + i * 768:512 + (i + 1) * 768], 192) for i in range(2)]
        m0 = NT * C + TT * TP
        prod = [grid(vx[0:TP, m0 + i * 768:m0 + (i + 1) * 768], 192) for i in range(2)]
        mcos, msin = ([vx[0:TP, m0 + 1536 + (2 * n + i) * 512:m0 + 1536 + (2 * n + i + 1) * 512]
                       .rearrange("p (t g d) -> p t g d", g=4, d=32) for i in range(2)] for n in range(2))
        assert m0 + 1536 + 2048 <= 2 * NT * C
        rot = [work[0:TP, 3840 + i * 512:3840 + (i + 1) * 512] for i in range(2)]
        unit_n = nrm[0:TP, 3 * NT:3 * NT + 64]
        root_u = [unit_n[:, i * 8:(i + 1) * 8] for i in range(2)]
        inv_u = [unit_n[:, 16 + i * 8:24 + i * 8] for i in range(2)]
        tmp_u = unit_n[:, 32:40]
        dots_u = [unit_n[:, 40 + i * 12:52 + i * 12].rearrange("p (t c) -> p t c", c=3) for i in range(2)]
        segw = [work[0:TP, 4864 + i * 72:4864 + (i + 1) * 72] for i in range(2)]
        assert 5008 <= tb0
        tok_hl = [stack[0:TP, i * 512:(i + 1) * 512] for i in range(2)]
        tok_t = [stack[:, 1024 + i * UN:1024 + (i + 1) * UN] for i in range(2)]
        inv = nrm[0:TP, 0:2 * NT]
        dot_qk = nrm[0:TP, 2 * NT:3 * NT]

        NR = TT * B * NV
        segr = vx[0:NSEG, NT * C:NT * C + TT * TP]
        val, dev, sqv, ex = (vx[0:TP, NT * C + TT * TP + i * NR:NT * C + TT * TP + (i + 1) * NR] for i in range(4))
        ks0 = work[0:C, 0:72]
        qk9 = work[0:NSEG, 72:108]
        bq9 = work[0:NSEG, 108:144]
        far9 = work[0:NSEG, 144:144 + B * NF]
        vpick = grid(work[0:C, 176:176 + B * 128], 128)
        vseg = stack[:, 2048:2304]
        carry = work[0:TT, 944:1200]
        mean1, mean2, mean3, den = (work[0:TP, 1200 + i * NT:1200 + (i + 1) * NT] for i in range(4))
        wown, wdiag = (work[0:TP, 1664 + i * NT:1664 + (i + 1) * NT] for i in range(2))
        dwt = work[0:TP, 1896:1896 + TT * B * NF]
        dhl = vx[0:TP, NT * C:NT * C + TT * 2 * B * NF]
        dwr = [work[0:TP, 2824 + i * 128:2824 + (i + 1) * 128] for i in range(2)]
        dwT = [stack[:, 2304 + i * TP:2304 + (i + 1) * TP] for i in range(2)]
        far_part = [work[0:TP, 3304 + i * 256:3304 + (i + 1) * 256] for i in range(2)]
        self_part = [work[0:TP, 3816 + i * 256:3816 + (i + 1) * 256] for i in range(2)]
        new_h = [work[0:TP, 4328 + i * 256:4328 + (i + 1) * 256] for i in range(2)]
        bn_u = [work[0:TP, 4840 + i * 24:4840 + (i + 1) * 24] for i in range(2)]

        all_t = stack[:, 0:NU * UN]
        hl2 = [work[0:TP, 512 + i * 512:512 + (i + 1) * 512] for i in range(2)]
        unit_t = [stack[:, NU * UN + i * UN:NU * UN + (i + 1) * UN] for i in range(2)]
        ew1_raw = work[:, 2432:2432 + 1024]
        ew2_sb = work[:, 3456:3456 + 512]
        gw_raw = work[:, 3968:3976]
        eb2_raw = work[:, 3976:3976 + 512]
        b2h, b2l = wts[:, 2560:3072], wts[:, 3072:3584]
        ew1h, ew1l = wts[:, 0:1024], wts[:, 1024:2048]
        g0 = NT * C
        logit = vx[0:TP, 6400:6400 + 928]
        prob, pick, keep, cand, last_p = (vx[0:TP, g0 + i * 928:g0 + (i + 1) * 928] for i in range(5))
        cw = vx[0:TP, g0 + 5 * 928:g0 + 6 * 928]
        cwhl = vx[0:TP, 4096:4096 + GROUPS * 128].rearrange("p (g k c) -> p g k c", k=2, c=64)
        gtop, gsum = stat[0:TP, 0:NT], stat[0:TP, NT:2 * NT]
        act_g = [vx[:, i * UN:(i + 1) * UN] for i in range(4)]
        wy = vx[0:TP, 4 * UN:4 * UN + 2048]
        wsum = vx[0:TP, 4 * UN + 2048:4 * UN + 2304]

        carry_rows = nc.dram_tensor("carry_rows", [B, TT, C], F32, kind="Internal").ap()

        names = """d_small d_w1 d_tokw d_first d_img0 d_img1 d_img2 d_img3 d_txt d_pin d_table d_segr d_rows d_carry
        d_ffnw d_ffn2 d_out
        z_text w_split x_hi x_up x_lo h1_ps h1_relu hl_ready s_ps s_sig u_ready u_hi u_lo_even u_lo_odd
        o_ps o_copy o_turn o_out
        p_init p_chain x_ready p_ps r_ready xn_ps w_ps w_hi w_ready
        ln1 ln1_root ln2 ln2_root ln_bn
        q_cen q_xn q_hi q_lo q_tps q_t q_ps q_sb q_sq q_qk q_dots q_root q_small q_invs q_segw q_cos q_sin q_rot
        q_rsum q_vsum q_racc q_vacc
        f_ps f_sb f_dve f_far f_carry f_vhi f_vsb f_exp f_pow f_dhi f_dw
        y_dwr y_dps y_dwt y_ps y_far y_self y_self2 y_sum y_h y_bn y_out y_bnc
        g_cen g_xn g_hi g_lo g_tps g_t g_ps g_gate g_logit g_w g_whi g_ewhi g_ew
        g_dve g_exp g_cw g_b2hi g_b2 g_zero g_cwhi g_part g_cwlo
        g_cwps g_cwt g_bps g_bias
        e_h e_g e_y e_used e_red e_early e_out""".split()
        s = {n: sem(n) for n in names}

        block = ctx.enter_context(nc.Block())
        d_img = [s["d_img0"], s["d_img1"], s["d_img2"], s["d_img3"]]

        def tiles(buf, start, n, inner=C):
            return grid(buf[:, bass.ds(start * inner, n * inner)], inner)

        def window(buf, lo, hi, off):
            return buf[lo:hi, bass.ds(off, STEP)].rearrange("p (r w) -> p r w", w=PW)[:, :, 0:HW]

        def tile_major(buf, width):
            return buf.rearrange("p (t c) -> p t c", c=width)

        def spread(ap, n):
            return ap.unsqueeze(2).to_broadcast([ap.shape[0], ap.shape[1], n])

        def rope_table(name, r, text):
            if text:
                return tab(name)[:, TI * 32:TT * 32].unsqueeze(1).unsqueeze(1).to_broadcast([TP, UT, 4, 32])
            return tab(name)[:, bass.ds(r * 32, UT * 32)].rearrange("p (t d) -> p t d", d=32).unsqueeze(2)\
                .to_broadcast([TP, UT, 4, 32])

        def rows_of(buf, j, text, inner=C):
            if text:
                return grid(buf[0:TP, B * TI * inner:NT * inner], inner)
            return buf[0:TP, 0:B * TI * inner].rearrange("p (b t c) -> p b t c", b=B, c=inner)[:, :, bass.ds(j, 1), :]\
                .rearrange("p b o c -> p b (o c)")

        @block.sync
        def _(sp):
            first = PW + PIECE
            sp.dma_start(w1_raw, tok_w1).then_inc(s["d_w1"], 16)
            sp.dma_start(xa[:, 0:first], pair[0][:, 0:first]).then_inc(s["d_first"], 16)
            sp.dma_start(w2_raw, tok_w2).then_inc(s["d_tokw"], 16)
            sp.dma_start(b1_sb, tok_b1).then_inc(s["d_tokw"], 16)
            sp.dma_start(b2_sb, tok_b2).then_inc(s["d_tokw"], 16)
            sp.dma_start(xa[:, first:XA_IMG], pair[0][:, first:XA_IMG]).then_inc(s["d_img0"], 16)
            sp.dma_start(small_sb[:, :], small).then_inc(s["d_small"], 16)
            sp.dma_start(w3_sb[:, :], tok_w3).then_inc(s["d_tokw"], 16)
            sp.dma_start(b3_sb, tok_b3).then_inc(s["d_tokw"], 16)
            sp.dma_start(eb1_sb, ffn_b1).then_inc(s["d_tokw"], 16)
            sp.dma_start(gb_sb, gate_b).then_inc(s["d_tokw"], 16)
            sp.dma_start(a_in, wq).then_inc(s["d_pin"], 16)
            sp.dma_start(a_tt, wq_t).then_inc(s["d_pin"], 16)
            sp.dma_start(wv_sb, wv).then_inc(s["d_pin"], 16)
            sp.dma_start(wo_sb, wo_t).then_inc(s["d_pin"], 16)
            for b in range(1, B):
                sp.dma_start(xa[:, b * XA_IMG:(b + 1) * XA_IMG], pair[b]).then_inc(d_img[b], 16)
            sp.wait_ge(s["z_text"], 1)
            for b in range(B):
                k = B * TI + b
                sp.dma_start(h[0:TXT, k * C:(k + 1) * C], txt[b]).then_inc(s["d_txt"], 16)
            sp.wait_ge(s["o_turn"], UNITS)
            sp.wait_ge(s["w_ps"], 1)
            sp.dma_start(work[:, tb0:tb0 + NTABLE], table).then_inc(s["d_table"], 16)
            sp.wait_ge(s["q_xn"], NU)
            sp.dma_start(segr, seg_rows).then_inc(s["d_segr"], 16)
            sp.wait_ge(s["f_carry"], 1)
            sp.dma_start(carry_rows.rearrange("b t c -> t b c"), carry.rearrange("t (b c) -> t b c", c=C))\
              .then_inc(s["d_rows"], 16)
            sp.wait_ge(s["d_rows"], 16)
            crow = vals[TP:TP + 1, :]
            sp.dma_start(crow[:, 0:B * TI * C].rearrange("o (b k) -> o b k", b=B),
                         carry_rows[:, 0:TI, :].rearrange("(o b) t c -> o b (t c)", o=1)).then_inc(s["d_carry"], 16)
            sp.dma_start(crow[:, B * TI * C:NT * C].rearrange("o (b c) -> o b c", b=B),
                         carry_rows[:, TI:TT, :].rearrange("(o b) t c -> o b (t c)", o=1)).then_inc(s["d_carry"], 16)
            sp.wait_ge(s["y_out"], TT)
            sp.wait_ge(s["y_bnc"], TT)
            sp.dma_start(gw_raw, gate_w).then_inc(s["d_ffnw"], 16)
            sp.dma_start(ew1_raw, ffn_w1).then_inc(s["d_ffnw"], 16)
            sp.dma_start(ew2_sb, ffn_w2).then_inc(s["d_ffn2"], 16)
            sp.dma_start(eb2_raw, ffn_b2).then_inc(s["d_ffn2"], 16)
            out_rows = out.rearrange("b s c -> (b s) c")
            with sp.Fori(0, UNITS) as m:
                sp.wait_ge(s["e_out"], m + 1)
                b = m // UPI
                dst = out_rows[bass.ds(m * UN + b * TXT, UN), :].rearrange("(t p) c -> p t c", p=TP)
                sp.dma_start(dst, tiles(h[0:TP, :], m * UT, UT)).then_inc(s["d_out"], 16)
            sp.wait_ge(s["e_out"], NU)
            for b in range(B):
                k = B * TI + b
                sp.dma_start(out[b, HW * HW:SEQ, :], h[0:TXT, k * C:(k + 1) * C]).then_inc(s["d_out"], 16)
            sp.wait_ge(s["d_out"], 16 * (UNITS + B))

        def wait(eng, name, value):
            if not (isinstance(value, int) and value <= 0):
                eng.wait_ge(s[name], value)

        def pipeline(eng, body, units, lead, lag):
            first = lag + 3 + (lag + 3) % 2
            pairs = (units - lead - first) // 2
            end = first + 2 * pairs
            for i in range(-lead, first):
                body(i, i % 2, lambda u: 0 <= u < units)
            with eng.Fori(first // 2, end // 2) as j:
                body(2 * j, 0, lambda u: True)
                body(2 * j + 1, 1, lambda u: True)
            for i in range(end, units + lag):
                body(i, i % 2, lambda u: 0 <= u < units)

        def tile_stats(eng, k):
            return eng.bn_stats(bn[:, bass.ds(k * 6, 6)], h[0:TP, bass.ds(k * C, C)])

        def norm_stats(eng, name, step0):
            count = [step0]

            def then(ins):
                count[0] += 1
                ins.then_inc(s[name], 1)
                eng.wait_ge(s[name], count[0])

            b6 = bn.rearrange("p (t c) -> p t c", c=6)
            then(eng.tensor_tensor(mean, b6[:, :, 1], b6[:, :, 4], ALU.add))
            then(eng.tensor_scalar(mean, mean, 0.5, None, ALU.mult))
            then(eng.tensor_tensor(vare, b6[:, :, 2], b6[:, :, 5], ALU.add))
            then(eng.tensor_tensor(rstd, b6[:, :, 1], b6[:, :, 4], ALU.subtract))
            then(eng.tensor_tensor(rstd, rstd, rstd, ALU.mult))
            then(eng.scalar_tensor_tensor(out=vare, in0=rstd, scalar=C / 4.0, in1=vare, op0=ALU.mult, op1=ALU.add))
            eng.tensor_scalar(vare, vare, 1.0 / C, EPS_LN, ALU.mult, ALU.add).then_inc(s[name], 1)
            eng.wait_ge(s[name + "_root"], 1)
            count[0] += 1
            then(eng.reciprocal(rstd, rstd))
            then(eng.tensor_tensor(tmp_n, rstd, rstd, ALU.mult))
            then(eng.tensor_tensor(tmp_n, tmp_n, vare, ALU.mult))
            then(eng.tensor_scalar(tmp_n, tmp_n, -0.5, 1.5, ALU.mult, ALU.add))
            then(eng.tensor_tensor(rstd, rstd, tmp_n, ALU.mult))

        @block.tensor
        def _(pe):
            def conv(off, last=False):
                n = 0
                for w in (w1h, w1l):
                    for tap in range(9):
                        mm = pe.matmul(ps[:, 0, 0:UN], w[:, tap * 128:(tap + 1) * 128],
                                       window(xh, 0, 128, off + (tap // 3) * PW + tap % 3),
                                       start=(n == 0), stop=(n == 17))
                        n += 1
                mm.then_inc(s["h1_ps"], 1)

            pe.wait_ge(s["w_split"], 2)
            pe.wait_ge(s["x_hi"], 1)
            pe.wait_ge(s["x_lo"], 1)
            conv(0)

            pe.wait_ge(s["d_pin"], 64)
            pe.wait_ge(s["d_small"], 16)
            pe.matmul(ps[0:C, 7, 0:C], a_t, a_t, start=True, stop=True).then_inc(s["p_init"], 1)
            pe.wait_ge(s["p_chain"], 1)
            pe.transpose(ps[0:1, 7, 64:128], rowsum, ident[0:C, 0:C]).then_inc(s["p_init"], 1)
            pe.wait_ge(s["p_chain"], 2)
            pe.matmul(ps[0:C, 7, 128:129], sm("ones", 1)[:, 0:C], rowmax[0:1, :], start=True, stop=True)\
              .then_inc(s["p_init"], 1)

            def taps_out(n, k):
                if k % 2 == 0:
                    pe.wait_ge(s["u_lo_even"], 3 * n + (k // 2 + 1))
                else:
                    pe.wait_ge(s["u_lo_odd"], 2 * n + (k // 2 + 1))
                for part in (ghi, glo):
                    mm = pe.matmul(ps[:, 6, 0:UN], w3hl[:, k], part[:, k * UN:(k + 1) * UN],
                                   start=(k == 0 and part is ghi), stop=(k == CHUNKS - 1 and part is glo))
                if k == CHUNKS - 1:
                    mm.then_inc(s["o_ps"], 1)

            def turn(n):
                pe.wait_ge(s["o_copy"], n + 1)
                pe.wait_ge(s["s_sig"], CHUNKS * min(n + 2, UNITS) if isinstance(n, int) else CHUNKS * n + 2 * CHUNKS)
                for t in range(UT):
                    mm = pe.matmul(ps[0:TP, 5, t * C:(t + 1) * C], turned[:, t * TP:(t + 1) * TP], sm("sum_i"),
                                   start=True, stop=True)
                mm.then_inc(s["o_turn"], 1)

            def unit(n, first, last):
                pe.wait_ge(s["hl_ready"], n + 1)
                if first:
                    pe.wait_ge(s["w_split"], 6)
                for k in range(CHUNKS):
                    if k == CHUNKS - 1:
                        wait(pe, "o_out", n - 1)
                    pe.matmul(ps[:, 1 + k, 0:UN], w2h[:, k * 128:(k + 1) * 128], hl, start=True, stop=False)
                    pe.matmul(ps[:, 1 + k, 0:UN], w2l[:, k * 128:(k + 1) * 128], hl, start=False, stop=True)\
                      .then_inc(s["s_ps"], 1)
                if not first:
                    taps_out(n - 1, 3)
                    taps_out(n - 1, 4)
                pe.wait_ge(s["x_ready"], n + 1)
                pe.matmul(ps[:, 7, 0:C], a_tt, xx, start=True, stop=True).then_inc(s["p_ps"], 1)
                if not last:
                    b = (n + 1) // UPI
                    pe.wait_ge(s["x_hi"], b * PIECES + 2)
                    pe.wait_ge(s["x_lo"], b * PIECES + 2)
                    conv((n + 1) % UPI * STEP + b % 2 * XH_IMG)
                pe.wait_ge(s["r_ready"], n + 1)
                pe.matmul(ps[:, 7, 128:192], xtx, resid, start=True, stop=True)
                pe.matmul(ps[0:C, 7, 64:128], resid, xt, start=True, stop=True)\
                  .then_inc(s["xn_ps"], 1)
                if not first:
                    turn(n - 1)
                for k in range(3):
                    taps_out(n, k)

            unit(0, True, False)
            unit(1, False, False)
            with pe.Fori(2, UNITS - 1) as n:
                unit(n, False, False)
            unit(UNITS - 1, False, True)
            taps_out(UNITS - 1, 3)
            taps_out(UNITS - 1, 4)
            pe.wait_ge(s["o_out"], UNITS - 1)
            turn(UNITS - 1)

            pe.wait_ge(s["x_ready"], UNITS + 1)
            pe.matmul(ps[:, 0, 0:C], sm("dup_i", C), a_in, start=True, stop=True)
            pe.matmul(ps[:, 0, C:2 * C], sm("dup_i", C), xt, start=True, stop=True)
            pe.matmul(ps[:, 0, 2 * C:3 * C], wv_sb, wo_sb, start=True, stop=True)
            pe.matmul(ps[:, 0, 3 * C:4 * C], wv_sb, wo_sb, start=True, stop=True).then_inc(s["w_ps"], 1)

            def attention(i, p, live):
                q = 1 - p
                if live(i + 1):
                    m = i + 1
                    wait(pe, "q_t", m + 1)
                    if is_zero(m):
                        pe.wait_ge(s["w_ready"], 1)
                    wait(pe, "q_sb", m)
                    for t in range(UT):
                        for n, w in enumerate((qkvh, qkvl)):
                            mm = pe.matmul(ps[0:TP, 3 + t // 2, t % 2 * 256:t % 2 * 256 + 256],
                                           tok_t[q][:, t * TP:(t + 1) * TP], w, start=(n == 0), stop=(n == 1))
                    mm.then_inc(s["q_ps"], 1)
                if live(i - 2):
                    m = i - 2
                    text = isinstance(m, int) and m == NU - 1
                    wait(pe, "q_rot", m + 1)
                    wait(pe, "q_segw", m + 1)
                    wait(pe, "q_racc", m - 1)
                    for t in range(UT):
                        o = ps[:, 5 + 2 * p, t * 18:(t + 1) * 18] if text else ps[:, 5 + 2 * p, 0:18]
                        mm = pe.matmul(o, rot[p][:, t * 128:(t + 1) * 128], segw[p][:, t * 18:(t + 1) * 18],
                                       start=(text or t == 0), stop=(text or t == UT - 1))
                    mm.then_inc(s["q_rsum"], 1)
                if live(i + 2):
                    m = i + 2
                    wait(pe, "q_lo", m + 1)
                    wait(pe, "q_t", m - 1)
                    for t in range(UT):
                        mm = pe.transpose(ps[:, 1 + p, t * TP:(t + 1) * TP],
                                          tok_hl[p][:, t * 128:(t + 1) * 128].bitcast(F32), ident[0:TP, 0:TP])
                    mm.then_inc(s["q_tps"], 1)
                if live(i):
                    m = i
                    text = isinstance(m, int) and m == NU - 1
                    r = TI if text else m % UPI * UT
                    wait(pe, "q_sb", m + 1)
                    wait(pe, "q_vacc", m - 1)
                    for t in range(UT):
                        j = r if text else r + t
                        o = ps[0:C, 6 * p, t * NSUM:(t + 1) * NSUM] if text else ps[0:C, 6 * p, 0:NSUM]
                        mm = pe.matmul(o, qkv[p][:, t, 128:192], tab("sums")[:, bass.ds(j * NSUM, NSUM)],
                                       start=(text or t == 0), stop=(text or t == UT - 1))
                    mm.then_inc(s["q_vsum"], 1)

            pe.wait_ge(s["d_table"], 16)
            pipeline(pe, attention, NU, 2, 3)

            pe.wait_ge(s["q_racc"], NU)
            pe.wait_ge(s["q_vacc"], NU)
            pe.matmul(ps[0:C, 0, 0:72], ident[:, C:128], seg_q[:, :], start=True, stop=True)\
              .then_inc(s["f_ps"], 1)
            pe.wait_ge(s["f_sb"], 1)
            for b in range(B):
                mm = pe.matmul(ps[0:NSEG, 1, b * NSEG:(b + 1) * NSEG], seg_q[0:C, b * 18:b * 18 + NSEG],
                               ks0[:, b * 18 + NSEG:(b + 1) * 18], start=True, stop=True)
            mm.then_inc(s["f_ps"], 1)
            pe.wait_ge(s["f_sb"], 2)
            for b in range(B):
                mm = pe.matmul(ps[0:NSEG, 2, b * NSEG:(b + 1) * NSEG], qk9[:, b * NSEG:(b + 1) * NSEG],
                               sm("basis", NSEG), start=True, stop=True)
            mm.then_inc(s["f_ps"], 1)
            pe.wait_ge(s["f_sb"], 3)
            for b in range(B):
                mm = pe.matmul(ps[0:NSEG, 0, b * NF:(b + 1) * NF], bq9[:, b * NSEG:(b + 1) * NSEG],
                               sm("basis", NSEG)[:, 0:NF], start=True, stop=True)
            mm.then_inc(s["f_ps"], 1)
            pe.wait_ge(s["f_sb"], 4)
            pe.wait_ge(s["d_segr"], 16)
            for j in range(TT):
                mm = pe.matmul(ps[0:TP, 5 + j // 16, j % 16 * 32:j % 16 * 32 + 32], segr[:, j * TP:(j + 1) * TP],
                               far9, start=True, stop=True)
            mm.then_inc(s["f_far"], 1)
            for b in range(B):
                mm = pe.transpose(ps[0:TT, 3, b * C:(b + 1) * C], seg_v[0:C, b * NSUM:b * NSUM + TT], ident[0:C, 0:C])
            mm.then_inc(s["f_ps"], 1)
            pe.wait_ge(s["f_vsb"], 1)
            for b in range(B):
                mm = pe.matmul(ps[:, 4, b * C:(b + 1) * C], vpick[:, b], ident[0:C, 0:C],
                               start=True, stop=True)
            mm.then_inc(s["f_ps"], 1)

            pe.wait_ge(s["f_vsb"], 2)
            pe.wait_ge(s["d_carry"], 32)

            def attend(i, p, live):
                q = 1 - p
                if live(i + 1):
                    wait(pe, "y_dwr", i + 2)
                    wait(pe, "y_dwt", i)
                    pe.transpose(ps[:, q, 0:TP], dwr[q], ident[0:TP, 0:TP]).then_inc(s["y_dps"], 1)
                if live(i):
                    text = isinstance(i, int) and i == TI
                    wait(pe, "y_sum", i - 1)
                    v = (tiles(vals[0:TP + 1, :], B * TI, B) if text else
                         vals[0:TP + 1, 0:B * TI * C].rearrange("p (b t c) -> p b t c", b=B, c=C)
                         [:, :, bass.ds(i, 1), :].rearrange("p b o c -> p b (o c)"))
                    pe.matmul(ps[0:TP, 2 + p, 0:256], tab("prefix", TP + 1), v, start=True, stop=True)
                    wait(pe, "y_dwt", i + 1)
                    pe.matmul(ps[0:TP, 4 + p, 0:256], dwT[p], vseg, start=True, stop=True).then_inc(s["y_ps"], 1)

            pipeline(pe, attend, TT, 2, 2)

            def route(i, p, live):
                q = 1 - p
                if live(i + 1):
                    m = i + 1
                    wait(pe, "g_lo", m + 1)
                    wait(pe, "g_t", m - 1)
                    for t in range(UT):
                        mm = pe.transpose(ps[:, q, t * TP:(t + 1) * TP], hl2[q][:, t * 128:(t + 1) * 128],
                                          ident[0:TP, 0:TP])
                    mm.then_inc(s["g_tps"], 1)
                if live(i):
                    wait(pe, "g_t", i + 1)
                    if is_zero(i):
                        pe.wait_ge(s["g_w"], 1)
                    wait(pe, "g_logit", i - 1)
                    for t in range(UT):
                        mm = pe.matmul(ps[0:TP, 4 + p, t * 2 * E:(t + 1) * 2 * E], unit_t[p][:, t * TP:(t + 1) * TP],
                                       gwhl, start=True, stop=True)
                    mm.then_inc(s["g_ps"], 1)

            pipeline(pe, route, NU, 2, 2)

            def turn_weights(n):
                for j, g in enumerate(BATCHES[n]):
                    mm = pe.transpose(ps[:, 6 + n % 2, j * TP:(j + 1) * TP], cwhl[:, g].rearrange("p k c -> p (k c)"),
                                      ident[0:TP, 0:TP])
                mm.then_inc(s["g_cwps"], 1)

            def bias_out(n):
                pe.wait_ge(s["g_cwt"], n + 1)
                for j, g in enumerate(BATCHES[n]):
                    if g >= 4:
                        pe.wait_ge(s["g_bias"], g - 3)
                    w = min(8, NT - 8 * g) * C
                    for part in (b2h, b2l):
                        mm = pe.matmul(ps[0:TP, 2 + g % 4, 0:w], unit_t[n % 2][:, j * TP:(j + 1) * TP], part[:, 0:w],
                                       start=(part is b2h), stop=(part is b2l))
                    mm.then_inc(s["g_bps"], 1)

            pe.wait_ge(s["g_ew"], 1)

            def hidden(m, e):
                pe.matmul(ps[:, e % 4, 0:UN], ew1h[:, e * HID:(e + 1) * HID], all_t[:, bass.ds(m * UN, UN)],
                          start=True, stop=False)
                pe.matmul(ps[:, e % 4, 0:UN], ew1l[:, e * HID:(e + 1) * HID], all_t[:, bass.ds(m * UN, UN)],
                          start=False, stop=True).then_inc(s["e_h"], 1)

            def experts(m, first, last):
                for e in range(E):
                    if e < E - 2:
                        hidden(m, e + 2)
                    elif not last:
                        hidden(m + 1, e + 2 - E)
                    if e % 4 == 0 and not first:
                        pe.wait_ge(s["e_used"], 2 * m + e // 4 - 1)
                    pe.wait_ge(s["e_g"], E * m + e + 1)
                    for t in range(UT):
                        col = t % 2 * 256 + e % 4 * C
                        mm = pe.matmul(ps[0:TP, 4 + e // 4 * 2 + t // 2, col:col + C], act_g[e % 4][:, t * TP:(t + 1) * TP],
                                       ew2_sb[:, e * C:(e + 1) * C], start=True, stop=True)
                    if e % 4 == 3:
                        mm.then_inc(s["e_y"], 1)

            for _ in range(WARM_UP):
                pe.matmul(ps[:, 0, 0:UN], ew1h[:, 0:HID], all_t[:, 0:UN], start=True, stop=True)
            hidden(0, 0)
            hidden(0, 1)
            for m in range(EARLY):
                experts(m, m == 0, False)
            pe.wait_ge(s["g_cwlo"], 1)
            pe.wait_ge(s["g_b2"], 1)
            pe.wait_ge(s["e_used"], 2 * EARLY)
            turn_weights(0)
            for n in range(len(BATCHES)):
                if n + 1 < len(BATCHES):
                    turn_weights(n + 1)
                bias_out(n)
            pe.wait_ge(s["g_bias"], GROUPS)
            with pe.Fori(EARLY, NU - 1) as m:
                experts(m, False, False)
            experts(NU - 1, False, True)

        @block.scalar
        def _(act):
            def round_image(b, a, w):
                act.activation(xh[0:C, bass.ds(b % 2 * XH_IMG + a, w)], xa[0:C, bass.ds(b * XA_IMG + PW + a, w)],
                               ACT.Copy).then_inc(s["x_hi"], 1)

            def hidden_layer(n):
                act.wait_ge(s["h1_ps"], n + 1)
                act.activation(hid[C:128], ps[C:128, 0, 0:UN], ACT.Relu, bias=b1_sb[C:128])
                act.activation(hl, ps[:, 0, 0:UN], ACT.Relu, bias=b1_sb).then_inc(s["h1_relu"], 1)

            def gates_of(n, first=False, last=False, piece=None):
                def hi(k):
                    act.wait_ge(s["u_ready"], CHUNKS * n + k + 1)
                    act.activation(ghi[:, k * UN:(k + 1) * UN], gated[:, k * UN:(k + 1) * UN], ACT.Copy)\
                       .then_inc(s["u_hi"], 1)

                def sigmoid(k):
                    act.wait_ge(s["s_ps"], CHUNKS * n + (k + 1))
                    act.activation(gates[:, k * UN:(k + 1) * UN], ps[:, 1 + k, 0:UN], ACT.Sigmoid,
                                   bias=b2_sb[:, k:k + 1]).then_inc(s["s_sig"], 1)

                sigmoid(0)
                sigmoid(1)
                hi(0)
                sigmoid(2)
                if not first:
                    turned_copy(n - 1)
                hi(1)
                sigmoid(3)
                hi(2)
                if piece is not None:
                    round_image(*piece)
                sigmoid(4)
                wait(act, "o_ps", n)
                hi(3)
                if not last:
                    hidden_layer(n + 1)
                hi(4)

            def turned_copy(n):
                act.wait_ge(s["o_ps"], n + 1)
                wait(act, "o_turn", n)
                act.activation(turned, ps[:, 6, 0:UN], ACT.Copy).then_inc(s["o_copy"], 1)

            act.wait_ge(s["d_w1"], 16)
            act.activation(tiny, w1_raw[:, 0:1], ACT.Sigmoid)
            act.wait_ge(s["d_first"], 16)
            round_image(0, 0, PIECE)
            act.wait_ge(d_img[0], 16)
            round_image(0, PIECE, (PIECES - 1) * PIECE)
            act.wait_ge(s["d_tokw"], 112)
            hidden_layer(0)
            for b in range(B):
                gates_of(b * UPI, first=(b == 0))
                if b + 1 < B:
                    act.wait_ge(d_img[b + 1], 16)
                    if b == 0:
                        gates_of(1, piece=(1, 0, PIECE))
                    with act.Fori(int(b == 0), PIECES) as u:
                        gates_of(u + (b * UPI + 1), piece=(b + 1, u * PIECE, PIECE))
                    gates_of(b * UPI + UPI - 1)
                else:
                    with act.Fori(b * UPI + 1, UNITS - 1) as n:
                        gates_of(n)
            gates_of(UNITS - 1, last=True)
            turned_copy(UNITS - 1)

            act.wait_ge(s["ln1"], 7)
            act.activation(rstd, vare, ACT.Sqrt).then_inc(s["ln1_root"], 1)

            def attention(i, p, live):
                q = 1 - p
                if live(i - 1):
                    wait(act, "q_dots", i)
                    wait(act, "q_invs", i - 2)
                    act.activation(root_u[q].rearrange("p (t c) -> p t c", c=2), dots_u[q][:, :, 0:2], ACT.Sqrt)\
                       .then_inc(s["q_root"], 1)
                if live(i + 1):
                    m = i + 1
                    wait(act, "q_tps", m + 1)
                    wait(act, "q_ps", m - 1)
                    act.activation(tok_t[q], ps[:, 1 + q, 0:UN], ACT.Copy).then_inc(s["q_t"], 1)
                if live(i):
                    wait(act, "q_sb", i + 1)
                    wait(act, "q_dots", i - 1)
                    act.activation(prod[p][:, :, 0:128], qkv[p][:, :, 0:128], ACT.Square).then_inc(s["q_sq"], 1)
                if live(i + 2):
                    m = i + 2
                    wait(act, "q_xn", m + 1)
                    wait(act, "q_tps", m - 1)
                    act.activation(tile_major(tok_hl[p], 128)[:, :, 0:C], tile_major(xn[p], C), ACT.Copy)\
                       .then_inc(s["q_hi"], 1)
                if live(i + 1):
                    m = i + 1
                    ps_u = ps[0:TP, 3:5, :].rearrange("p b (t c) -> p b t c", c=256)
                    wait(act, "q_ps", m + 1)
                    wait(act, "q_vsum", m - 1)
                    wait(act, "q_rot", m - 1)
                    act.activation(qkv[q].rearrange("p (b t) c -> p b t c", b=2), ps_u[:, :, :, 0:192], ACT.Copy)
                    act.activation(vals[0:TP, bass.ds(m * UT * C, UT * C)].rearrange("p (b t c) -> p b t c", b=2, c=C),
                                   ps_u[:, :, :, 128:192], ACT.Copy).then_inc(s["q_sb"], 1)

            pipeline(act, attention, NU, 2, 3)

            act.wait_ge(s["f_pow"], 1)
            act.activation(mean3, mean2, ACT.Sqrt).then_inc(s["f_pow"], 1)
            act.wait_ge(s["f_exp"], 1)
            act.activation(ex, dev, ACT.Exp).then_inc(s["f_exp"], 1)

            act.wait_ge(s["f_dw"], 1)

            def attend(i, p, live):
                q = 1 - p
                if live(i + 1):
                    wait(act, "y_dps", i + 2)
                    wait(act, "y_ps", i)
                    act.activation(dwT[q], ps[:, q, 0:TP], ACT.Copy).then_inc(s["y_dwt"], 1)
                if live(i + 2):
                    wait(act, "y_dps", i + 1)
                    act.activation(grid(dwr[p], 64), dhl[:, bass.ds((i + 2) * 64, 64)].unsqueeze(1)
                                   .to_broadcast([TP, 2, 64]), ACT.Copy).then_inc(s["y_dwr"], 1)
                if live(i - 1):
                    m = i - 1
                    wait(act, "y_h", m + 1)
                    act.activation(rows_of(h, m, isinstance(m, int) and m == TI), grid(new_h[q], C), ACT.Copy)\
                       .then_inc(s["y_out"], 1)
                if live(i - 2):
                    m = i - 2
                    wait(act, "y_bn", m + 1)
                    act.activation(rows_of(bn, m, isinstance(m, int) and m == TI, 6), grid(bn_u[p], 6), ACT.Copy)\
                       .then_inc(s["y_bnc"], 1)

            pipeline(act, attend, TT, 2, 2)

            act.wait_ge(s["ln2"], 7)
            act.activation(rstd, vare, ACT.Sqrt).then_inc(s["ln2_root"], 1)
            act.wait_ge(s["d_ffnw"], 32)
            act.activation(ew1h, ew1_raw, ACT.Copy).then_inc(s["g_ewhi"], 1)

            def route(i, p, live):
                q = 1 - p
                if live(i + 2):
                    wait(act, "g_xn", i + 3)
                    wait(act, "g_tps", i + 1)
                    act.activation(tile_major(hl2[p], 128)[:, :, 0:C].bitcast(F32R), tile_major(xn[p], C), ACT.Copy)\
                       .then_inc(s["g_hi"], 1)
                if live(i + 1):
                    wait(act, "g_tps", i + 2)
                    wait(act, "g_ps", i)
                    act.activation(unit_t[q], ps[:, q, 0:UN], ACT.Copy)
                    act.activation(all_t[:, bass.ds((i + 1) * UN, UN)], ps[:, q, 0:UN], ACT.Copy)\
                       .then_inc(s["g_t"], 1)

            pipeline(act, route, NU, 2, 2)

            act.wait_ge(s["d_ffn2"], 32)
            act.activation(b2h, eb2_raw, ACT.Copy).then_inc(s["g_b2hi"], 1)
            act.wait_ge(s["g_exp"], 1)
            act.activation(prob, pick, ACT.Exp).then_inc(s["g_exp"], 1)
            act.activation(tiny, sm("two_i")[:, 0:1], ACT.Gelu)

            def weights_hi():
                act.wait_ge(s["g_cw"], 2)
                for a, b, c in GROUP_SPANS:
                    ins = act.activation(cwhl[:, a:b, 0, 0:c].bitcast(F32R),
                                         cw[:, a * 64:a * 64 + (b - a) * c].rearrange("p (g c) -> p g c", c=c), ACT.Copy)
                ins.then_inc(s["g_cwhi"], 1)

            def weights_turned(n):
                act.wait_ge(s["g_cwps"], n + 1)
                if n >= 2:
                    act.wait_ge(s["g_bps"], BATCHES[n - 2][-1] + 1)
                w = len(BATCHES[n]) * TP
                act.activation(unit_t[n % 2][:, 0:w], ps[:, 6 + n % 2, 0:w], ACT.Copy).then_inc(s["g_cwt"], 1)

            def gelus(m):
                for e in range(E):
                    act.wait_ge(s["e_h"], E * m + (e + 1))
                    act.activation(act_g[e % 4], ps[:, e % 4, 0:UN], ACT.Gelu, bias=eb1_sb[:, e:e + 1])\
                       .then_inc(s["e_g"], 1)

            act.wait_ge(s["g_zero"], 1)
            for m in range(EARLY):
                gelus(m)
            weights_hi()
            for n in range(len(BATCHES)):
                weights_turned(n)
            with act.Fori(EARLY, NU) as m:
                gelus(m)

        @block.gpsimd
        def _(pool):
            pool.memset(h[0:TP, B * TI * C:NT * C], 0.0).then_inc(s["z_text"], 1)
            pool.wait_ge(s["z_text"], 1)

            def gated_lo(n):
                for k in range(0, CHUNKS, 2):
                    pool.wait_ge(s["u_hi"], CHUNKS * n + k + 1)
                    c = slice(k * UN, (k + 1) * UN)
                    pool.tensor_tensor(glo[:, c], gated[:, c], ghi[:, c].bitcast(F32), ALU.subtract)\
                        .then_inc(s["u_lo_even"], 1)

            for b in range(B):
                gated_lo(b * UPI)
                if b + 1 < B:
                    with pool.Fori(0, PIECES) as u:
                        gated_lo(u + (b * UPI + 1))
                        pool.wait_ge(s["u_lo_even"], 3 * u + 3 * (b * UPI + 2))
                        pool.wait_ge(s["x_up"], u + (b * PIECES + 3))
                        up = xh[C:128, bass.ds((b + 1) % 2 * XH_IMG + u * PIECE, PIECE)]
                        pool.tensor_tensor(up, xa[C:128, bass.ds((b + 1) * XA_IMG + u * PIECE, PIECE)],
                                           up.bitcast(F32), ALU.subtract).then_inc(s["x_lo"], 1)
                        pool.wait_ge(s["x_lo"], u + (b * PIECES + 3))
                    gated_lo(b * UPI + UPI - 1)
                else:
                    with pool.Fori(b * UPI + 1, UNITS) as n:
                        gated_lo(n)

            pool.wait_ge(s["d_table"], 16)

            def attention(i, p, live):
                if live(i):
                    text = isinstance(i, int) and i == NU - 1
                    wait(pool, "q_sb", i + 1)
                    wait(pool, "q_dots", i - 1)
                    pool.tensor_tensor(prod[p][:, :, 128:192], qkv[p][:, :, 0:64], qkv[p][:, :, 64:128], ALU.mult)\
                        .then_inc(s["q_qk"], 1)
                    wait(pool, "q_rot", i - 1)
                    pool.tensor_tensor(mcos[p], qkv[p][:, :, 0:128].rearrange("p t (g d) -> p t g d", d=32),
                                       rope_table("cos", TI if text else i % UPI * UT, text), ALU.mult)\
                        .then_inc(s["q_cos"], 1)
                if live(i + 2):
                    wait(pool, "q_hi", i + 3)
                    t3 = tile_major(tok_hl[p], 128)
                    pool.tensor_tensor(t3[:, :, C:128], tile_major(xn[p], C), t3[:, :, 0:C].bitcast(F32),
                                       ALU.subtract).then_inc(s["q_lo"], 1)

            pipeline(pool, attention, NU, 2, 3)

            pool.wait_ge(s["f_dw"], 1)

            def attend(i, p, live):
                if live(i):
                    text = isinstance(i, int) and i == TI
                    wait(pool, "y_h", i - 1)
                    pool.tensor_tensor(grid(self_part[p], C), rows_of(vals, i, text),
                                       spread(wdiag[:, bass.ds(i * B, B)], C), ALU.mult).then_inc(s["y_self"], 1)
                    wait(pool, "y_self", i + 1)
                    pool.tensor_tensor(grid(self_part[p], C), grid(self_part[p], C), rows_of(h, i, text), ALU.add)\
                        .then_inc(s["y_self2"], 1)

            pipeline(pool, attend, TT, 2, 2)

            pool.wait_ge(s["g_ewhi"], 1)
            pool.tensor_tensor(ew1l, ew1_raw, ew1h.bitcast(F32), ALU.subtract).then_inc(s["g_ew"], 1)
            pool.wait_ge(s["g_ew"], 1)

            def route(i, p, live):
                if live(i + 2):
                    wait(pool, "g_hi", i + 3)
                    t3 = tile_major(hl2[p], 128)
                    pool.tensor_tensor(t3[:, :, C:128], tile_major(xn[p], C), t3[:, :, 0:C], ALU.subtract)\
                        .then_inc(s["g_lo"], 1)

            pipeline(pool, route, NU, 2, 2)

            pool.memset(vx[0:TP, 4096 + (GROUPS - 1) * 128:4096 + GROUPS * 128], 0.0).then_inc(s["g_zero"], 1)
            pool.wait_ge(s["g_zero"], 1)
            pool.wait_ge(s["g_b2hi"], 1)
            pool.tensor_tensor(b2l, eb2_raw, b2h.bitcast(F32), ALU.subtract).then_inc(s["g_b2"], 1)
            pool.wait_ge(s["g_b2"], 1)
            pool.wait_ge(s["g_cwhi"], 1)
            for k, (a, b, c) in enumerate(GROUP_SPANS):
                pool.tensor_tensor(cwhl[:, a:b, 1, 0:c],
                                   cw[:, a * 64:a * 64 + (b - a) * c].rearrange("p (g c) -> p g c", c=c),
                                   cwhl[:, a:b, 0, 0:c], ALU.subtract).then_inc(s["g_part" if k == 0 else "g_cwlo"], 1)
                if k == 0:
                    pool.wait_ge(s["g_part"], 1)

        @block.vector
        def _(dve):
            def split_weights(n, hi, lo, raw):
                dve.tensor_copy(hi, raw).then_inc(s["w_split"], 1)
                dve.wait_ge(s["w_split"], 2 * n + 1)
                dve.tensor_tensor(lo, raw, hi.bitcast(F32), ALU.subtract).then_inc(s["w_split"], 1)

            def split_image(b, a, w):
                dve.tensor_copy(xh[C:128, bass.ds(b % 2 * XH_IMG + a, w)], xa[C:128, bass.ds(b * XA_IMG + a, w)])\
                   .then_inc(s["x_up"], 1)

            def first_lo(a, w):
                dve.wait_ge(s["x_up"], 2 if a else 1)
                up = xh[C:128, a:a + w]
                dve.tensor_tensor(up, xa[C:128, a:a + w], up.bitcast(F32), ALU.subtract).then_inc(s["x_lo"], 1)

            def split_hidden(n):
                dve.wait_ge(s["h1_relu"], n + 1)
                dve.tensor_tensor(hl[C:128, :], hid[C:128, :], hl[C:128, :].bitcast(F32), ALU.subtract)\
                   .then_inc(s["hl_ready"], 1)

            dve.wait_ge(s["d_w1"], 16)
            split_weights(0, w1h, w1l, w1_raw)
            dve.wait_ge(s["d_first"], 16)
            split_image(0, 0, PIECE)
            first_lo(0, PIECE)
            dve.wait_ge(s["d_tokw"], 112)
            split_weights(1, w2h, w2l, w2_raw)
            w3_raw = w3_sb[:, :].rearrange("p (k c) -> p k c", c=C)
            split_weights(2, w3hl[:, :, 0:C], w3hl[:, :, C:128], w3_raw)
            dve.wait_ge(d_img[0], 16)
            split_image(0, PIECE, (PIECES - 1) * PIECE)
            split_hidden(0)
            dve.wait_ge(s["p_init"], 1)
            dve.tensor_reduce(rowsum, ps[0:C, 7, 0:C], AX.X, ALU.add, apply_absolute_value=True)\
               .then_inc(s["p_chain"], 1)
            dve.wait_ge(s["p_init"], 2)
            dve.tensor_reduce(rowmax[0:1, :], ps[0:1, 7, 64:128], AX.X, ALU.max).then_inc(s["p_chain"], 1)
            dve.wait_ge(s["p_init"], 3)
            dve.tensor_scalar(bound, ps[0:C, 7, 128:129], 1e-30, None, ALU.max).then_inc(s["p_chain"], 1)
            dve.wait_ge(s["p_chain"], 3)
            dve.reciprocal(bound_inv, bound).then_inc(s["p_chain"], 1)
            dve.wait_ge(s["p_chain"], 4)
            dve.tensor_scalar(xx, a_t, bound_inv, None, ALU.mult)
            dve.tensor_scalar(xt, a_in, bound_inv, None, ALU.mult).then_inc(s["x_ready"], 1)

            def tokens_out(n):
                dve.wait_ge(s["o_turn"], n + 1)
                dve.tensor_tensor(tiles(h[0:TP, :], n * UT, UT), grid(ps[0:TP, 5, 0:UT * C], C),
                                  b3_sb.unsqueeze(1).to_broadcast([TP, UT, C]), ALU.add).then_inc(s["o_out"], 1)

            def stats_of(n):
                dve.wait_ge(s["o_out"], n + 1)
                for t in range(UT):
                    tile_stats(dve, n * UT + t)

            first_lo(PIECE, (PIECES - 1) * PIECE)

            def tokenizer(n, first, last, piece=None):
                off = n * STEP + (n // UPI) * (XA_IMG - UPI * STEP)

                def gate(k):
                    dve.wait_ge(s["s_sig"], CHUNKS * n + (k + 1))
                    g3 = gates[:, k * UN:(k + 1) * UN].rearrange("p (r w) -> p r w", w=HW)
                    u3 = gated[:, k * UN:(k + 1) * UN].rearrange("p (r w) -> p r w", w=HW)
                    if k < 3:
                        ins = dve.tensor_tensor(u3, g3, window(xa, 0, 128, off + PW + k), ALU.mult)
                    elif k == 3:
                        dve.tensor_tensor(u3[0:C], g3[0:C], window(xa, 0, C, off + 3 * PW), ALU.mult)
                        ins = dve.tensor_tensor(u3[C:128], g3[C:128], window(xa, C, 128, off + 2 * PW + 1), ALU.mult)
                    else:
                        ins = dve.tensor_tensor(u3, g3, window(xa, 0, 128, off + 3 * PW + 2), ALU.mult)
                    ins.then_inc(s["u_ready"], 1)

                def odd_lo(k):
                    dve.wait_ge(s["u_hi"], CHUNKS * n + (k + 1))
                    c = slice(k * UN, (k + 1) * UN)
                    dve.tensor_tensor(glo[:, c], gated[:, c], ghi[:, c].bitcast(F32), ALU.subtract)\
                       .then_inc(s["u_lo_odd"], 1)

                gate(0)
                gate(1)
                dve.wait_ge(s["p_ps"], n + 1)
                dve.tensor_scalar(resid, ps[0:C, 7, 0:C], sm("rho", C)[:, bass.ds(n, 1)], None, ALU.mult)\
                   .then_inc(s["p_chain"], 1)
                gate(2)
                dve.wait_ge(s["p_chain"], n + 5)
                dve.tensor_tensor(resid, sm("two_i", C), resid, ALU.subtract).then_inc(s["r_ready"], 1)
                odd_lo(1)
                gate(3)
                wait(dve, "u_lo_even", 3 * n)
                gate(4)
                odd_lo(3)
                if not last:
                    split_hidden(n + 1)
                dve.wait_ge(s["xn_ps"], n + 1)
                dve.tensor_scalar(xtx, ps[0:C, 7, 64:192], sm("rho", C)[:, bass.ds(n, 1)], None, ALU.mult)\
                   .then_inc(s["x_ready"], 1)
                if piece is not None:
                    split_image(*piece)
                if not first:
                    tokens_out(n - 1)
                if not first and not (isinstance(n, int) and n == 1):
                    stats_of(n - 2)

            for b in range(B):
                tokenizer(b * UPI, b == 0, False)
                if b + 1 < B:
                    dve.wait_ge(d_img[b + 1], 16)
                    if b == 0:
                        tokenizer(1, False, False, (1, 0, PIECE))
                    with dve.Fori(int(b == 0), PIECES) as u:
                        tokenizer(u + (b * UPI + 1), False, False, (b + 1, u * PIECE, PIECE))
                    tokenizer(b * UPI + UPI - 1, False, False)
                else:
                    with dve.Fori(b * UPI + 1, UNITS - 1) as n:
                        tokenizer(n, False, False)
            tokenizer(UNITS - 1, False, True)
            tokens_out(UNITS - 1)
            stats_of(UNITS - 2)

            dve.wait_ge(s["w_ps"], 1)
            dve.tensor_copy(qkvh, ps[:, 0, 0:256]).then_inc(s["w_hi"], 1)
            dve.wait_ge(s["w_hi"], 1)
            dve.tensor_tensor(qkvl, ps[:, 0, 0:256], qkvh.bitcast(F32), ALU.subtract).then_inc(s["w_ready"], 1)

            dve.wait_ge(s["d_txt"], 64)
            stats_of(UNITS - 1)
            for b in range(B - 1):
                tile_stats(dve, B * TI + b)
            tile_stats(dve, NT - 1).then_inc(s["ln_bn"], 1)
            dve.wait_ge(s["ln_bn"], 1)
            norm_stats(dve, "ln1", 0)
            dve.wait_ge(s["d_table"], 16)

            def centre(m, p, step, taken):
                wait(dve, taken, m - 1)
                dve.tensor_tensor(grid(xn[p], C), tiles(h[0:TP, :], m * UT, UT), spread(mean[:, bass.ds(m * UT, UT)], C),
                                  ALU.subtract).then_inc(s[step], 1)

            def scale(m, p, step, ready):
                wait(dve, step, m + 1)
                dve.tensor_tensor(grid(xn[p], C), grid(xn[p], C), spread(rstd[:, bass.ds(m * UT, UT)], C),
                                  ALU.mult).then_inc(s[ready], 1)

            def attention(i, p, live):
                q = 1 - p

                def refine(n):
                    if not live(i - 1):
                        return
                    m = i - 1
                    r0, r1, r2 = root_u[q], inv_u[q], tmp_u
                    if n:
                        wait(dve, "q_small", 6 * m + n)
                    if n == 0:
                        wait(dve, "q_root", m + 1)
                        ins = dve.tensor_scalar(r2, r0, 1e-18, None, ALU.add)
                    elif n == 1 or n == 5:
                        ins = dve.reciprocal(r1, r2)
                    elif n == 2:
                        ins = dve.tensor_tensor(r2.rearrange("p (t c) -> p t c", c=2), dots_u[q][:, :, 0:2],
                                                r1.rearrange("p (t c) -> p t c", c=2), ALU.mult)
                    elif n == 3:
                        ins = dve.tensor_tensor(r2, r2, r0, ALU.add)
                    else:
                        ins = dve.tensor_scalar(r2, r2, 0.5, EPS_L2, ALU.mult, ALU.add)
                    ins.then_inc(s["q_small"], 1)

                if live(i + 2):
                    centre(i + 2, p, "q_cen", "q_lo")
                for m, name, used, sums, src, w in (
                        (i - 3, "q_racc", "q_rsum", seg_q[:, :], ps[:, 5 + 2 * q], 18),
                        (i - 1, "q_vacc", "q_vsum", seg_v[0:C, :], ps[0:C, 6 * q], NSUM)):
                    if live(m):
                        wait(dve, used, m + 1)
                        wait(dve, name, m)
                        last = isinstance(m, int) and m == NU - 1
                        dst = sums if last else sums[:, bass.ds(m // UPI * w, w)]
                        dve.tensor_tensor(dst, dst, src[:, 0:B * w] if last else src[:, 0:w], ALU.add)\
                           .then_inc(s[name], 1)
                if live(i + 2):
                    scale(i + 2, p, "q_cen", "q_xn")
                refine(0)
                text = isinstance(i, int) and i == NU - 1
                if live(i):
                    wait(dve, "q_sb", i + 1)
                    wait(dve, "q_rot", i - 1)
                    dve.tensor_tensor(msin[p], qkv[p][:, :, 0:128].rearrange("p t (g d) -> p t g d", d=32),
                                      rope_table("sin", TI if text else i % UPI * UT, text), ALU.mult)\
                       .then_inc(s["q_sin"], 1)
                refine(1)
                if live(i):
                    wait(dve, "q_sq", i + 1)
                    wait(dve, "q_qk", i + 1)
                    dve.tensor_reduce(dots_u[p], prod[p].rearrange("p t (g c) -> p t g c", c=C), AX.X,
                                      ALU.add).then_inc(s["q_dots"], 1)
                refine(2)
                ro = rot[p].rearrange("p (t q g d) -> p t q g d", q=2, g=2, d=32)
                mc = mcos[p].rearrange("p t (q g) d -> p t q g d", g=2)
                ms = msin[p].rearrange("p t (q g) d -> p t q g d", g=2)
                if live(i):
                    wait(dve, "q_cos", i + 1)
                    wait(dve, "q_sin", i + 1)
                    wait(dve, "q_rsum", i - 1)
                    dve.tensor_tensor(ro[:, :, :, 0], mc[:, :, :, 0], ms[:, :, :, 1], ALU.subtract)
                refine(3)
                if live(i):
                    dve.tensor_tensor(ro[:, :, :, 1], ms[:, :, :, 0], mc[:, :, :, 1], ALU.add)\
                       .then_inc(s["q_rot"], 1)
                refine(4)
                if live(i - 1):
                    m = i - 1
                    last = isinstance(m, int) and m == NU - 1
                    dve.tensor_copy(dot_qk[:, bass.ds(m * UT, UT)], dots_u[q][:, :, 2])
                    refine(5)
                    wait(dve, "q_small", 6 * m + 6)
                    wait(dve, "q_rsum", m - 1)
                    if last:
                        ind = tab("seg")[:, TI * NSEG:TT * NSEG].unsqueeze(1).unsqueeze(1)\
                            .to_broadcast([TP, UT, 2, NSEG])
                    else:
                        ind = tab("seg")[:, bass.ds(m % UPI * UT * NSEG, UT * NSEG)]\
                            .rearrange("p (t g) -> p t g", g=NSEG).unsqueeze(2).to_broadcast([TP, UT, 2, NSEG])
                    dve.tensor_tensor(segw[q].rearrange("p (t q g) -> p t q g", q=2, g=NSEG), ind,
                                      inv_u[q].rearrange("p (t c) -> p t c", c=2).unsqueeze(3)
                                      .to_broadcast([TP, UT, 2, NSEG]), ALU.mult).then_inc(s["q_segw"], 1)
                    dve.tensor_copy(inv[:, bass.ds(m * UT * 2, UT * 2)], inv_u[q]).then_inc(s["q_invs"], 1)

            dve.memset(seg_q[:, :], 0.0)
            dve.memset(seg_v[:, :], 0.0).then_inc(s["f_dve"], 1)
            dve.wait_ge(s["f_dve"], 1)
            pipeline(dve, attention, NU, 2, 3)

            dve.memset(work[0:C, 176:176 + B * 128], 0.0).then_inc(s["f_dve"], 1)
            dve.wait_ge(s["q_racc"], NU)
            dve.wait_ge(s["q_vacc"], NU)
            dve.wait_ge(s["f_dve"], 2)
            for b in range(B):
                ins = dve.tensor_copy(grid(vpick[:, b], 32)[:, :, b * NF:(b + 1) * NF],
                                      seg_v[0:C, b * NSUM + TT:(b + 1) * NSUM].unsqueeze(1).to_broadcast([C, 4, NF]))
            ins.then_inc(s["f_vsb"], 1)
            for n, (dst, src) in enumerate(((ks0, ps[0:C, 0, 0:72]), (qk9, ps[0:NSEG, 1, 0:B * NSEG]),
                                            (bq9, ps[0:NSEG, 2, 0:B * NSEG]))):
                dve.wait_ge(s["f_ps"], n + 1)
                dve.tensor_copy(dst, src).then_inc(s["f_sb"], 1)
            dve.wait_ge(s["f_ps"], 4)
            dve.tensor_scalar(far9, ps[0:NSEG, 0, 0:B * NF], SCALE, None, ALU.mult).then_inc(s["f_sb"], 1)

            step = [2]

            def then(ins):
                step[0] += 1
                ins.then_inc(s["f_dve"], 1)
                dve.wait_ge(s["f_dve"], step[0])

            v4 = val.rearrange("p (t b j) -> p t b j", b=B, j=NV)
            d3 = dot_qk
            i3 = inv.rearrange("p (t c) -> p t c", c=2)
            then(dve.tensor_tensor(mean1, i3[:, :, 0], i3[:, :, 1], ALU.mult))
            then(dve.scalar_tensor_tensor(out=mean2, in0=d3, scalar=SCALE, in1=mean1, op0=ALU.mult, op1=ALU.mult))
            dve.tensor_copy(v4[:, 0:TI, :, NF], mean2[:, 0:B * TI].rearrange("p (b t) -> p t b", b=B))
            dve.tensor_copy(v4[:, TI, :, NF], mean2[:, B * TI:NT])
            dve.wait_ge(s["f_far"], 1)
            dve.tensor_copy(v4[:, 0:16, :, 0:NF],
                            ps[0:TP, 5, :].rearrange("p (t b j) -> p t b j", b=B, j=NF))
            then(dve.tensor_copy(v4[:, 16:TT, :, 0:NF],
                                 ps[0:TP, 6, 0:(TT - 16) * 32].rearrange("p (t b j) -> p t b j", b=B, j=NF)))

            dve.wait_ge(s["f_ps"], 5)
            dve.tensor_copy(carry, ps[0:TT, 3, 0:B * C]).then_inc(s["f_carry"], 1)
            dve.wait_ge(s["f_ps"], 6)
            dve.tensor_copy(vseg, ps[:, 4, 0:B * C]).then_inc(s["f_vhi"], 1)
            dve.wait_ge(s["f_vhi"], 1)
            dve.tensor_tensor(vseg[C:128], ps[C:128, 4, 0:B * C], vseg[C:128].bitcast(F32), ALU.subtract)\
               .then_inc(s["f_vsb"], 1)

            def rows(ap):
                return ap.rearrange("p (t b j) -> p t b j", b=B, j=NV)

            def flat(ap):
                return ap.rearrange("p (n j) -> p n j", j=NV)

            def per_pos(name, width):
                return tab(name).rearrange("p (t j) -> p t j", j=width).unsqueeze(2).to_broadcast([TP, TT, B, width])

            def per_row(ap):
                return ap.unsqueeze(2).to_broadcast([TP, NT, NV])

            def by_pos(ap):
                return ap.rearrange("p (t b) -> p t b", b=B)

            inv_n = tab("inv_n").unsqueeze(2).to_broadcast([TP, TT, B])
            root_n = tab("root_n").unsqueeze(2).unsqueeze(2).to_broadcast([TP, TT, B, NV])
            then(dve.tensor_tensor(v4, v4, root_n, ALU.mult))
            then(dve.tensor_tensor(rows(sqv), v4, per_pos("count", NV), ALU.mult))
            then(dve.tensor_reduce(mean1, flat(sqv), AX.X, ALU.add))
            then(dve.tensor_tensor(by_pos(mean1), by_pos(mean1), inv_n, ALU.mult))
            then(dve.tensor_tensor(flat(dev), flat(val), per_row(mean1), ALU.subtract))
            then(dve.tensor_tensor(sqv, dev, dev, ALU.mult))
            then(dve.tensor_tensor(rows(sqv), rows(sqv), per_pos("count", NV), ALU.mult))
            then(dve.tensor_reduce(mean1, flat(sqv), AX.X, ALU.add))
            then(dve.tensor_tensor(by_pos(mean2), by_pos(mean1), inv_n, ALU.mult))
            dve.tensor_scalar(mean2, mean2, EPS_VAR, None, ALU.max).then_inc(s["f_pow"], 1)
            dve.wait_ge(s["f_pow"], 2)
            then(dve.reciprocal(mean3, mean3))
            then(dve.tensor_tensor(mean1, mean3, mean3, ALU.mult))
            then(dve.tensor_tensor(mean1, mean1, mean2, ALU.mult))
            then(dve.tensor_scalar(mean1, mean1, -0.5, 1.5, ALU.mult, ALU.add))
            then(dve.tensor_tensor(mean3, mean3, mean1, ALU.mult))
            then(dve.tensor_tensor(flat(dev), flat(dev), per_row(mean3), ALU.mult))
            then(dve.tensor_tensor(rows(dev), rows(dev), per_pos("absent", NV), ALU.add))
            then(dve.tensor_reduce(mean1, flat(dev), AX.X, ALU.max))
            dve.tensor_tensor(flat(dev), flat(dev), per_row(mean1), ALU.subtract).then_inc(s["f_exp"], 1)
            dve.wait_ge(s["f_exp"], 2)
            then(dve.tensor_tensor(rows(sqv), rows(ex), per_pos("count", NV), ALU.mult))
            then(dve.tensor_reduce(mean1, flat(sqv), AX.X, ALU.add))
            then(dve.reciprocal(den, mean1))
            then(dve.tensor_tensor(flat(val), flat(ex), per_row(den), ALU.mult))
            then(dve.tensor_tensor(rows(sqv)[:, :, :, 0:NF], v4[:, :, :, 0:NF], per_pos("own", NF), ALU.mult))
            then(dve.tensor_reduce(wown, flat(sqv)[:, :, 0:NF], AX.X, ALU.add))
            then(dve.tensor_copy(wdiag, flat(val)[:, :, NF]))
            d4 = dwt.rearrange("p (t b j) -> p t b j", b=B, j=NF)
            then(dve.tensor_tensor(dwt.rearrange("p (n j) -> p n j", j=NF), flat(val)[:, :, 0:NF],
                                   wown.unsqueeze(2).to_broadcast([TP, NT, NF]), ALU.subtract))
            then(dve.tensor_tensor(d4, d4, per_pos("before", NF), ALU.mult))
            d32, hl3 = dwt.rearrange("p (t c) -> p t c", c=32), dhl.rearrange("p (t c) -> p t c", c=64)
            dve.tensor_copy(hl3[:, :, 0:32].bitcast(F32R), d32).then_inc(s["f_dhi"], 1)
            dve.wait_ge(s["f_dhi"], 1)
            dve.tensor_tensor(hl3[:, :, 32:64], d32, hl3[:, :, 0:32], ALU.subtract).then_inc(s["f_dw"], 1)

            def attend(i, p, live):
                q = 1 - p

                def stats(half):
                    if live(i - 1):
                        if half == 0:
                            wait(dve, "y_h", i)
                            wait(dve, "y_bnc", i - 2)
                        for b in (2 * half, 2 * half + 1):
                            ins = dve.bn_stats(bn_u[q][:, b * 6:(b + 1) * 6], new_h[q][:, b * C:(b + 1) * C])
                        if half == 1:
                            ins.then_inc(s["y_bn"], 1)

                if live(i):
                    wait(dve, "y_ps", i + 1)
                    dve.tensor_tensor(grid(far_part[p], C), grid(ps[0:TP, 2 + p, 0:256], C),
                                      spread(wown[:, bass.ds(i * B, B)], C), ALU.mult).then_inc(s["y_far"], 1)
                stats(0)
                if live(i):
                    wait(dve, "y_far", i + 1)
                    dve.tensor_tensor(far_part[p], far_part[p], ps[0:TP, 4 + p, 0:256], ALU.add).then_inc(s["y_sum"], 1)
                stats(1)
                if live(i):
                    wait(dve, "y_sum", i + 1)
                    wait(dve, "y_self2", i + 1)
                    wait(dve, "y_out", i - 1)
                    dve.tensor_tensor(new_h[p], far_part[p], self_part[p], ALU.add).then_inc(s["y_h"], 1)

            pipeline(dve, attend, TT, 2, 2)
            dve.wait_ge(s["y_out"], TT)
            dve.wait_ge(s["y_bnc"], TT)
            norm_stats(dve, "ln2", 0)
            dve.wait_ge(s["d_ffnw"], 32)
            dve.tensor_copy(gwhl[:, 0:E], gw_raw).then_inc(s["g_whi"], 1)
            dve.wait_ge(s["g_whi"], 1)
            dve.tensor_tensor(gwhl[:, E:2 * E], gw_raw, gwhl[:, 0:E].bitcast(F32), ALU.subtract).then_inc(s["g_w"], 1)
            dve.wait_ge(s["g_w"], 1)

            def route(i, p, live):
                m = i - 2
                if live(i + 2):
                    centre(i + 2, p, "g_cen", "g_lo")
                if live(m):
                    own = tiles(logit, m * UT, UT, E)
                    parts = ps[0:TP, 4 + p, 0:UT * 2 * E].rearrange("p (t k e) -> p t k e", k=2, e=E)
                    wait(dve, "g_ps", m + 1)
                    dve.tensor_tensor(own, parts[:, :, 0], gb_sb.unsqueeze(1).to_broadcast([TP, UT, E]), ALU.add)\
                       .then_inc(s["g_gate"], 1)
                if live(i + 2):
                    scale(i + 2, p, "g_cen", "g_xn")
                if live(m):
                    wait(dve, "g_gate", m + 1)
                    dve.tensor_tensor(own, own, parts[:, :, 1], ALU.add).then_inc(s["g_logit"], 1)

            pipeline(dve, route, NU, 2, 2)

            gstep = [0]

            def then2(ins):
                gstep[0] += 1
                ins.then_inc(s["g_dve"], 1)
                dve.wait_ge(s["g_dve"], gstep[0])

            def g3(ap):
                return grid(ap, E)

            def each(ap):
                return spread(ap, E)

            dve.wait_ge(s["g_logit"], NU)
            then2(dve.tensor_reduce(gtop, g3(logit), AX.X, ALU.max))
            dve.tensor_tensor(g3(pick), g3(logit), each(gtop), ALU.subtract).then_inc(s["g_exp"], 1)
            dve.wait_ge(s["g_exp"], 2)
            rank = sm("rank", TP).unsqueeze(1)

            def gate_step(k, t0, t1):
                lg, pb, lp, cd, kp, pk = (ap[:, t0 * E:t1 * E] for ap in (logit, prob, last_p, cand, keep, pick))
                top, total = gtop[:, t0:t1], gsum[:, t0:t1]
                rk = rank.to_broadcast([TP, t1 - t0, E])
                if k == 0:
                    then2(dve.tensor_reduce(total, g3(pb), AX.X, ALU.add))
                    then2(dve.reciprocal(total, total))
                elif k == 1:
                    then2(dve.tensor_tensor(g3(pb), g3(pb), each(total), ALU.mult))
                    then2(dve.tensor_copy(lp, pb))
                elif k in (2, 5):
                    then2(dve.tensor_reduce(top, g3(lp), AX.X, ALU.max))
                    then2(dve.tensor_tensor(g3(cd), g3(lp), each(top), ALU.is_ge))
                elif k in (3, 6):
                    then2(dve.tensor_tensor(g3(cd), g3(cd), rk, ALU.mult))
                    then2(dve.tensor_reduce(top, g3(cd), AX.X, ALU.max))
                elif k == 4:
                    then2(dve.tensor_tensor(g3(kp), g3(cd), each(top), ALU.is_equal))
                    then2(dve.scalar_tensor_tensor(out=lp, in0=kp, scalar=-2.0, in1=lp, op0=ALU.mult, op1=ALU.add))
                elif k == 7:
                    then2(dve.tensor_tensor(g3(pk), g3(cd), each(top), ALU.is_equal))
                    then2(dve.tensor_tensor(kp, kp, pk, ALU.add))
                else:
                    dve.tensor_tensor(cw[:, t0 * E:t1 * E], pb, kp, ALU.mult).then_inc(s["g_cw"], 1)

            wy4 = wy.rearrange("p (t e c) -> p t e c", e=E, c=C)

            def weigh(m, hf):
                dve.wait_ge(s["e_y"], 2 * m + (hf + 1))
                w = tiles(cw, m * UT, UT, E)[:, :, 4 * hf:4 * hf + 4].unsqueeze(3).to_broadcast([TP, UT, 4, C])
                y = ps[0:TP, 4 + 2 * hf:6 + 2 * hf, :].rearrange("p b (t e c) -> p (b t) e c", e=4, c=C)
                dve.tensor_tensor(wy4[:, :, 4 * hf:4 * hf + 4], y, w, ALU.mult).then_inc(s["e_used"], 1)

            def gather(m, done="e_out"):
                dve.wait_ge(s["e_used"], 2 * m + 2)
                dve.tensor_reduce(grid(wsum, C), wy4.rearrange("p t e c -> p t c e"), AX.X, ALU.add)\
                   .then_inc(s["e_red"], 1)
                dve.wait_ge(s["e_red"], m + 1)
                hm = h[0:TP, bass.ds(m * UT * C, UT * C)]
                dve.tensor_tensor(hm, hm, wsum, ALU.add).then_inc(s[done], 1)

            for k in range(9):
                gate_step(k, 0, EARLY * UT)
            dve.wait_ge(s["g_cw"], 1)
            gate_step(0, EARLY * UT, NT)
            for m in range(EARLY):
                for hf in range(2):
                    if 2 * m + hf + 1 < 9:
                        gate_step(2 * m + hf + 1, EARLY * UT, NT)
                    weigh(m, hf)
                gather(m, "e_early")
            dve.wait_ge(s["e_early"], EARLY)
            for g in range(GROUPS):
                w = min(8, NT - 8 * g) * C
                dve.wait_ge(s["g_bps"], g + 1)
                hg = h[0:TP, g * 512:g * 512 + w]
                dve.tensor_tensor(hg, hg, ps[0:TP, 2 + g % 4, 0:w], ALU.add).then_inc(s["g_bias"], 1)
            dve.wait_ge(s["g_bias"], GROUPS)
            dve.tensor_copy(tiny, tiny).then_inc(s["e_out"], EARLY)

            with dve.Fori(EARLY, NU) as m:
                for hf in range(2):
                    weigh(m, hf)
                gather(m)


_INS = ["pair", "txt", "tok_w1", "tok_b1", "tok_w2", "tok_b2", "tok_w3", "tok_b3", "wq", "wq_t", "wv", "wo_t",
        "gate_w", "gate_b", "ffn_w1", "ffn_b1", "ffn_w2", "ffn_b2", "small", "table", "seg_rows"]


def kernel(**inputs):
    import numpy as _np
    import concourse.bacc as _bacc
    from concourse import mybir as _mybir
    from concourse.bass_utils import run_bass_kernel_spmd as _run

    f = _np.float32
    x = _np.asarray(inputs["x"])
    pad = _np.zeros((B, C, PW, PW), x.dtype)
    pad[:, :, 1:-1, 1:-1] = x
    pad = pad.reshape(B, C, PW * PW)
    pair = _np.zeros((B, 128, XA_IMG), x.dtype)
    pair[:, :C, PW:PW + PW * PW] = pad
    pair[:, C:, :PW * PW] = pad

    pairs = [(0, 3), (1, 4), (2, 5), (6, 7), (8, None)]
    w1 = _np.asarray(inputs["L0_tok_W1"]).reshape(C, 9, C)
    w1 = _np.concatenate([_np.concatenate([w1, w1], 2)] * 2, 0).reshape(128, 9 * 128)
    w2_src = _np.asarray(inputs["L0_tok_W2"]).reshape(C, C, 9)
    b2_src = _np.asarray(inputs["L0_tok_b2"]).reshape(C, 9)
    w3_src = _np.asarray(inputs["L0_tok_W3"]).reshape(C, 9, C)
    w2 = _np.zeros((C, CHUNKS, 2, C), x.dtype)
    b2 = _np.zeros((2, C, CHUNKS), x.dtype)
    w3 = _np.zeros((2, C, CHUNKS, C), x.dtype)
    for k, taps in enumerate(pairs):
        for j, tap in enumerate(taps):
            if tap is not None:
                w2[:, k, j] = w2_src[:, :, tap]
                b2[j, :, k] = b2_src[:, tap]
                w3[j, :, k] = w3_src[:, tap]
    w2 = _np.concatenate([w2.reshape(C, -1)] * 2, 0)
    b1 = _np.asarray(inputs["L0_tok_b1"])
    wv = _np.asarray(inputs["L0_attn_W_V"])
    gw = _np.asarray(inputs["L0_ffn_gate_w"])
    fw1 = _np.asarray(inputs["L0_ffn_W1"]).transpose(1, 0, 2).reshape(C, E * HID)
    fb2 = _np.asarray(inputs["L0_ffn_b2"])
    blk = _np.zeros((2, 8, E, 8, C), x.dtype)
    for i in range(8):
        blk[:, i, :, i] = fb2
    small, table, seg_rows = make_tables()
    data = {
        "pair": pair, "txt": inputs["txt"], "tok_w1": w1, "tok_b1": _np.concatenate([b1, b1])[:, None],
        "tok_w2": w2, "tok_b2": b2.reshape(128, CHUNKS), "tok_w3": w3.reshape(128, CHUNKS * C),
        "tok_b3": _np.tile(_np.asarray(inputs["L0_tok_b3"])[None], (TP, 1)),
        "wq": inputs["L0_attn_W_Q"], "wq_t": _np.concatenate([_np.asarray(inputs["L0_attn_W_Q"]).T] * 2, 1),
        "wv": _np.concatenate([wv, wv], 1), "wo_t": _np.asarray(inputs["L0_attn_W_O"]).T,
        "gate_w": _np.concatenate([gw, gw], 0), "gate_b": _np.tile(_np.asarray(inputs["L0_ffn_gate_b"])[None], (TP, 1)),
        "ffn_w1": _np.concatenate([fw1, fw1], 0), "ffn_b1": _np.asarray(inputs["L0_ffn_b1"]).T,
        "ffn_w2": _np.asarray(inputs["L0_ffn_W2"]).transpose(1, 0, 2).reshape(HID, E * C),
        "ffn_b2": blk.reshape(128, 8 * C), "small": small, "table": table, "seg_rows": seg_rows,
    }

    nc = _bacc.Bacc("TRN2", target_bir_lowering=False, num_devices=1)
    arrays, args = {}, []
    for name in _INS:
        a = _np.ascontiguousarray(data[name])
        arrays[f"in_{name}_dram"] = a
        args.append(nc.dram_tensor(f"in_{name}_dram", a.shape, _mybir.dt.from_np(a.dtype), kind="ExternalInput").ap())
    args.append(nc.dram_tensor("out_0_dram", (B, SEQ, C), _mybir.dt.from_np(_np.dtype("float32")),
                               kind="ExternalOutput").ap())
    build(nc, *args)
    r = _run(nc, [arrays], core_ids=[0])
    return r.results[0]["out_0_dram"]
```
